# Optimizing a Trainium2 kernel written in Bass

```python
import numpy as np
import jax
import jax.numpy as jnp

def _softmax(x, axis=-1):
    return jax.nn.softmax(x, axis=axis)

def _gelu(x):
    return jax.nn.gelu(x, approximate=True)

def _silu(x):
    return jax.nn.silu(x)

def _sigmoid(x):
    return jax.nn.sigmoid(x)

def _layernorm(x, axis=-1, eps=1e-05):
    m = jnp.mean(x, axis=axis, keepdims=True)
    v = jnp.var(x, axis=axis, keepdims=True)
    return (x - m) / jnp.sqrt(v + eps)

def _scatter_add(tgt, idx, src, axis=0):
    return tgt.at[idx].add(src)

def _segment_sum(src, seg, n):
    return jax.ops.segment_sum(src, seg, n)
kernel_name = 'mk_adj_preln_d4_adj_r2_4cccb4'

def setup_inputs(seed: int=0):
    np.random.seed(seed)
    _w = jnp.asarray

    def _rec_inputs():
        import jax
        import jax.numpy as jnp
        _gk = jax.random.key(seed)
        x = -0.0005207 + 1.001 * jax.random.normal(jax.random.fold_in(_gk, 1), (128, 128, 128), jnp.float32)
        _a = jax.random.bernoulli(jax.random.fold_in(_gk, 2), 0.0625, (128, 128, 128))
        _a = jnp.logical_or(_a, jnp.swapaxes(_a, -1, -2))
        _a = jnp.logical_or(_a, jnp.eye(128, dtype=bool))
        _af = _a.astype(jnp.float32)
        adj = _af
        _nm = jnp.ones((128, 128), dtype=bool)
        nodemask = jnp.where(_nm, 1.0, 0.0).astype(jnp.float32)
        return (x, adj, nodemask)
    x, adj, nodemask = _rec_inputs()

    def _L0_gnn_setup():
        import jax, jax.numpy as jnp
        import numpy as np
        DIM = 128
        HEADS = 8
        BS = 8
        N = 512
        NEG = -1000000000.0
        key = jax.random.key(seed)
        ks = jax.random.split(key, 8)
        feats = jax.random.normal(ks[0], (BS, N, DIM), dtype=jnp.float32)
        adj_mat = (jax.random.uniform(ks[1], (BS, N, N)) < 0.1).astype(jnp.float32)
        s = 1.0 / np.sqrt(DIM)
        fc_w = jax.random.normal(ks[2], (DIM, DIM * HEADS), dtype=jnp.float32) * s
        fc_b = jnp.zeros((DIM * HEADS,), dtype=jnp.float32)
        q_w = jax.random.normal(ks[3], (DIM, 1), dtype=jnp.float32) * s
        q_b = jnp.zeros((1,), dtype=jnp.float32)
        k_w = jax.random.normal(ks[4], (DIM, 1), dtype=jnp.float32) * s
        k_b = jnp.zeros((1,), dtype=jnp.float32)
        fp_w = jax.random.normal(ks[5], (DIM * HEADS, DIM), dtype=jnp.float32) * (1.0 / np.sqrt(DIM * HEADS))
        fp_b = jnp.zeros((DIM,), dtype=jnp.float32)
        return {'feats': feats, 'adj_mat': adj_mat, 'fc_w': fc_w, 'fc_b': fc_b, 'q_w': q_w, 'q_b': q_b, 'k_w': k_w, 'k_b': k_b, 'fp_w': fp_w, 'fp_b': fp_b}
    _L0_gnn_all = _L0_gnn_setup()
    _L0_gnn_in = {k: v for k, v in _L0_gnn_all.items() if k in ('fc_w', 'fc_b', 'q_w', 'q_b', 'k_w', 'k_b', 'fp_w', 'fp_b')}
    del _L0_gnn_all

    def _L1_gnn_setup():
        import jax, jax.numpy as jnp
        import numpy as np
        B, N, D_IN, D_OUT = (16, 512, 128, 128)
        NEG_INF = -9000000000000000.0
        LRELU_SLOPE = 0.2
        key = jax.random.key(seed)
        k1, k2, k3, k4 = jax.random.split(key, 4)
        x = jax.random.normal(k1, (B, N, D_IN), dtype=jnp.float32)
        adj_matrix = jax.random.randint(k2, (B, N, N), 0, 2).astype(jnp.float32)
        w_lim = float(np.sqrt(6.0 / (D_IN + D_OUT)))
        a_lim = float(np.sqrt(6.0 / (2 * D_OUT + 1)))
        W = jax.random.uniform(k3, (D_IN, D_OUT), minval=-w_lim, maxval=w_lim, dtype=jnp.float32)
        a = jax.random.uniform(k4, (2 * D_OUT, 1), minval=-a_lim, maxval=a_lim, dtype=jnp.float32)
        return {'x': x, 'adj_matrix': adj_matrix, 'W': W, 'a': a}
    _L1_gnn_all = _L1_gnn_setup()
    _L1_gnn_in = {k: v for k, v in _L1_gnn_all.items() if k in ('W', 'a')}
    del _L1_gnn_all

    def _L2_gnn_setup():
        import jax, jax.numpy as jnp
        import numpy as np
        D_IN = 128
        D_HID = 256
        key = jax.random.key(seed)
        k1, k2, k3, k4, k5, k6 = jax.random.split(key, 6)
        x = jax.random.normal(k1, (8, 2048, D_IN), dtype=jnp.float32)
        adj = jax.random.uniform(k2, (8, 2048, 2048), dtype=jnp.float32)
        s1 = 1.0 / np.sqrt(D_IN)
        s2 = 1.0 / np.sqrt(D_HID)
        W1 = jax.random.uniform(k3, (D_IN, D_HID), dtype=jnp.float32, minval=-s1, maxval=s1)
        b1 = jax.random.uniform(k4, (D_HID,), dtype=jnp.float32, minval=-s1, maxval=s1)
        W2 = jax.random.uniform(k5, (D_HID, D_IN), dtype=jnp.float32, minval=-s2, maxval=s2)
        b2 = jax.random.uniform(k6, (D_IN,), dtype=jnp.float32, minval=-s2, maxval=s2)
        eps = jnp.zeros((1,), dtype=jnp.float32)
        return {'x': x, 'adj': adj, 'eps': eps, 'W1': W1, 'b1': b1, 'W2': W2, 'b2': b2}
    _L2_gnn_all = _L2_gnn_setup()
    _L2_gnn_in = {k: v for k, v in _L2_gnn_all.items() if k in ('eps', 'W1', 'b1', 'W2', 'b2')}
    del _L2_gnn_all

    def _L3_gnn_setup():
        import jax, jax.numpy as jnp
        import numpy as np
        B, N, D, C, L = (64, 256, 128, 128, 5)
        EDGE_P = 0.02

        def _gru_cell(m, h, w_ih, w_hh, b_ih, b_hh):
            gi = m @ w_ih.T + b_ih
            gh = h @ w_hh.T + b_hh
            i_r, i_z, i_n = jnp.split(gi, 3, axis=-1)
            h_r, h_z, h_n = jnp.split(gh, 3, axis=-1)
            r = jax.nn.sigmoid(i_r + h_r)
            z = jax.nn.sigmoid(i_z + h_z)
            n = jnp.tanh(i_n + r * h_n)
            return (1.0 - z) * n + z * h
        key = jax.random.key(seed)
        ks = jax.random.split(key, 8)
        x = jax.random.normal(ks[0], (B, N, D), dtype=jnp.float32)
        adj = (jax.random.uniform(ks[1], (B, N, N)) < EDGE_P).astype(jnp.float32)
        mask = jnp.ones((B, N), dtype=jnp.float32)
        s = 1.0 / np.sqrt(C).astype(np.float32)
        weight = jax.random.uniform(ks[2], (L, C, C), minval=-s, maxval=s, dtype=jnp.float32)
        w_ih = jax.random.uniform(ks[3], (3 * C, C), minval=-s, maxval=s, dtype=jnp.float32)
        w_hh = jax.random.uniform(ks[4], (3 * C, C), minval=-s, maxval=s, dtype=jnp.float32)
        b_ih = jax.random.uniform(ks[5], (3 * C,), minval=-s, maxval=s, dtype=jnp.float32)
        b_hh = jax.random.uniform(ks[6], (3 * C,), minval=-s, maxval=s, dtype=jnp.float32)
        return dict(x=x, adj=adj, mask=mask, weight=weight, w_ih=w_ih, w_hh=w_hh, b_ih=b_ih, b_hh=b_hh)
    _L3_gnn_all = _L3_gnn_setup()
    _L3_gnn_in = {k: v for k, v in _L3_gnn_all.items() if k in ('weight', 'w_ih', 'w_hh', 'b_ih', 'b_hh')}
    del _L3_gnn_all
    return {'x': x, 'adj': adj, 'nodemask': nodemask, 'L0_gnn_fc_w': _L0_gnn_in['fc_w'], 'L0_gnn_fc_b': _L0_gnn_in['fc_b'], 'L0_gnn_q_w': _L0_gnn_in['q_w'], 'L0_gnn_q_b': _L0_gnn_in['q_b'], 'L0_gnn_k_w': _L0_gnn_in['k_w'], 'L0_gnn_k_b': _L0_gnn_in['k_b'], 'L0_gnn_fp_w': _L0_gnn_in['fp_w'], 'L0_gnn_fp_b': _L0_gnn_in['fp_b'], 'L1_gnn_W': _L1_gnn_in['W'], 'L1_gnn_a': _L1_gnn_in['a'], 'L2_gnn_eps': _L2_gnn_in['eps'], 'L2_gnn_W1': _L2_gnn_in['W1'], 'L2_gnn_b1': _L2_gnn_in['b1'], 'L2_gnn_W2': _L2_gnn_in['W2'], 'L2_gnn_b2': _L2_gnn_in['b2'], 'L3_gnn_weight': _L3_gnn_in['weight'], 'L3_gnn_w_ih': _L3_gnn_in['w_ih'], 'L3_gnn_w_hh': _L3_gnn_in['w_hh'], 'L3_gnn_b_ih': _L3_gnn_in['b_ih'], 'L3_gnn_b_hh': _L3_gnn_in['b_hh']}

def reference(x, adj, nodemask, L0_gnn_fc_w, L0_gnn_fc_b, L0_gnn_q_w, L0_gnn_q_b, L0_gnn_k_w, L0_gnn_k_b, L0_gnn_fp_w, L0_gnn_fp_b, L1_gnn_W, L1_gnn_a, L2_gnn_eps, L2_gnn_W1, L2_gnn_b1, L2_gnn_W2, L2_gnn_b2, L3_gnn_weight, L3_gnn_w_ih, L3_gnn_w_hh, L3_gnn_b_ih, L3_gnn_b_hh):
    import jax
    import jax.numpy as jnp

    def _L0_gnn_ref(feats, adj_mat, fc_w, fc_b, q_w, q_b, k_w, k_b, fp_w, fp_b):
        import jax, jax.numpy as jnp
        import numpy as np
        DIM = 128
        HEADS = 8
        BS = 8
        N = 512
        NEG = -1000000000.0
        bs, n, dim = feats.shape
        feat_proj = (feats @ fc_w + fc_b).reshape(bs, n, HEADS, dim).transpose(0, 2, 1, 3)
        q = feat_proj @ q_w + q_b
        k = feat_proj @ k_w + k_b
        logits = q + jnp.swapaxes(k, -1, -2)
        masked = logits + (1.0 - adj_mat[:, None]) * NEG
        masked = jax.nn.leaky_relu(masked, negative_slope=0.01)
        attn = jax.nn.softmax(masked, axis=-1)
        out = attn @ feat_proj
        out = out.transpose(0, 2, 1, 3).reshape(bs, n, HEADS * dim)
        out = out @ fp_w + fp_b + feats
        return jax.nn.sigmoid(out)

    def _L1_gnn_ref(x, adj_matrix, W, a):
        import jax, jax.numpy as jnp
        import numpy as np
        B, N, D_IN, D_OUT = (16, 512, 128, 128)
        NEG_INF = -9000000000000000.0
        LRELU_SLOPE = 0.2
        h = jnp.einsum('bni,io->bno', x, W)
        d = h.shape[-1]
        a1 = a[:d, 0]
        a2 = a[d:, 0]
        src = h @ a1
        dst = h @ a2
        e = src[:, :, None] + dst[:, None, :]
        e = jnp.where(e >= 0, e, LRELU_SLOPE * e)
        masked_e = jnp.where(adj_matrix > 0, e, NEG_INF)
        attention = jax.nn.softmax(masked_e, axis=2)
        h_out = jnp.einsum('bij,bjd->bid', attention, h)
        return h_out

    def _L2_gnn_ref(x, adj, eps, W1, b1, W2, b2):
        import jax, jax.numpy as jnp
        import numpy as np
        D_IN = 128
        D_HID = 256
        aggregated = jnp.einsum('bnm,bmd->bnd', adj, x)
        h = (1.0 + eps) * x + aggregated
        h = jax.nn.relu(h @ W1 + b1)
        return h @ W2 + b2

    def _L3_gnn_ref(x, adj, mask, weight, w_ih, w_hh, b_ih, b_hh):
        import jax, jax.numpy as jnp
        import numpy as np
        B, N, D, C, L = (64, 256, 128, 128, 5)
        EDGE_P = 0.02

        def _gru_cell(m, h, w_ih, w_hh, b_ih, b_hh):
            gi = m @ w_ih.T + b_ih
            gh = h @ w_hh.T + b_hh
            i_r, i_z, i_n = jnp.split(gi, 3, axis=-1)
            h_r, h_z, h_n = jnp.split(gh, 3, axis=-1)
            r = jax.nn.sigmoid(i_r + h_r)
            z = jax.nn.sigmoid(i_z + h_z)
            n = jnp.tanh(i_n + r * h_n)
            return (1.0 - z) * n + z * h
        A = (adj != 0).astype(x.dtype)
        h = x
        for l in range(weight.shape[0]):
            m = jnp.einsum('bnd,de->bne', h, weight[l])
            agg = jnp.einsum('bij,bid->bjd', A, m)
            h = _gru_cell(agg, h, w_ih, w_hh, b_ih, b_hh)
        return h * mask[..., None]
    h = jnp.maximum(_layernorm(x, axis=-1), 0.0)
    x = x + _L0_gnn_ref(h, adj, L0_gnn_fc_w, L0_gnn_fc_b, L0_gnn_q_w, L0_gnn_q_b, L0_gnn_k_w, L0_gnn_k_b, L0_gnn_fp_w, L0_gnn_fp_b)
    h = jnp.maximum(_layernorm(x, axis=-1), 0.0)
    x = x + _L1_gnn_ref(h, adj, L1_gnn_W, L1_gnn_a)
    h = jnp.maximum(_layernorm(x, axis=-1), 0.0)
    x = x + _L2_gnn_ref(h, adj, L2_gnn_eps, L2_gnn_W1, L2_gnn_b1, L2_gnn_W2, L2_gnn_b2)
    h = jnp.maximum(_layernorm(x, axis=-1), 0.0)
    x = x + _L3_gnn_ref(h, adj, nodemask, L3_gnn_weight, L3_gnn_w_ih, L3_gnn_w_hh, L3_gnn_b_ih, L3_gnn_b_hh)
    return x

_drawn_inputs = setup_inputs


def setup_inputs(seed=0):
    import zlib

    import numpy as np

    out = dict(_drawn_inputs(seed))
    spreads = {'L0_gnn_fc_b': (0.0, 0.1), 'L0_gnn_fp_b': (0.0, 0.1)}
    factors = {'L0_gnn_q_w': 8.0, 'L0_gnn_k_w': 4.15}
    for name, (base, spread) in spreads.items():
        noise = np.random.default_rng([zlib.crc32(name.encode()), seed]).standard_normal(out[name].shape)
        drawn = base * np.exp(spread * noise) if base else spread * noise
        out[name] = jnp.asarray(drawn.astype(out[name].dtype))
    for name, factor in factors.items():
        out[name] = (out[name] * factor).astype(out[name].dtype)
    return out
```

```python
import concourse.bass as bass
from concourse import mybir
from contextlib import ExitStack

B, N, D = 128, 128, 128
HEADS = 8
HID = 256
LAYERS = 5
GB = 4
W4 = GB * N
S = 4
NB = S * GB
ITERS = B // NB
BANKS = 8
LN_EPS = 1e-5
K_ROWS, Q_ROWS, LO = 0, 64, 32


class Signal:

    def __init__(self, sem, per, unit=1):
        self.sem, self.per, self.unit = sem, per, unit

    def at(self, it, k):
        return it * (self.per * self.unit) + (self.per + k + 1) * self.unit


def schedule():
    pe, rest = [], []

    def add(steps, kind, *index):
        if 0 <= index[-1] < (NB if kind in ("S", "U", "E", "PT", "O") else LAYERS * S if kind in SLOTS else S):
            steps.append((kind, *index))

    SLOTS = ("T", "AG", "GA", "GB", "EW")

    def fill(steps, tick, j):
        for kind, *index in FILL[j]:
            add(steps, kind, *index[:-1], tick + index[-1])

    FILL = [
        [("LN", 0, 1), ("D1", -2), ("V1", -2), ("Z", -3)],
        [("HT", 0, 1), ("E1", -2), ("H", -3)],
        [("X1", -1), ("LN", 1, -1), ("KQ", 1), ("PT1", -2), ("Y", -3), ("LN", 3, -3)],
        [("ADJ", 1), ("XB", 1), ("HT", 1, -1), ("O1", -2), ("LN", 2, -2), ("HT3", -3)],
    ]
    both = (pe, rest)
    for steps in both:
        for j in range(GB):
            fill(steps, -1, j)
    add(pe, "S", 0)
    for b in range(NB + 3):
        tick, j = divmod(b, GB)
        add(pe, "U", b)
        fill(pe, tick, j)
        add(pe, "O", b - 3)
        add(pe, "S", b + 1) if b + 1 else None
        add(pe, "PT", b - 2)
        add(rest, "PT", b - 3)
        add(rest, "S", b)
        add(rest, "E", b - 1)
        add(rest, "U", b)
        add(rest, "O", b - 3)
        fill(rest, tick, j)
    left = [divmod(b, GB) for b in range(NB + 3, (S + 3) * GB)]
    while left and left[0] <= (S + 1, 1):
        for steps in both:
            fill(steps, *left[0])
        left.pop(0)
    slots = LAYERS * S
    for s in range(-2, slots + 2):
        for steps in both:
            for tick, j in left[:2]:
                fill(steps, tick, j)
            for kind, t in (("GA", s), ("AG", s + 1), ("GB", s), ("T", s + 2), ("EW", s - 1)):
                add(steps, kind, t)
            if s - 2 >= slots - S:
                steps.append(("XT", s - 2 - (slots - S)))
        left = left[2:]
    return pe, rest


def adj_gnn_stack_kernel(nc, x, adj, maskT, ident_in, fcwT, fpw, fcb, qkw, qkb, fpb, l1W, l1WT, l1a,
                         eps, l2W1, l2b1, l2W2, l2b2, l3wT, wihT, whhT, bih, bhh, out):
    f32, f16 = mybir.dt.float32, mybir.dt.float16
    ALU, ACT, AX = mybir.AluOpType, mybir.ActivationFunctionType, mybir.AxisListType
    PE_STEPS, STEPS = schedule()

    x_flat, adj_flat, out_flat = (t.rearrange("b n d -> (b n d)") for t in (x, adj, out))

    ctx = ExitStack()
    with ctx:
        def sb(name, shape, dt=f32):
            return ctx.enter_context(nc.sbuf_tensor(name, shape, dt))

        def sem(name):
            return ctx.enter_context(nc.semaphore(name))

        signals = []

        def signal(name, per, unit=1):
            s = Signal(sem(name), per, unit)
            signals.append(s)
            return s

        bank = [ctx.enter_context(nc.psum_tensor(f"bank{i}", [128, W4], f32)) for i in range(BANKS)]

        ident = sb("ident", [128, 128])
        ident16 = sb("ident16", [128, 128], f16)
        sel_k = sb("sel_k", [128, HEADS, 128], f16)
        sel_q = sb("sel_q", [128, HEADS, 128], f16)
        G_hi = sb("G_hi", [128, HEADS * D], f16)
        G_lo = sb("G_lo", [128, HEADS * D], f16)
        wkq_hi = sb("wkq_hi", [128, 128], f16)
        wkq_lo = sb("wkq_lo", [128, 128], f16)
        kq_bias = sb("kq_bias", [128, 1])
        l0_bias = sb("l0_bias", [128, 128])
        W_hi = sb("W_hi", [128, 128], f16)
        W_lo = sb("W_lo", [128, 128], f16)
        wsrc_hi = sb("wsrc_hi", [128, 128], f16)
        wsrc_lo = sb("wsrc_lo", [128, 128], f16)
        wdst_hi = sb("wdst_hi", [128, 128], f16)
        wdst_lo = sb("wdst_lo", [128, 128], f16)
        ident_eps = sb("ident_eps", [128, 128])
        W1_hi = sb("W1_hi", [128, HID], f16)
        W1_lo = sb("W1_lo", [128, HID], f16)
        b1_sb = sb("b1_sb", [128, 2])
        W2_sb = sb("W2_sb", [128, 2, D])
        b2_sb = sb("b2_sb", [128, D])
        wih_hi = sb("wih_hi", [128, LAYERS, 3 * D], f16)
        wih_lo = sb("wih_lo", [128, LAYERS, 3 * D], f16)
        whh_hi = sb("whh_hi", [128, 3 * D], f16)
        whh_lo = sb("whh_lo", [128, 3 * D], f16)
        bih_sb = sb("bih_sb", [128, 3])
        bhh_sb = sb("bhh_sb", [128, 3])
        brz_sb = sb("brz_sb", [128, 2])
        minus_half = sb("minus_half", [128, GB])
        ln_eps = sb("ln_eps", [128, GB])
        half_col = sb("half_col", [128, 1])

        s_w = sem("weights_loaded")
        s_zero = sem("zeroed")
        s_sel = sem("selectors_ready")
        s_pp = sem("prep_products")
        s_pv = sem("prep_vector")
        with ExitStack() as prep:
            def tmp(name, shape, dt=f32):
                return prep.enter_context(nc.sbuf_tensor(name, shape, dt))

            fcwT_sb = tmp("fcwT_sb", [128, HEADS, D])
            fpw_sb = tmp("fpw_sb", [128, HEADS, D])
            fcb_sb = tmp("fcb_sb", [128, HEADS])
            qkw_sb = tmp("qkw_sb", [128, 2])
            qkb_sb = tmp("qkb_sb", [1, 2])
            fpb_sb = tmp("fpb_sb", [1, D])
            fcb_rep = tmp("fcb_rep", [128, HEADS, 128])
            fcb_k = tmp("fcb_k", [128, 128])
            fcb_q = tmp("fcb_q", [128, 128])
            k_ind = tmp("k_ind", [1, 128])
            q_ind = tmp("q_ind", [1, 128])
            ones_row = tmp("ones_row", [1, 128])
            l1W_sb = tmp("l1W_sb", [128, 128])
            l1WT_sb = tmp("l1WT_sb", [128, 128])
            l1a_sb = tmp("l1a_sb", [128, 2])
            eps_sb = tmp("eps_sb", [128, 1])
            W1_sb = tmp("W1_sb", [128, HID])
            wT_sb = tmp("wT_sb", [128, LAYERS, D])
            wihT_sb = tmp("wihT_sb", [128, 3 * D])
            whhT_sb = tmp("whhT_sb", [128, 3 * D])
            wkq = tmp("wkq", [128, 128])
            loads = [(ident, ident_in), (fcwT_sb, fcwT), (fpw_sb, fpw), (fcb_sb, fcb), (qkw_sb, qkw),
                     (qkb_sb, qkb), (fpb_sb, fpb), (l1W_sb, l1W), (l1WT_sb, l1WT), (l1a_sb, l1a),
                     (W1_sb, l2W1), (b1_sb, l2b1), (W2_sb, l2W2), (wT_sb, l3wT), (wihT_sb, wihT),
                     (whhT_sb, whhT), (bih_sb, bih), (bhh_sb, bhh)]
            WL = 16 * (len(loads) + 2)
            P_G0, P_G1, P_WKQ, P_BKQ, P_B0, P_SRC, P_L3 = 1, 2, 3, 4, 5, 6, 7
            src_dst_ps = bank[5]

            with nc.Block() as block:
                @block.sync
                def _(sp):
                    for dst, src in loads:
                        sp.dma_start(dst[...], src).then_inc(s_w, 16)
                    sp.dma_start(eps_sb[:, :], eps.partition_broadcast(128)).then_inc(s_w, 16)
                    sp.dma_start(b2_sb[:, :], l2b2.partition_broadcast(128)).then_inc(s_w, 16)

                @block.gpsimd
                def _(pool):
                    pool.memset(minus_half[:, :], -0.5)
                    pool.memset(ln_eps[:, :], LN_EPS)
                    pool.memset(half_col[:, :], 0.5)
                    pool.memset(sel_k[:, :, :], 0.0).then_inc(s_zero, 1)
                    pool.memset(sel_q[:, :, :], 0.0).then_inc(s_zero, 1)
                    pool.wait_ge(s_zero, 2)
                    n = 0
                    for rows, tile in ((K_ROWS, sel_k), (Q_ROWS, sel_q)):
                        for part in (0, LO):
                            if n:
                                pool.wait_ge(s_sel, n)
                            pool.affine_select(out=tile[:, :, :], in_=tile[:, :, :], compare_op=ALU.not_equal,
                                               fill=1.0, base=-(rows + part), pattern=[[-1, HEADS], [0, 128]],
                                               channel_multiplier=1).then_inc(s_sel, 1)
                            n += 1

                @block.tensor
                def _(pe):
                    pe.wait_ge(s_w, WL)
                    for half in range(2):
                        for h in range(4):
                            hh = 4 * half + h
                            mm = nc.tensor.matmul(bank[half][:, h * D:(h + 1) * D], fcwT_sb[:, hh, :],
                                                  fpw_sb[:, hh, :], start=True, stop=True)
                        mm.then_inc(s_pp, 1)
                    for h in range(HEADS):
                        mm = nc.tensor.matmul(bank[2][:, 2 * h:2 * h + 2], fcwT_sb[:, h, :], qkw_sb[:, :],
                                              start=True, stop=True)
                    mm.then_inc(s_pp, 1)
                    pe.wait_ge(s_pv, 3)
                    nc.tensor.matmul(bank[3][:, 0:1], fcb_k[:, :], qkw_sb[:, 1:2], start=True, stop=False)
                    nc.tensor.matmul(bank[3][:, 0:1], fcb_q[:, :], qkw_sb[:, 0:1], start=False, stop=False)
                    nc.tensor.matmul(bank[3][:, 0:1], k_ind[:, :], qkb_sb[:, 1:2], start=False, stop=False)
                    nc.tensor.matmul(bank[3][:, 0:1], q_ind[:, :], qkb_sb[:, 0:1], start=False,
                                     stop=True).then_inc(s_pp, 1)
                    for h in range(HEADS):
                        nc.tensor.matmul(bank[4][:, 0:D], fcb_rep[:, h, :], fpw_sb[:, h, :], start=(h == 0), stop=False)
                    nc.tensor.matmul(bank[4][:, 0:D], ones_row[:, :], fpb_sb[:, :], start=False,
                                     stop=True).then_inc(s_pp, 1)
                    nc.tensor.matmul(src_dst_ps[:, 0:2], l1WT_sb[:, :], l1a_sb[:, :], start=True,
                                     stop=True).then_inc(s_pp, 1)
                    for l in range(LAYERS):
                        if l >= 2:
                            pe.wait_ge(s_pv, 100 + 2 * (l - 1))
                        nc.tensor.matmul(bank[6 + l % 2][:, 0:3 * D], wT_sb[:, l, :], wihT_sb[:, :], start=True,
                                         stop=True).then_inc(s_pp, 1)

                @block.vector
                def _(dve):
                    v = nc.vector
                    done = [0]

                    def own(ins):
                        ins.then_inc(s_pv, 1)
                        done[0] += 1
                        return done[0]

                    dve.wait_ge(s_w, WL)
                    own(v.memset(fcb_k[:, :], 0.0))
                    own(v.memset(fcb_q[:, :], 0.0))
                    dve.wait_ge(s_pv, 2)
                    for part in (0, LO):
                        v.tensor_copy(fcb_k[:, K_ROWS + part:K_ROWS + part + HEADS], fcb_sb[:, :])
                        v.tensor_copy(fcb_q[:, Q_ROWS + part:Q_ROWS + part + HEADS], fcb_sb[:, :])
                    for ind, rows in ((k_ind, K_ROWS), (q_ind, Q_ROWS)):
                        v.memset(ind[:, 0:rows], 0.0) if rows else None
                        v.memset(ind[:, rows + HEADS:rows + LO], 0.0)
                        v.memset(ind[:, rows + LO + HEADS:128], 0.0)
                        for part in (0, LO):
                            v.memset(ind[:, rows + part:rows + part + HEADS], 1.0)
                    v.memset(ones_row[:, :], 1.0)
                    own(v.tensor_copy(fcb_rep[:, :, :], fcb_sb[:, :].unsqueeze(2).broadcast_to([128, HEADS, 128])))

                    def split(src, hi, lo):
                        n = own(v.tensor_copy(hi, src))
                        dve.wait_ge(s_pv, n)
                        return own(v.tensor_tensor(lo, src, hi, ALU.subtract))

                    own(v.tensor_copy(ident16[:, :], ident[:, :]))
                    for half in range(2):
                        dve.wait_ge(s_pp, P_G0 + half)
                        c = slice(half * 4 * D, (half + 1) * 4 * D)
                        split(bank[half][:, :], G_hi[:, c], G_lo[:, c])
                    dve.wait_ge(s_pp, P_WKQ)
                    n = own(v.memset(wkq[:, :], 0.0))
                    dve.wait_ge(s_pv, n)
                    qk = bank[2][:, 0:2 * HEADS].rearrange("p (h t) -> p t h", t=2)
                    for part in (0, LO):
                        own(v.tensor_copy(wkq[:, Q_ROWS + part:Q_ROWS + part + HEADS], qk[:, 0, :]))
                        n = own(v.tensor_copy(wkq[:, K_ROWS + part:K_ROWS + part + HEADS], qk[:, 1, :]))
                    dve.wait_ge(s_pv, n)
                    split(wkq[:, :], wkq_hi[:, :], wkq_lo[:, :])
                    dve.wait_ge(s_pp, P_BKQ)
                    own(v.tensor_copy(kq_bias[:, :], bank[3][:, 0:1]))
                    dve.wait_ge(s_pp, P_B0)
                    own(v.tensor_copy(l0_bias[:, :], bank[4][:, 0:D]))
                    dve.wait_ge(s_pp, P_SRC)
                    split(l1W_sb[:, :], W_hi[:, :], W_lo[:, :])
                    split(src_dst_ps[:, 0:1].broadcast_to([128, 128]), wsrc_hi[:, :], wsrc_lo[:, :])
                    split(src_dst_ps[:, 1:2].broadcast_to([128, 128]), wdst_hi[:, :], wdst_lo[:, :])
                    n = own(v.tensor_scalar(eps_sb[:, :], eps_sb[:, :], 1.0, None, ALU.add))
                    dve.wait_ge(s_pv, n)
                    own(v.tensor_scalar(ident_eps[:, :], ident[:, :], eps_sb[:, 0:1], None, ALU.mult))
                    split(W1_sb[:, :], W1_hi[:, :], W1_lo[:, :])
                    split(whhT_sb[:, :], whh_hi[:, :], whh_lo[:, :])
                    own(v.tensor_tensor(brz_sb[:, :], bih_sb[:, 0:2], bhh_sb[:, 0:2], ALU.add))
                    assert done[0] <= 100
                    v.memset(ones_row[:, :], 1.0).then_inc(s_pv, 100 - done[0])
                    done[0] = 100
                    for l in range(LAYERS):
                        dve.wait_ge(s_pp, P_L3 + l)
                        split(bank[6 + l % 2][:, 0:3 * D], wih_hi[:, l, :], wih_lo[:, l, :])

        x_in = sb("x_in", [128, S, W4])
        adj_in = sb("adj_in", [128, S, W4])
        mask_in = sb("mask_in", [128, NB])
        xw = sb("xw", [128, S, W4])
        l0_mask = sb("l0_mask_t", [128, 2, W4])
        l1_mask = sb("l1_mask_t", [128, S, W4], mybir.dt.bfloat16)
        adj_self = sb("adj_self_t", [128, S, W4])
        edges = sb("edges_t", [128, S, W4], f16)
        ln_stats_t = sb("ln_stats_t", [128, 2, GB, 6])
        ln_mom_t = sb("ln_mom_t", [128, 2, GB, 2])
        ln_rstd_t = sb("ln_rstd_t", [128, 2, GB])
        ln_var_t = sb("ln_var_t", [128, 2, GB])
        ln_shift_t = sb("ln_shift_t", [128, 2, GB])
        hn = [sb(f"hn{n}", [128, 2, W4]) for n in range(4)]
        hT_hi_t = [sb(f"hT_hi{n}", [128, 2, W4], f16) for n in range(2)]
        hT_lo_t = [sb(f"hT_lo{n}", [128, 2, W4], f16) for n in range(2)]
        h0b = sb("h0b", [128, 2, W4])
        x_half_t = sb("x_half_t", [128, 2, W4])
        kq = sb("kq", [128, 2, W4], f16)
        RT, RP, RU, RPT = 2, 3, 3, 2
        logit = sb("logit", [128, RT, HEADS * N])
        negmax = sb("negmax", [128, RT, HEADS])
        prob = sb("prob", [128, RP, HEADS * N])
        rowsum = sb("rowsum", [128, RP, HEADS])
        rowinv = sb("rowinv", [128, RP, HEADS])
        probT = sb("probT", [128, RPT, HEADS * N])
        u_t = sb("u_t", [128, RU, HEADS * D])
        e1_t = sb("e1_t", [128, 2, W4])
        negmax1 = sb("negmax1", [128, 2, GB])
        prob1 = sb("prob1", [128, 2, W4])
        rowsum1 = sb("rowsum1", [128, 2, GB])
        rowinv1 = sb("rowinv1", [128, 2, GB])
        prob1T = sb("prob1T", [128, 2, W4])
        v_t = sb("v_t", [128, 2, W4])
        x2b = sb("x2b", [128, 2, W4])
        z_hi_t = sb("z_hi_t", [128, 2, W4], f16)
        z_lo_t = sb("z_lo_t", [128, 2, W4], f16)
        hid_t = sb("hid_t", [128, 2, 2, W4])
        hs = sb("hs", [128, S, W4])
        hs_hi = sb("hs_hi", [128, S, W4], f16)
        hs_lo = sb("hs_lo", [128, S, W4], f16)
        nat = sb("nat", [128, 2, 2 * W4], f16)
        agg_hi_t = sb("agg_hi_t", [128, 2, W4], f16)
        agg_lo_t = sb("agg_lo_t", [128, 2, W4], f16)
        rn_t, z_t, diff_t = (u_t[:, i, :].rearrange("p (r c) -> p r c", r=2) for i in range(RU))

        x_loaded = [signal(f"x_loaded{g}", 1, 16) for g in range(S)]
        adj_loaded = [signal(f"adj_loaded{g}", 1, 16) for g in range(S)]
        mask_loaded = signal("mask_loaded", 1, 16)
        out_stored = [signal(f"out_stored{g}", 1, 16) for g in range(S)]
        ln_stats = signal("ln_stats", 4 * S * GB)
        ln_moments = signal("ln_moments", 4 * S * GB)
        ln_var = signal("ln_var", 4 * S)
        ln_rstd = signal("ln_rstd", 4 * S)
        ln_shift = signal("ln_shift", 4 * S)
        h_normed = signal("h_normed", 4 * S * GB)
        hT_ready = signal("hT_ready", 2 * S)
        hT_hi = signal("hT_hi", 2 * S)
        hT_lo = signal("hT_lo", 2 * S)
        kq_ready = signal("kq_ready", S)
        kq_hi = signal("kq_hi", S)
        kq_lo = signal("kq_lo", 2 * S)
        adjT_ready = signal("adjT_ready", S)
        adj_self_ready = signal("adj_self_ready", S)
        l1_mask_ready = signal("l1_mask_ready", S)
        edges_ready = signal("edges_ready", S)
        l0_mask_ready = signal("l0_mask_ready", S)
        h0_biased = signal("h0_biased", S)
        x_half = signal("x_half", S)
        s_ready = signal("s_ready", 2 * NB)
        s_masked = signal("s_masked", 2 * NB)
        s_leaky = signal("s_leaky", 2 * NB)
        s_negmax = signal("s_negmax", 2 * NB)
        exps = signal("exps", HEADS * NB)
        row_inv = signal("row_inv", NB)
        prob_normed = signal("prob_normed", 2 * NB)
        probT_ready = signal("probT_ready", 2 * NB)
        probT_act = signal("probT_act", NB)
        probT_dve = signal("probT_dve", NB)
        u_ready = signal("u_ready", 2 * NB)
        u_kept = signal("u_kept", 2 * NB)
        o_ready = signal("o_ready", NB)
        y_ready = signal("y_ready", NB)
        y_tanh = signal("y_tanh", S)
        x1_ready = signal("x1_ready", S)
        e_ready = signal("e_ready", S)
        e_masked = signal("e_masked", S)
        e_leaky = signal("e_leaky", S)
        e_negmax = signal("e_negmax", S)
        exps1 = signal("exps1", GB * S)
        row_inv1 = signal("row_inv1", S)
        prob1T_ready = signal("prob1T_ready", S)
        prob1T_kept = signal("prob1T_kept", S)
        v_ready = signal("v_ready", S)
        v_kept = signal("v_kept", S)
        o1_ready = signal("o1_ready", S)
        x2_ready = signal("x2_ready", GB * S)
        x2_biased = signal("x2_biased", S)
        z_ready = signal("z_ready", S)
        z_hi = signal("z_hi", S)
        z_lo = signal("z_lo", S)
        hid_ready = signal("hid_ready", 2 * S)
        hid_kept = signal("hid_kept", 2 * S)
        l2_ready = signal("l2_ready", S)
        x3_ready = signal("x3_ready", S)
        h3T_ready = signal("h3T_ready", S)
        h_init = signal("h_init", S)
        h_hi = signal("h_hi", LAYERS * S)
        h_lo = signal("h_lo", LAYERS * S)
        h_new = signal("h_new", LAYERS * S)
        nat_ready = signal("nat_ready", LAYERS * S)
        nat_kept = signal("nat_kept", LAYERS * S)
        agg_ready = signal("agg_ready", LAYERS * S)
        agg_hi = signal("agg_hi", LAYERS * S)
        agg_lo = signal("agg_lo", LAYERS * S)
        gate_ready = signal("gate_ready", 4 * LAYERS * S)
        r_gate = signal("r_gate", LAYERS * S)
        z_gate = signal("z_gate", LAYERS * S)
        hn_gated = signal("hn_gated", LAYERS * S)
        n_pre = signal("n_pre", LAYERS * S)
        n_gate = signal("n_gate", LAYERS * S)
        diff = signal("diff", LAYERS * S)
        zdiff = signal("zdiff", LAYERS * S)
        outT_ready = signal("outT_ready", S)
        out_ready = signal("out_ready", GB * S)

        LN_AT = {st[1:]: i for i, st in enumerate(st for st in STEPS if st[0] == "LN")}
        HT_AT = {st[1:]: i for i, st in enumerate(st for st in STEPS if st[0] == "HT")}

        RELEASES = {
            "HT": lambda n, g: [(hT_lo, HT_AT[n, g])],
            "KQ": lambda g: [(kq_lo, 2 * g + 1)],
            "ADJ": lambda g: [(adj_self_ready, g)],
            "S": lambda b: [(s_masked, 2 * b), (s_masked, 2 * b + 1)],
            "U": lambda b: [(u_kept, 2 * b), (u_kept, 2 * b + 1)],
            "PT": lambda b: [(probT_act, b), (probT_dve, b)],
            "O": lambda b: [(y_ready, b)],
            "D1": lambda g: [(e_masked, g)],
            "V1": lambda g: [(v_kept, g)],
            "PT1": lambda g: [(prob1T_kept, g)],
            "O1": lambda g: [(x2_ready, GB * g + GB - 1)],
            "Z": lambda g: [(z_lo, g)],
            "H": lambda g: [(hid_kept, 2 * g), (hid_kept, 2 * g + 1)],
            "Y": lambda g: [(x3_ready, g)],
            "HT3": lambda g: [(h_init, g)],
            "T": lambda s: [(nat_kept, s)],
            "AG": lambda s: [(agg_lo, s)],
            "GA": lambda s: [(r_gate, s), (hn_gated, s)],
            "GB": lambda s: [(n_pre, s), (z_gate, s)],
            "XT": lambda g: [(out_ready, GB * g + GB - 1)],
        }
        JOB, released = {}, []
        for st in PE_STEPS:
            if st[0] in RELEASES:
                JOB[st] = len(released)
                released += RELEASES[st[0]](*st[1:])

        def bank_of(step, part=0):
            return bank[(JOB[step] + part) % BANKS]

        def bank_free(it, step, part=0):
            n = JOB[step] + part
            if n >= BANKS:
                sig, k = released[n - BANKS]
                return sig.sem, sig.at(it, k)
            last = max(m for m in range(len(released)) if m % BANKS == n)
            sig, k = released[last]
            return sig.sem, sig.at(it, k - sig.per)

        def cols(b):
            return slice(b * N, (b + 1) * N)

        GROUP = GB * N * D

        def rows(t, start):
            return t[bass.ds(start, GROUP)].rearrange("(b n d) -> n b d", b=GB, n=N)

        def four(ap):
            return ap.rearrange("p (b j) -> p b j", b=GB)

        with nc.Block() as block:
            @block.sync
            def _(sp):
                def load(start, g):
                    sp.dma_start(four(x_in[:, g, :]), rows(x_flat, start)).then_inc(x_loaded[g].sem, 16)
                    sp.dma_start(four(adj_in[:, g, :]), rows(adj_flat, start)).then_inc(adj_loaded[g].sem, 16)

                for s in signals:
                    sp.sem_inc(s.sem, s.per * s.unit)
                for g in range(S):
                    load(g * GROUP, g)
                sp.dma_start(mask_in[:, :], maskT[:, 0:NB]).then_inc(mask_loaded.sem, 16)
                with sp.Fori(0, ITERS - 1) as it:
                    for g in range(S):
                        for sig in (x_half, kq_ready, adj_self_ready, edges_ready, l1_mask_ready, l0_mask_ready):
                            sp.wait_ge(sig.sem, sig.at(it, g))
                        load(it * (S * GROUP) + (S + g) * GROUP, g)
                    sp.wait_ge(out_ready.sem, out_ready.at(it, GB * S - 1))
                    sp.dma_start(mask_in[:, :], maskT[:, bass.ds(it * NB + NB, NB)]).then_inc(mask_loaded.sem, 16)
                for g in range(S):
                    sp.wait_ge(out_stored[g].sem, out_stored[g].at(ITERS - 1, 0))

            @block.tensor
            def _(pe):
                mm = nc.tensor.matmul
                pe.wait_ge(out_stored[S - 1].sem, 16)

                def split_product(dst, a_hi, a_lo, b_hi, b_lo, start, stop):
                    mm(dst, a_hi, b_hi, start=start, stop=False)
                    mm(dst, a_hi, b_lo, start=False, stop=False)
                    return mm(dst, a_lo, b_hi, start=False, stop=stop)

                with pe.Fori(0, ITERS) as it:
                    for st in PE_STEPS:
                        kind = st[0]
                        if kind == "HT":
                            _, n, g = st
                            pe.wait_ge(h_normed.sem, h_normed.at(it, GB * LN_AT[n, g] + GB - 1))
                            pe.wait_ge(*bank_free(it, st))
                            ps = bank_of(st)
                            for b in range(GB):
                                last = nc.tensor.transpose(ps[:, cols(b)], hn[n][:, g % 2, cols(b)], ident[:, :])
                            last.then_inc(hT_ready.sem, 1)
                        elif kind == "KQ":
                            g = st[1]
                            pe.wait_ge(hT_lo.sem, hT_lo.at(it, HT_AT[0, g]))
                            pe.wait_ge(*bank_free(it, st))
                            split_product(bank_of(st)[:, :], wkq_hi[:, :], wkq_lo[:, :], hT_hi_t[0][:, g % 2, :],
                                          hT_lo_t[0][:, g % 2, :], True, True).then_inc(kq_ready.sem, 1)
                        elif kind == "ADJ":
                            g = st[1]
                            pe.wait_ge(adj_loaded[g].sem, adj_loaded[g].at(it, 0))
                            pe.wait_ge(*bank_free(it, st))
                            ps = bank_of(st)
                            for b in range(GB):
                                last = nc.tensor.transpose(ps[:, cols(b)], adj_in[:, g, cols(b)], ident[:, :])
                            last.then_inc(adjT_ready.sem, 1)
                        elif kind == "S":
                            b = st[1]
                            g, j = divmod(b, GB)
                            pe.wait_ge(kq_lo.sem, kq_lo.at(it, 2 * g + 1))
                            for half in range(2):
                                pe.wait_ge(*bank_free(it, st, half))
                                ps = bank_of(st, half)
                                mm(ps[:, :], kq[:, g % 2, cols(j)], sel_q[:, 4 * half:4 * half + 4, :],
                                   start=True, stop=False)
                                for h in range(4):
                                    last = mm(ps[:, cols(h)], sel_k[:, 4 * half + h, :], kq[:, g % 2, cols(j)],
                                              start=False, stop=(h == 3))
                                last.then_inc(s_ready.sem, 1)
                        elif kind == "U":
                            b = st[1]
                            g, j = divmod(b, GB)
                            for half in range(2):
                                pe.wait_ge(*bank_free(it, st, half))
                                c = slice(half * 4 * D, (half + 1) * 4 * D)
                                split_product(bank_of(st, half)[:, :], hT_hi_t[0][:, g % 2, cols(j)],
                                              hT_lo_t[0][:, g % 2, cols(j)], G_hi[:, c], G_lo[:, c],
                                              True, True).then_inc(u_ready.sem, 1)
                        elif kind == "PT":
                            b = st[1]
                            for half in range(2):
                                pe.wait_ge(prob_normed.sem, prob_normed.at(it, 2 * b + half))
                                pe.wait_ge(*bank_free(it, st, half))
                                ps = bank_of(st, half)
                                for h in range(4):
                                    last = nc.tensor.transpose(ps[:, cols(h)], prob[:, b % RP, cols(4 * half + h)],
                                                               ident[:, :])
                                last.then_inc(probT_ready.sem, 1)
                        elif kind == "O":
                            b = st[1]
                            pe.wait_ge(probT_act.sem, probT_act.at(it, b))
                            pe.wait_ge(probT_dve.sem, probT_dve.at(it, b))
                            pe.wait_ge(u_kept.sem, u_kept.at(it, 2 * b + 1))
                            free = bank_free(it, st)
                            if free[0] not in (probT_act.sem, probT_dve.sem, u_kept.sem):
                                pe.wait_ge(*free)
                            for h in range(HEADS):
                                last = mm(bank_of(st)[:, 0:D], probT[:, b % RPT, cols(h)], u_t[:, b % RU, cols(h)],
                                          start=(h == 0), stop=(h == HEADS - 1))
                            last.then_inc(o_ready.sem, 1)
                        elif kind == "D1":
                            g = st[1]
                            pe.wait_ge(hT_lo.sem, hT_lo.at(it, HT_AT[1, g]))
                            pe.wait_ge(*bank_free(it, st))
                            ps = bank_of(st)
                            split_product(ps[:, :], wdst_hi[:, :], wdst_lo[:, :], hT_hi_t[1][:, g % 2, :],
                                          hT_lo_t[1][:, g % 2, :], True, False)
                            for b in range(GB):
                                last = split_product(ps[:, cols(b)], hT_hi_t[1][:, g % 2, cols(b)],
                                                     hT_lo_t[1][:, g % 2, cols(b)], wsrc_hi[:, :], wsrc_lo[:, :],
                                                     False, b == GB - 1)
                            last.then_inc(e_ready.sem, 1)
                        elif kind == "V1":
                            g = st[1]
                            pe.wait_ge(*bank_free(it, st))
                            for b in range(GB):
                                last = split_product(bank_of(st)[:, cols(b)], hT_hi_t[1][:, g % 2, cols(b)],
                                                     hT_lo_t[1][:, g % 2, cols(b)], W_hi[:, :], W_lo[:, :], True, True)
                            last.then_inc(v_ready.sem, 1)
                        elif kind == "PT1":
                            g = st[1]
                            pe.wait_ge(exps1.sem, exps1.at(it, GB * g + GB - 1))
                            pe.wait_ge(*bank_free(it, st))
                            for b in range(GB):
                                last = nc.tensor.transpose(bank_of(st)[:, cols(b)], prob1[:, g % 2, cols(b)], ident[:, :])
                            last.then_inc(prob1T_ready.sem, 1)
                        elif kind == "O1":
                            g = st[1]
                            pe.wait_ge(v_kept.sem, v_kept.at(it, g))
                            pe.wait_ge(prob1T_kept.sem, prob1T_kept.at(it, g))
                            pe.wait_ge(*bank_free(it, st))
                            for b in range(GB):
                                last = mm(bank_of(st)[:, cols(b)], prob1T[:, g % 2, cols(b)], v_t[:, g % 2, cols(b)],
                                          start=True, stop=True)
                            last.then_inc(o1_ready.sem, 1)
                        elif kind == "Z":
                            g = st[1]
                            pe.wait_ge(h_normed.sem, h_normed.at(it, GB * LN_AT[2, g] + GB - 1))
                            pe.wait_ge(adj_self_ready.sem, adj_self_ready.at(it, g))
                            pe.wait_ge(*bank_free(it, st))
                            for b in range(GB):
                                last = mm(bank_of(st)[:, cols(b)], hn[2][:, g % 2, cols(b)], adj_self[:, g, cols(b)],
                                          start=True, stop=True)
                            last.then_inc(z_ready.sem, 1)
                        elif kind == "H":
                            g = st[1]
                            pe.wait_ge(z_lo.sem, z_lo.at(it, g))
                            for c in range(2):
                                pe.wait_ge(*bank_free(it, st, c))
                                split_product(bank_of(st, c)[:, :], W1_hi[:, c * 128:(c + 1) * 128],
                                              W1_lo[:, c * 128:(c + 1) * 128], z_hi_t[:, g % 2, :], z_lo_t[:, g % 2, :],
                                              True, True).then_inc(hid_ready.sem, 1)
                        elif kind == "Y":
                            g = st[1]
                            pe.wait_ge(hid_kept.sem, hid_kept.at(it, 2 * g + 1))
                            pe.wait_ge(*bank_free(it, st))
                            for b in range(GB):
                                for c in range(2):
                                    last = mm(bank_of(st)[:, cols(b)], hid_t[:, g % 2, c, cols(b)], W2_sb[:, c, :],
                                              start=(c == 0), stop=(c == 1))
                            last.then_inc(l2_ready.sem, 1)
                        elif kind == "HT3":
                            g = st[1]
                            pe.wait_ge(h_normed.sem, h_normed.at(it, GB * LN_AT[3, g] + GB - 1))
                            pe.wait_ge(*bank_free(it, st))
                            for b in range(GB):
                                last = nc.tensor.transpose(bank_of(st)[:, cols(b)], hn[3][:, g % 2, cols(b)], ident[:, :])
                            last.then_inc(h3T_ready.sem, 1)
                        elif kind == "T":
                            s = st[1]
                            g = s % S
                            pe.wait_ge(h_lo.sem, h_lo.at(it, s))
                            pe.wait_ge(*bank_free(it, st))
                            ps = bank_of(st)[:, :].bitcast(f16)
                            for part, src in enumerate((hs_hi, hs_lo)):
                                for b in range(GB):
                                    last = nc.tensor.transpose(ps[:, part * W4 + b * N:part * W4 + (b + 1) * N],
                                                               src[:, g, cols(b)], ident16[:, :])
                            last.then_inc(nat_ready.sem, 1)
                        elif kind == "AG":
                            s = st[1]
                            g = s % S
                            pe.wait_ge(nat_kept.sem, nat_kept.at(it, s))
                            pe.wait_ge(*bank_free(it, st))
                            for b in range(GB):
                                for part in range(2):
                                    last = mm(bank_of(st)[:, cols(b)],
                                              nat[:, s % 2, part * W4 + b * N:part * W4 + (b + 1) * N],
                                              edges[:, g, cols(b)], start=(part == 0), stop=(part == 1))
                            last.then_inc(agg_ready.sem, 1)
                        elif kind in ("GA", "GB"):
                            s = st[1]
                            l, g = divmod(s, S)
                            gates = ((0, True, True), (2, False, True)) if kind == "GA" else \
                                ((2, True, False), (1, True, True))
                            for part, (gate, agg_in, h_in) in enumerate(gates):
                                pe.wait_ge(*bank_free(it, st, part))
                                ps = bank_of(st, part)[:, :]
                                c = slice(gate * D, (gate + 1) * D)
                                if h_in:
                                    last = split_product(ps, whh_hi[:, c], whh_lo[:, c], hs_hi[:, g, :],
                                                         hs_lo[:, g, :], True, not agg_in)
                                if agg_in:
                                    if kind == "GA":
                                        pe.wait_ge(agg_lo.sem, agg_lo.at(it, s))
                                    last = split_product(ps, wih_hi[:, l, c], wih_lo[:, l, c], agg_hi_t[:, s % 2, :],
                                                         agg_lo_t[:, s % 2, :], not h_in, True)
                                last.then_inc(gate_ready.sem, 1)
                        elif kind == "XT":
                            g = st[1]
                            pe.wait_ge(h_new.sem, h_new.at(it, (LAYERS - 1) * S + g))
                            pe.wait_ge(*bank_free(it, st))
                            for b in range(GB):
                                last = nc.tensor.transpose(bank_of(st)[:, cols(b)], hs[:, g, cols(b)], ident[:, :])
                            last.then_inc(outT_ready.sem, 1)

            @block.scalar
            def _(act):
                a = nc.scalar

                def store(it, g):
                    act.wait_ge(out_ready.sem, out_ready.at(it, GB * g + GB - 1))
                    act.dma_start(rows(out_flat, it * (S * GROUP) + g * GROUP), four(xw[:, g, :]))\
                        .then_inc(out_stored[g].sem, 16)

                act.wait_ge(out_stored[S - 1].sem, 16)
                with act.Fori(0, ITERS) as it:
                    for st in STEPS:
                        kind = st[0]
                        if kind == "LN":
                            _, n, g = st
                            k = LN_AT[n, g]
                            act.wait_ge(ln_shift.sem, ln_shift.at(it, k))
                            if n == 0:
                                act.wait_ge(h0_biased.sem, h0_biased.at(it, g - 2))
                            src = x_in if n == 0 else xw
                            for b in range(GB):
                                a.activation(hn[n][:, g % 2, cols(b)], src[:, g, cols(b)], ACT.Relu,
                                             bias=ln_shift_t[:, k % 2, b:b + 1], scale=ln_rstd_t[:, k % 2, b:b + 1])\
                                    .then_inc(h_normed.sem, 1)
                        elif kind == "HT":
                            _, n, g = st
                            act.wait_ge(hT_ready.sem, hT_ready.at(it, HT_AT[n, g]))
                            a.activation(hT_hi_t[n][:, g % 2, :], bank_of(st)[:, :], ACT.Copy).then_inc(hT_hi.sem, 1)
                        elif kind == "KQ":
                            g = st[1]
                            act.wait_ge(kq_ready.sem, kq_ready.at(it, g))
                            a.activation(kq[:, g % 2, :], bank_of(st)[:, :], ACT.Identity, bias=kq_bias[:, 0:1])\
                                .then_inc(kq_hi.sem, 1)
                        elif kind == "U":
                            b = st[1]
                            act.wait_ge(o_ready.sem, o_ready.at(it, b - RU))
                            for half in range(2):
                                act.wait_ge(u_ready.sem, u_ready.at(it, 2 * b + half))
                                a.activation(u_t[:, b % RU, half * 4 * D:(half + 1) * 4 * D], bank_of(st, half)[:, :],
                                             ACT.Copy).then_inc(u_kept.sem, 1)
                        elif kind == "E":
                            b = st[1]
                            act.wait_ge(s_negmax.sem, s_negmax.at(it, 2 * b + 1))
                            for h in range(HEADS):
                                a.activation(prob[:, b % RP, cols(h)], logit[:, b % RT, cols(h)], ACT.Exp,
                                             bias=negmax[:, b % RT, h:h + 1], accum_out=rowsum[:, b % RP, h:h + 1])\
                                    .then_inc(exps.sem, 1)
                        elif kind == "PT":
                            b = st[1]
                            act.wait_ge(probT_ready.sem, probT_ready.at(it, 2 * b))
                            act.wait_ge(o_ready.sem, o_ready.at(it, b - RPT))
                            a.activation(probT[:, b % RPT, 0:4 * N], bank_of(st)[:, :], ACT.Copy)\
                                .then_inc(probT_act.sem, 1)
                        elif kind == "X1":
                            g = st[1]
                            act.wait_ge(y_ready.sem, y_ready.at(it, GB * g + GB - 1))
                            a.activation(h0b[:, g % 2, :], h0b[:, g % 2, :], ACT.Tanh, scale=0.5).then_inc(y_tanh.sem, 1)
                        elif kind == "V1":
                            g = st[1]
                            act.wait_ge(v_ready.sem, v_ready.at(it, g))
                            act.wait_ge(o1_ready.sem, o1_ready.at(it, g - 2))
                            a.activation(v_t[:, g % 2, :], bank_of(st)[:, :], ACT.Copy).then_inc(v_kept.sem, 1)
                        elif kind == "E1":
                            g = st[1]
                            act.wait_ge(e_negmax.sem, e_negmax.at(it, g))
                            act.wait_ge(row_inv1.sem, row_inv1.at(it, g - 2))
                            for b in range(GB):
                                a.activation(prob1[:, g % 2, cols(b)], e1_t[:, g % 2, cols(b)], ACT.Exp,
                                             bias=negmax1[:, g % 2, b:b + 1], accum_out=rowsum1[:, g % 2, b:b + 1])\
                                    .then_inc(exps1.sem, 1)
                        elif kind == "PT1":
                            g = st[1]
                            act.wait_ge(prob1T_ready.sem, prob1T_ready.at(it, g))
                            a.activation(prob1T[:, g % 2, :], bank_of(st)[:, :], ACT.Copy).then_inc(prob1T_kept.sem, 1)
                        elif kind == "Z":
                            g = st[1]
                            act.wait_ge(z_ready.sem, z_ready.at(it, g))
                            a.activation(z_hi_t[:, g % 2, :], bank_of(st)[:, :], ACT.Copy).then_inc(z_hi.sem, 1)
                        elif kind == "H":
                            g = st[1]
                            act.wait_ge(l2_ready.sem, l2_ready.at(it, g - 2))
                            for c in range(2):
                                act.wait_ge(hid_ready.sem, hid_ready.at(it, 2 * g + c))
                                a.activation(hid_t[:, g % 2, c, :], bank_of(st, c)[:, :], ACT.Relu, bias=b1_sb[:, c:c + 1])\
                                    .then_inc(hid_kept.sem, 1)
                        elif kind == "HT3":
                            g = st[1]
                            act.wait_ge(h3T_ready.sem, h3T_ready.at(it, g))
                            act.wait_ge(outT_ready.sem, outT_ready.at(it, g - S))
                            a.activation(hs[:, g, :], bank_of(st)[:, :], ACT.Copy).then_inc(h_init.sem, 1)
                        elif kind == "T":
                            s = st[1]
                            act.wait_ge(nat_ready.sem, nat_ready.at(it, s))
                            a.activation(nat[:, s % 2, :], bank_of(st)[:, :].bitcast(f16), ACT.Copy).then_inc(nat_kept.sem, 1)
                        elif kind == "AG":
                            s = st[1]
                            act.wait_ge(agg_ready.sem, agg_ready.at(it, s))
                            a.activation(agg_hi_t[:, s % 2, :], bank_of(st)[:, :], ACT.Copy).then_inc(agg_hi.sem, 1)
                        elif kind == "GA":
                            s = st[1]
                            act.wait_ge(h_new.sem, h_new.at(it, s - 2))
                            act.wait_ge(gate_ready.sem, gate_ready.at(it, 4 * s))
                            a.activation(rn_t[:, s % 2, :], bank_of(st, 0)[:, :], ACT.Sigmoid, bias=brz_sb[:, 0:1])\
                                .then_inc(r_gate.sem, 1)
                        elif kind == "GB":
                            s = st[1]
                            act.wait_ge(n_pre.sem, n_pre.at(it, s))
                            a.activation(rn_t[:, s % 2, :], rn_t[:, s % 2, :], ACT.Tanh, bias=bih_sb[:, 2:3])\
                                .then_inc(n_gate.sem, 1)
                            act.wait_ge(gate_ready.sem, gate_ready.at(it, 4 * s + 3))
                            act.wait_ge(zdiff.sem, zdiff.at(it, s - 2))
                            a.activation(z_t[:, s % 2, :], bank_of(st, 1)[:, :], ACT.Sigmoid, bias=brz_sb[:, 1:2])\
                                .then_inc(z_gate.sem, 1)
                        elif kind == "XT" and st[1]:
                            store(it, st[1] - 1)
                    store(it, S - 1)

            @block.gpsimd
            def _(pool):
                p = nc.gpsimd
                pool.wait_ge(out_stored[S - 1].sem, 16)
                with pool.Fori(0, ITERS) as it:
                    for st in STEPS:
                        kind = st[0]
                        if kind == "LN":
                            k = LN_AT[st[1], st[2]]
                            pool.wait_ge(ln_moments.sem, ln_moments.at(it, GB * k + GB - 1))
                            pool.wait_ge(h_normed.sem, h_normed.at(it, GB * (k - 2) + GB - 1))
                            p.tensor_tensor(ln_var_t[:, k % 2, :], ln_mom_t[:, k % 2, :, 1], ln_eps[:, :], ALU.add)\
                                .then_inc(ln_var.sem, 1)
                            pool.wait_ge(ln_var.sem, ln_var.at(it, k))
                            p.tensor_tensor(ln_rstd_t[:, k % 2, :], ln_var_t[:, k % 2, :], minus_half[:, :], ALU.pow)\
                                .then_inc(ln_rstd.sem, 1)
                        if kind == "XB":
                            g = st[1]
                            pool.wait_ge(x_loaded[g].sem, x_loaded[g].at(it, 0))
                            pool.wait_ge(x1_ready.sem, x1_ready.at(it, g - 2))
                            p.tensor_tensor(x_half_t[:, g % 2, :], x_in[:, g, :], half_col[:, :].broadcast_to([128, W4]),
                                            ALU.add).then_inc(x_half.sem, 1)
                            pool.wait_ge(h_normed.sem, h_normed.at(it, GB * LN_AT[0, g] + GB - 1))
                            pool.wait_ge(y_ready.sem, y_ready.at(it, GB * (g - 2) + GB - 1))
                            p.tensor_tensor(four(h0b[:, g % 2, :]), four(hn[0][:, g % 2, :]),
                                            l0_bias[:, :].unsqueeze(1).broadcast_to([128, GB, D]), ALU.add)\
                                .then_inc(h0_biased.sem, 1)
                        elif kind == "E":
                            b = st[1]
                            pool.wait_ge(row_inv.sem, row_inv.at(it, b))
                            for half in range(2):
                                c = slice(half * 4 * N, (half + 1) * 4 * N)
                                p.tensor_tensor(four(prob[:, b % RP, c]), four(prob[:, b % RP, c]),
                                                rowinv[:, b % RP, 4 * half:4 * half + 4].unsqueeze(2)
                                                .broadcast_to([128, 4, N]), ALU.mult).then_inc(prob_normed.sem, 1)
                        elif kind == "LN" and st[1] == 2:
                            g = st[2]
                            pool.wait_ge(x2_ready.sem, x2_ready.at(it, GB * g + GB - 1))
                            pool.wait_ge(x3_ready.sem, x3_ready.at(it, g - 2))
                            p.tensor_tensor(four(x2b[:, g % 2, :]), four(xw[:, g, :]),
                                            b2_sb[:, :].unsqueeze(1).broadcast_to([128, GB, D]), ALU.add)\
                                .then_inc(x2_biased.sem, 1)
                        elif kind == "GB":
                            s = st[1]
                            g = s % S
                            pool.wait_ge(n_gate.sem, n_gate.at(it, s))
                            pool.wait_ge(h_new.sem, h_new.at(it, s - 2))
                            p.tensor_tensor(diff_t[:, s % 2, :], hs[:, g, :], rn_t[:, s % 2, :], ALU.subtract)\
                                .then_inc(diff.sem, 1)
                            pool.wait_ge(diff.sem, diff.at(it, s))
                            pool.wait_ge(z_gate.sem, z_gate.at(it, s))
                            p.tensor_tensor(diff_t[:, s % 2, :], diff_t[:, s % 2, :], z_t[:, s % 2, :], ALU.mult)\
                                .then_inc(zdiff.sem, 1)

            @block.vector
            def _(dve):
                v = nc.vector
                dve.wait_ge(out_stored[S - 1].sem, 16)
                with dve.Fori(0, ITERS) as it:
                    for st in STEPS:
                        kind = st[0]
                        if kind == "LN":
                            _, n, g = st
                            k = LN_AT[n, g]
                            src = x_in if n == 0 else xw
                            if n == 0:
                                dve.wait_ge(x_loaded[g].sem, x_loaded[g].at(it, 0))
                            elif n == 1:
                                dve.wait_ge(x1_ready.sem, x1_ready.at(it, g))
                            elif n == 2:
                                dve.wait_ge(x2_ready.sem, x2_ready.at(it, GB * g + GB - 1))
                            else:
                                dve.wait_ge(x3_ready.sem, x3_ready.at(it, g))
                            for b in range(GB):
                                v.bn_stats(ln_stats_t[:, k % 2, b, :], src[:, g, cols(b)]).then_inc(ln_stats.sem, 1)
                            dve.drain()
                            for b in range(GB):
                                v.bn_aggr(ln_mom_t[:, k % 2, b, :], ln_stats_t[:, k % 2, b, :]).then_inc(ln_moments.sem, 1)
                            dve.wait_ge(ln_moments.sem, ln_moments.at(it, GB * k + GB - 1))
                            dve.wait_ge(ln_rstd.sem, ln_rstd.at(it, k))
                            v.scalar_tensor_tensor(ln_shift_t[:, k % 2, :], ln_mom_t[:, k % 2, :, 0], -1.0,
                                                   ln_rstd_t[:, k % 2, :], ALU.mult, ALU.mult).then_inc(ln_shift.sem, 1)
                        elif kind == "HT":
                            _, n, g = st
                            dve.wait_ge(hT_hi.sem, hT_hi.at(it, HT_AT[n, g]))
                            v.tensor_tensor(hT_lo_t[n][:, g % 2, :], bank_of(st)[:, :], hT_hi_t[n][:, g % 2, :],
                                            ALU.subtract).then_inc(hT_lo.sem, 1)
                        elif kind == "KQ":
                            g = st[1]
                            dve.wait_ge(kq_hi.sem, kq_hi.at(it, g))
                            for rows in (K_ROWS, Q_ROWS):
                                r = slice(rows + LO, rows + 2 * LO)
                                v.scalar_tensor_tensor(kq[r, g % 2, :], bank_of(st)[r, :], kq_bias[r, 0:1],
                                                       kq[r, g % 2, :], ALU.add, ALU.subtract).then_inc(kq_lo.sem, 1)
                        elif kind == "ADJ":
                            g = st[1]
                            dve.wait_ge(adj_loaded[g].sem, adj_loaded[g].at(it, 0))
                            v.tensor_scalar(l0_mask[:, g % 2, :], adj_in[:, g, :], 1.0, 1e9, ALU.subtract, ALU.mult)\
                                .then_inc(l0_mask_ready.sem, 1)
                            dve.wait_ge(adjT_ready.sem, adjT_ready.at(it, g))
                            v.tensor_tensor(four(adj_self[:, g, :]), four(bank_of(st)[:, :]),
                                            ident_eps[:, :].unsqueeze(1).broadcast_to([128, GB, N]), ALU.add)\
                                .then_inc(adj_self_ready.sem, 1)
                            v.tensor_scalar(l1_mask[:, g, :], adj_in[:, g, :], 0.0, -9e15, ALU.is_le, ALU.mult)\
                                .then_inc(l1_mask_ready.sem, 1)
                            v.tensor_scalar(edges[:, g, :], adj_in[:, g, :], 0.0, None, ALU.not_equal)\
                                .then_inc(edges_ready.sem, 1)
                        elif kind == "S":
                            b = st[1]
                            g, j = divmod(b, GB)
                            dve.wait_ge(l0_mask_ready.sem, l0_mask_ready.at(it, g))
                            dve.wait_ge(exps.sem, exps.at(it, HEADS * (b - RT) + HEADS - 1))
                            halves = [logit[:, b % RT, half * 4 * N:(half + 1) * 4 * N] for half in range(2)]
                            for half, t in enumerate(halves):
                                dve.wait_ge(s_ready.sem, s_ready.at(it, 2 * b + half))
                                v.tensor_tensor(four(t), four(bank_of(st, half)[:, :]),
                                                l0_mask[:, g % 2, cols(j)].unsqueeze(1).broadcast_to([128, 4, N]), ALU.add)\
                                    .then_inc(s_masked.sem, 1)
                            for half, t in enumerate(halves):
                                dve.wait_ge(s_masked.sem, s_masked.at(it, 2 * b + half))
                                v.scalar_tensor_tensor(t, t, 0.01, t, ALU.mult, ALU.max).then_inc(s_leaky.sem, 1)
                            for half, t in enumerate(halves):
                                dve.wait_ge(s_leaky.sem, s_leaky.at(it, 2 * b + half))
                                v.tensor_reduce(negmax[:, b % RT, 4 * half:4 * half + 4], four(t), AX.X, ALU.max,
                                                negate=True).then_inc(s_negmax.sem, 1)
                        elif kind == "E":
                            b = st[1]
                            dve.wait_ge(exps.sem, exps.at(it, HEADS * b + HEADS - 1))
                            dve.wait_ge(prob_normed.sem, prob_normed.at(it, 2 * (b - RP) + 1))
                            v.reciprocal(rowinv[:, b % RP, :], rowsum[:, b % RP, :]).then_inc(row_inv.sem, 1)
                        elif kind == "PT":
                            b = st[1]
                            dve.wait_ge(probT_ready.sem, probT_ready.at(it, 2 * b + 1))
                            dve.wait_ge(o_ready.sem, o_ready.at(it, b - RPT))
                            v.tensor_copy(probT[:, b % RPT, 4 * N:8 * N], bank_of(st, 1)[:, :]).then_inc(probT_dve.sem, 1)
                        elif kind == "O":
                            b = st[1]
                            g, j = divmod(b, GB)
                            dve.wait_ge(o_ready.sem, o_ready.at(it, b))
                            dve.wait_ge(h0_biased.sem, h0_biased.at(it, g))
                            v.tensor_tensor(h0b[:, g % 2, cols(j)], bank_of(st)[:, 0:D], h0b[:, g % 2, cols(j)], ALU.add)\
                                .then_inc(y_ready.sem, 1)
                        elif kind == "X1":
                            g = st[1]
                            dve.wait_ge(y_tanh.sem, y_tanh.at(it, g))
                            dve.wait_ge(x_half.sem, x_half.at(it, g))
                            dve.wait_ge(out_stored[g].sem, out_stored[g].at(it, -1))
                            v.scalar_tensor_tensor(xw[:, g, :], h0b[:, g % 2, :], 0.5, x_half_t[:, g % 2, :],
                                                   ALU.mult, ALU.add).then_inc(x1_ready.sem, 1)
                        elif kind == "D1":
                            g = st[1]
                            t = e1_t[:, g % 2, :]
                            dve.wait_ge(e_ready.sem, e_ready.at(it, g))
                            dve.wait_ge(exps1.sem, exps1.at(it, GB * (g - 2) + GB - 1))
                            dve.wait_ge(l1_mask_ready.sem, l1_mask_ready.at(it, g))
                            v.tensor_tensor(t, bank_of(st)[:, :], l1_mask[:, g, :], ALU.add).then_inc(e_masked.sem, 1)
                            dve.wait_ge(e_masked.sem, e_masked.at(it, g))
                            v.scalar_tensor_tensor(t, t, 0.2, t, ALU.mult, ALU.max).then_inc(e_leaky.sem, 1)
                            dve.wait_ge(e_leaky.sem, e_leaky.at(it, g))
                            v.tensor_reduce(negmax1[:, g % 2, :], four(t), AX.X, ALU.max, negate=True)\
                                .then_inc(e_negmax.sem, 1)
                        elif kind == "E1":
                            g = st[1]
                            dve.wait_ge(exps1.sem, exps1.at(it, GB * g + GB - 1))
                            v.reciprocal(rowinv1[:, g % 2, :], rowsum1[:, g % 2, :]).then_inc(row_inv1.sem, 1)
                        elif kind == "O1":
                            g = st[1]
                            dve.wait_ge(o1_ready.sem, o1_ready.at(it, g))
                            dve.wait_ge(row_inv1.sem, row_inv1.at(it, g))
                            for b in range(GB):
                                v.scalar_tensor_tensor(xw[:, g, cols(b)], bank_of(st)[:, cols(b)],
                                                       rowinv1[:, g % 2, b:b + 1], xw[:, g, cols(b)],
                                                       ALU.mult, ALU.add).then_inc(x2_ready.sem, 1)
                        elif kind == "Z":
                            g = st[1]
                            dve.wait_ge(z_hi.sem, z_hi.at(it, g))
                            v.tensor_tensor(z_lo_t[:, g % 2, :], bank_of(st)[:, :], z_hi_t[:, g % 2, :], ALU.subtract)\
                                .then_inc(z_lo.sem, 1)
                        elif kind == "Y":
                            g = st[1]
                            dve.wait_ge(l2_ready.sem, l2_ready.at(it, g))
                            dve.wait_ge(x2_biased.sem, x2_biased.at(it, g))
                            v.tensor_tensor(xw[:, g, :], bank_of(st)[:, :], x2b[:, g % 2, :], ALU.add)\
                                .then_inc(x3_ready.sem, 1)
                        elif kind == "HT3":
                            g = st[1]
                            dve.wait_ge(h_init.sem, h_init.at(it, g))
                            v.tensor_copy(hs_hi[:, g, :], hs[:, g, :]).then_inc(h_hi.sem, 1)
                            dve.wait_ge(h_hi.sem, h_hi.at(it, g))
                            v.tensor_tensor(hs_lo[:, g, :], hs[:, g, :], hs_hi[:, g, :], ALU.subtract)\
                                .then_inc(h_lo.sem, 1)
                        elif kind == "AG":
                            s = st[1]
                            dve.wait_ge(agg_hi.sem, agg_hi.at(it, s))
                            v.tensor_tensor(agg_lo_t[:, s % 2, :], bank_of(st)[:, :], agg_hi_t[:, s % 2, :],
                                            ALU.subtract).then_inc(agg_lo.sem, 1)
                        elif kind == "GA":
                            s = st[1]
                            u = rn_t[:, s % 2, :]
                            dve.wait_ge(gate_ready.sem, gate_ready.at(it, 4 * s + 1))
                            dve.wait_ge(r_gate.sem, r_gate.at(it, s))
                            v.scalar_tensor_tensor(u, bank_of(st, 1)[:, :], bhh_sb[:, 2:3], u,
                                                   ALU.add, ALU.mult).then_inc(hn_gated.sem, 1)
                        elif kind == "GB":
                            s = st[1]
                            u = rn_t[:, s % 2, :]
                            dve.wait_ge(gate_ready.sem, gate_ready.at(it, 4 * s + 2))
                            dve.wait_ge(hn_gated.sem, hn_gated.at(it, s))
                            v.tensor_tensor(u, bank_of(st, 0)[:, :], u, ALU.add).then_inc(n_pre.sem, 1)
                        elif kind == "EW":
                            s = st[1]
                            g = s % S
                            dve.wait_ge(zdiff.sem, zdiff.at(it, s))
                            v.tensor_tensor(hs[:, g, :], diff_t[:, s % 2, :], rn_t[:, s % 2, :], ALU.add)\
                                .then_inc(h_new.sem, 1)
                            if s < (LAYERS - 1) * S:
                                dve.wait_ge(h_new.sem, h_new.at(it, s))
                                dve.wait_ge(gate_ready.sem, gate_ready.at(it, 4 * s + 3))
                                v.tensor_copy(hs_hi[:, g, :], hs[:, g, :]).then_inc(h_hi.sem, 1)
                                dve.wait_ge(h_hi.sem, h_hi.at(it, s + S))
                                v.tensor_tensor(hs_lo[:, g, :], hs[:, g, :], hs_hi[:, g, :], ALU.subtract)\
                                    .then_inc(h_lo.sem, 1)
                        elif kind == "XT":
                            g = st[1]
                            dve.wait_ge(outT_ready.sem, outT_ready.at(it, g))
                            dve.wait_ge(mask_loaded.sem, mask_loaded.at(it, 0))
                            for b in range(GB):
                                v.scalar_tensor_tensor(xw[:, g, cols(b)], bank_of(st)[:, cols(b)],
                                                       mask_in[:, g * GB + b:g * GB + b + 1], xw[:, g, cols(b)],
                                                       ALU.mult, ALU.add).then_inc(out_ready.sem, 1)


def kernel(**inputs):
    import numpy as np
    import concourse.bacc as bacc
    from concourse.bass_utils import run_bass_kernel_spmd

    a = {k: np.asarray(v) for k, v in inputs.items()}
    arrays = {
        "x": a["x"],
        "adj": a["adj"],
        "maskT": a["nodemask"].T,
        "ident": np.eye(128, dtype=np.float32),
        "fcwT": a["L0_gnn_fc_w"].reshape(D, HEADS, D).transpose(2, 1, 0),
        "fpw": a["L0_gnn_fp_w"].reshape(HEADS, D, D).transpose(1, 0, 2),
        "fcb": a["L0_gnn_fc_b"].reshape(HEADS, D).T,
        "qkw": np.concatenate([a["L0_gnn_q_w"], a["L0_gnn_k_w"]], axis=1),
        "qkb": np.concatenate([a["L0_gnn_q_b"], a["L0_gnn_k_b"]]).reshape(1, 2),
        "fpb": a["L0_gnn_fp_b"].reshape(1, D),
        "l1W": a["L1_gnn_W"],
        "l1WT": a["L1_gnn_W"].T,
        "l1a": a["L1_gnn_a"].reshape(2, D).T,
        "eps": a["L2_gnn_eps"],
        "l2W1": a["L2_gnn_W1"],
        "l2b1": a["L2_gnn_b1"].reshape(2, 128).T,
        "l2W2": a["L2_gnn_W2"].reshape(2, 128, D).transpose(1, 0, 2),
        "l2b2": a["L2_gnn_b2"],
        "l3wT": a["L3_gnn_weight"].transpose(2, 0, 1),
        "wihT": a["L3_gnn_w_ih"].T,
        "whhT": a["L3_gnn_w_hh"].T,
        "bih": a["L3_gnn_b_ih"].reshape(3, 128).T,
        "bhh": a["L3_gnn_b_hh"].reshape(3, 128).T,
    }
    nc = bacc.Bacc("TRN2", target_bir_lowering=False, num_devices=1)
    data, args = {}, []
    for name, value in arrays.items():
        value = np.ascontiguousarray(value)
        data[f"in_{name}"] = value
        args.append(nc.dram_tensor(f"in_{name}", value.shape, mybir.dt.from_np(value.dtype), kind="ExternalInput").ap())
    args.append(nc.dram_tensor("out_0", (B, N, D), mybir.dt.float32, kind="ExternalOutput").ap())
    adj_gnn_stack_kernel(nc, *args)
    r = run_bass_kernel_spmd(nc, [data], core_ids=[0])
    return r.results[0]["out_0"]
```

```python
import concourse.bass as bass
from concourse import mybir
from contextlib import ExitStack

B, N, D = 128, 128, 128
HEADS = 8
HID = 256
LAYERS = 5
GB = 4
W4 = GB * N
S = 4
NB = S * GB
ITERS = B // NB
RING_BANKS = {"pairs": (0, 1, 2), "singles": (3, 4), "gru": (5, 6, 7)}
LN_EPS = 1e-5
K_ROWS, Q_ROWS, LO = 0, 64, 32


class Signal:

    def __init__(self, sem, per, unit=1, lag=0):
        self.sem, self.per, self.unit, self.lag = sem, per, unit, lag

    def at(self, it, k):
        return it * (self.per * self.unit) + (self.per * (1 - self.lag) + k + 1) * self.unit


ORDER = {
    "tensor": """
        ADJ:0 HT3:0 ADJ:1 HT:0,0 U:0 U:1 HT3:1 KQ:0 HT:0,1 T:0 S:0 S:1 HT3:2 HT3:3 S:2 ADJ:2 U:2 KQ:1 S:3 T:1
        AG:0 T:2 PT:0 U:3 AG:1 GA:0 GB:0 T:3 O:0 S:4 PT:1 U:4 HT:0,2 AG:2 O:1 S:5 PT:2 U:5 GA:1 O:2 KQ:2 S:6
        PT:3 U:6 GB:1 O:3 S:7 PT:4 T:4 AG:3 U:7 GA:2 O:4 GB:2 HT:1,0 S:8 PT:5 U:8 T:5 AG:4 GA:3 O:5 D1:0 GB:3
        V1:0 S:9 PT:6 HT:0,3 U:9 T:6 AG:5 O:6 GA:4 GB:4 S:10 PT:7 T:7 AG:6 KQ:3 U:10 GA:5 O:7 GB:5 S:11 PT1:0
        PT:8 ADJ:3 T:8 U:11 AG:7 GA:6 O:8 S:12 HT:1,1 GB:6 O1:0 PT:9 U:12 T:9 AG:8 D1:1 O:9 GA:7 V1:1 S:13 GB:7
        Z:0 PT:10 T:10 U:13 AG:9 GA:8 O:10 H:0 GB:8 S:14 PT:11 U:14 T:11 AG:10 GA:9 O:11 PT1:1 GB:9 Y:0 S:15
        T:12 AG:11 GA:10 PT:12 O1:1 U:15 O:12 PT:13 GB:10 HT:1,2 T:13 AG:12 O:13 D1:2 GA:11 V1:2 GB:11 Z:1 PT:14
        T:14 AG:13 O:14 GA:12 H:1 GB:12 PT:15 T:15 AG:14 O:15 GA:13 GB:13 PT1:2 Y:1 O1:2 T:16 AG:15 HT:1,3 GA:14
        D1:3 GB:14 V1:3 T:17 AG:16 Z:2 GA:15 GB:15 T:18 AG:17 H:2 GA:16 PT1:3 Y:2 GB:16 T:19 AG:18 GA:17 O1:3
        GB:17 AG:19 GA:18 GB:18 XT:0 Z:3 GA:19 GB:19 XT:1 H:3 XT:2 Y:3 XT:3
    """,
    "scalar": """
        LN:3,0 HT3:0 LN:0,0 HT:0,0 U:0 LN:3,1 LN:0,1 KQ:0 HT3:1 LN:3,2 U:1 HT:0,1 LN:3,3 HT3:2 HT3:3 E:0 T:0 E:1
        U:2 KQ:1 E:2 PT:0 T:1 AG:0 T:2 E:3 AG:1 GA:0 LN:0,2 GB:0 T:3 U:3 PT:1 HT:0,2 E:4 U:4 PT:2 AG:2 E:5 U:5
        GA:1 PT:3 KQ:2 E:6 U:6 GB:1 X1:0 PT:4 T:4 AG:3 E:7 GA:2 LN:1,0 U:7 GB:2 HT:1,0 PT:5 T:5 AG:4 LN:0,3 GA:3
        U:8 E:8 GB:3 V1:0 PT:6 HT:0,3 E1:0 T:6 AG:5 U:9 GA:4 E:9 GB:4 PT:7 T:7 AG:6 KQ:3 GA:5 E:10 U:10 GB:5
        X1:1 PT1:0 PT:8 T:8 AG:7 E:11 LN:1,1 U:11 GA:6 HT:1,1 PT:9 E:12 GB:6 T:9 U:12 LN:2,0 AG:8 GA:7 V1:1 E1:1
        GB:7 Z:0 PT:10 T:10 AG:9 E:13 U:13 GA:8 H:0 GB:8 PT:11 T:11 AG:10 GA:9 E:14 U:14 GB:9 X1:2 PT1:1 T:12
        AG:11 GA:10 LN:1,2 PT:12 E:15 U:15 PT:13 GB:10 HT:1,2 T:13 AG:12 LN:2,1 GA:11 V1:2 E1:2 GB:11 Z:1 PT:14
        T:14 AG:13 GA:12 H:1 GB:12 PT:15 T:15 AG:14 X1:3 GA:13 PT1:2 GB:13 LN:1,3 T:16 HT:1,3 AG:15 GA:14 GB:14
        LN:2,2 V1:3 T:17 AG:16 Z:2 GA:15 E1:3 GB:15 T:18 AG:17 H:2 GA:16 PT1:3 GB:16 T:19 AG:18 GA:17 GB:17
        AG:19 GA:18 LN:2,3 GB:18 XT:0 Z:3 GA:19 GB:19 XT:1 H:3 XT:2 XT:3
    """,
    "gpsimd": """
        XD:0 LN:3,0 XD:1 LN:0,0 XB:0 LN:3,1 LN:0,1 XD:2 LN:3,2 XD:3 LN:3,3 XB:1 E:0 E:1 E:2 LN:0,2 E:3 GB:0 E:4
        E:5 GB:1 XB:2 LN:1,0 E:6 E:7 GB:2 LN:0,3 GB:3 E:8 GB:4 E:9 GB:5 XB:3 LN:1,1 E:10 GB:6 LN:2,0 E:11 GB:7
        E:12 E:13 GB:8 E:14 GB:9 LN:1,2 GB:10 LN:2,1 E:15 GB:11 GB:12 LN:1,3 GB:13 LN:2,2 GB:14 GB:15 GB:16
        GB:17 LN:2,3 GB:18 GB:19
    """,
    "vector": """
        XD:0 LN:3,0 XD:1 LN:3,1 LN:0,0 ADJ:0 HT3:0 LN:0,1 HT:0,0 XD:2 LN:3,2 XD:3 LN:3,3 ADJ:1 KQ:0 HT3:1 S:0
        S:1 E:0 HT3:2 HT:0,1 S:2 E:1 HT3:3 KQ:1 S:3 PT:0 E:2 AG:0 LN:0,2 E:3 AG:1 GA:0 GB:0 ADJ:2 O:0 S:4 PT:1
        HT:0,2 EW:0 O:1 S:5 PT:2 E:4 AG:2 O:2 E:5 S:6 PT:3 GA:1 GB:1 KQ:2 O:3 S:7 X1:0 LN:1,0 PT:4 E:6 EW:1 AG:3
        GA:2 O:4 GB:2 E:7 LN:0,3 S:8 HT:1,0 PT:5 EW:2 AG:4 GA:3 O:5 D1:0 GB:3 S:9 PT:6 E:8 EW:3 AG:5 O:6 HT:0,3
        E1:0 GA:4 GB:4 S:10 PT:7 E:9 EW:4 AG:6 GA:5 O:7 GB:5 KQ:3 S:11 X1:1 LN:1,1 PT:8 E:10 EW:5 O:8 AG:7 ADJ:3
        S:12 GA:6 GB:6 HT:1,1 O1:0 PT:9 LN:2,0 E:11 D1:1 EW:6 AG:8 O:9 GA:7 GB:7 S:13 Z:0 PT:10 E:12 EW:7 AG:9
        O:10 E1:1 E:13 GA:8 GB:8 S:14 PT:11 EW:8 AG:10 O:11 GA:9 GB:9 E:14 Y:0 X1:2 LN:1,2 S:15 PT:12 EW:9 AG:11
        GA:10 O:12 O1:1 GB:10 LN:2,1 PT:13 HT:1,2 E:15 EW:10 O:13 AG:12 D1:2 GA:11 GB:11 E1:2 PT:14 Z:1 EW:11
        O:14 AG:13 GA:12 GB:12 PT:15 EW:12 O:15 AG:14 X1:3 LN:1,3 GA:13 GB:13 Y:1 EW:13 HT:1,3 O1:2 AG:15 GA:14
        LN:2,2 GB:14 D1:3 EW:14 AG:16 Z:2 GA:15 GB:15 E1:3 EW:15 AG:17 GA:16 Y:2 GB:16 EW:16 AG:18 GA:17 GB:17
        O1:3 LN:2,3 EW:17 AG:19 GA:18 GB:18 XT:0 EW:18 Z:3 GA:19 GB:19 XT:1 EW:19 XT:2 Y:3 XT:3
    """,
}
LAST_LAYER = ("XD", "HT3", "T", "AG", "GA", "GB", "EW", "XT")


def steps_of(engine, front, last):
    steps = []
    for word in ORDER[engine].split():
        kind, index = word.split(":")
        step = (kind, *(int(i) for i in index.split(",")))
        if last if kind in LAST_LAYER or step[:2] == ("LN", 3) else front:
            steps.append(step)
    return steps


def adj_gnn_stack_kernel(nc, x, adj, maskT, ident_in, fcwT, fpw, fcb, qkw, qkb, fpb, l1W, l1WT, l1a,
                         eps, l2W1, l2b1, l2W2, l2b2, l3wT, wihT, whhT, bih, bhh, out):
    f32, f16 = mybir.dt.float32, mybir.dt.float16
    ALU, ACT, AX = mybir.AluOpType, mybir.ActivationFunctionType, mybir.AxisListType
    FIRST, LOOP, LAST = ({engine: steps_of(engine, front, last) for engine in ORDER}
                         for front, last in ((True, False), (True, True), (False, True)))

    x_flat, adj_flat, out_flat = (t.rearrange("b n d -> (b n d)") for t in (x, adj, out))

    ctx = ExitStack()
    with ctx:
        def sb(name, shape, dt=f32):
            return ctx.enter_context(nc.sbuf_tensor(name, shape, dt))

        def sem(name):
            return ctx.enter_context(nc.semaphore(name))

        signals = []

        def signal(name, per, unit=1, lag=0):
            s = Signal(sem(name), per, unit, lag)
            signals.append(s)
            return s

        bank = [ctx.enter_context(nc.psum_tensor(f"bank{i}", [128, W4], f32)) for i in range(8)]

        ident = sb("ident", [128, 128])
        ident16 = sb("ident16", [128, 128], f16)
        sel_k = sb("sel_k", [128, HEADS, 128], f16)
        sel_q = sb("sel_q", [128, HEADS, 128], f16)
        G_hi = sb("G_hi", [128, HEADS * D], f16)
        G_lo = sb("G_lo", [128, HEADS * D], f16)
        wkq_hi = sb("wkq_hi", [128, 128], f16)
        wkq_lo = sb("wkq_lo", [128, 128], f16)
        kq_bias = sb("kq_bias", [128, 1])
        l0_bias = sb("l0_bias", [128, 128])
        W_hi = sb("W_hi", [128, 128], f16)
        W_lo = sb("W_lo", [128, 128], f16)
        wsrc_hi = sb("wsrc_hi", [128, 128], f16)
        wsrc_lo = sb("wsrc_lo", [128, 128], f16)
        wdst_hi = sb("wdst_hi", [128, 128], f16)
        wdst_lo = sb("wdst_lo", [128, 128], f16)
        ident_eps = sb("ident_eps", [128, 128])
        W1_hi = sb("W1_hi", [128, HID], f16)
        W1_lo = sb("W1_lo", [128, HID], f16)
        b1_sb = sb("b1_sb", [128, 2])
        W2_sb = sb("W2_sb", [128, 2, D])
        b2_sb = sb("b2_sb", [128, D])
        wih_hi = sb("wih_hi", [128, LAYERS, 3 * D], f16)
        wih_lo = sb("wih_lo", [128, LAYERS, 3 * D], f16)
        whh_hi = sb("whh_hi", [128, 3 * D], f16)
        whh_lo = sb("whh_lo", [128, 3 * D], f16)
        bih_sb = sb("bih_sb", [128, 3])
        bhh_sb = sb("bhh_sb", [128, 3])
        brz_sb = sb("brz_sb", [128, 2])
        bhn_sb = sb("bhn_sb", [128, 1])
        minus_half = sb("minus_half", [128, GB])
        ln_eps = sb("ln_eps", [128, GB])
        minus_one = sb("minus_one", [128, GB])
        half_col = sb("half_col", [128, 1])
        zero_col = sb("zero_col", [128, 1])

        s_w = sem("weights_loaded")
        s_zero = sem("zeroed")
        s_sel = sem("selectors_ready")
        s_pp = sem("prep_products")
        s_pv = sem("prep_vector")
        with ExitStack() as prep:
            def tmp(name, shape, dt=f32):
                return prep.enter_context(nc.sbuf_tensor(name, shape, dt))

            fcwT_sb = tmp("fcwT_sb", [128, HEADS, D])
            fpw_sb = tmp("fpw_sb", [128, HEADS, D])
            fcb_sb = tmp("fcb_sb", [128, HEADS])
            qkw_sb = tmp("qkw_sb", [128, 2])
            qkb_sb = tmp("qkb_sb", [1, 2])
            fpb_sb = tmp("fpb_sb", [1, D])
            fcb_rep = tmp("fcb_rep", [128, HEADS, 128])
            fcb_k = tmp("fcb_k", [128, 128])
            fcb_q = tmp("fcb_q", [128, 128])
            k_ind = tmp("k_ind", [1, 128])
            q_ind = tmp("q_ind", [1, 128])
            ones_row = tmp("ones_row", [1, 128])
            l1W_sb = tmp("l1W_sb", [128, 128])
            l1WT_sb = tmp("l1WT_sb", [128, 128])
            l1a_sb = tmp("l1a_sb", [128, 2])
            eps_sb = tmp("eps_sb", [128, 1])
            W1_sb = tmp("W1_sb", [128, HID])
            wT_sb = tmp("wT_sb", [128, LAYERS, D])
            wihT_sb = tmp("wihT_sb", [128, 3 * D])
            whhT_sb = tmp("whhT_sb", [128, 3 * D])
            wkq = tmp("wkq", [128, 128])
            loads = [(ident, ident_in), (fcwT_sb, fcwT), (fpw_sb, fpw), (fcb_sb, fcb), (qkw_sb, qkw),
                     (qkb_sb, qkb), (fpb_sb, fpb), (l1W_sb, l1W), (l1WT_sb, l1WT), (l1a_sb, l1a),
                     (W1_sb, l2W1), (b1_sb, l2b1), (W2_sb, l2W2), (wT_sb, l3wT), (wihT_sb, wihT),
                     (whhT_sb, whhT), (bih_sb, bih), (bhh_sb, bhh)]
            WL = 16 * (len(loads) + 2)
            P_G0, P_G1, P_WKQ, P_BKQ, P_B0, P_SRC, P_L3 = 1, 2, 3, 4, 5, 6, 7
            src_dst_ps = bank[5]

            with nc.Block() as block:
                @block.sync
                def _(sp):
                    for dst, src in loads:
                        sp.dma_start(dst[...], src).then_inc(s_w, 16)
                    sp.dma_start(eps_sb[:, :], eps.partition_broadcast(128)).then_inc(s_w, 16)
                    sp.dma_start(b2_sb[:, :], l2b2.partition_broadcast(128)).then_inc(s_w, 16)

                @block.gpsimd
                def _(pool):
                    pool.memset(minus_half[:, :], -0.5)
                    pool.memset(ln_eps[:, :], LN_EPS)
                    pool.memset(minus_one[:, :], -1.0)
                    pool.memset(half_col[:, :], 0.5)
                    pool.memset(zero_col[:, :], 0.0)
                    pool.memset(sel_k[:, :, :], 0.0).then_inc(s_zero, 1)
                    pool.memset(sel_q[:, :, :], 0.0).then_inc(s_zero, 1)
                    pool.wait_ge(s_zero, 2)
                    n = 0
                    for rows, tile in ((K_ROWS, sel_k), (Q_ROWS, sel_q)):
                        for part in (0, LO):
                            if n:
                                pool.wait_ge(s_sel, n)
                            pool.affine_select(out=tile[:, :, :], in_=tile[:, :, :], compare_op=ALU.not_equal,
                                               fill=1.0, base=-(rows + part), pattern=[[-1, HEADS], [0, 128]],
                                               channel_multiplier=1).then_inc(s_sel, 1)
                            n += 1

                @block.tensor
                def _(pe):
                    pe.wait_ge(s_w, WL)
                    for half in range(2):
                        for h in range(4):
                            hh = 4 * half + h
                            mm = nc.tensor.matmul(bank[half][:, h * D:(h + 1) * D], fcwT_sb[:, hh, :],
                                                  fpw_sb[:, hh, :], start=True, stop=True)
                        mm.then_inc(s_pp, 1)
                    for h in range(HEADS):
                        mm = nc.tensor.matmul(bank[2][:, 2 * h:2 * h + 2], fcwT_sb[:, h, :], qkw_sb[:, :],
                                              start=True, stop=True)
                    mm.then_inc(s_pp, 1)
                    pe.wait_ge(s_pv, 3)
                    nc.tensor.matmul(bank[3][:, 0:1], fcb_k[:, :], qkw_sb[:, 1:2], start=True, stop=False)
                    nc.tensor.matmul(bank[3][:, 0:1], fcb_q[:, :], qkw_sb[:, 0:1], start=False, stop=False)
                    nc.tensor.matmul(bank[3][:, 0:1], k_ind[:, :], qkb_sb[:, 1:2], start=False, stop=False)
                    nc.tensor.matmul(bank[3][:, 0:1], q_ind[:, :], qkb_sb[:, 0:1], start=False,
                                     stop=True).then_inc(s_pp, 1)
                    for h in range(HEADS):
                        nc.tensor.matmul(bank[4][:, 0:D], fcb_rep[:, h, :], fpw_sb[:, h, :], start=(h == 0), stop=False)
                    nc.tensor.matmul(bank[4][:, 0:D], ones_row[:, :], fpb_sb[:, :], start=False,
                                     stop=True).then_inc(s_pp, 1)
                    nc.tensor.matmul(src_dst_ps[:, 0:2], l1WT_sb[:, :], l1a_sb[:, :], start=True,
                                     stop=True).then_inc(s_pp, 1)
                    for l in range(LAYERS):
                        if l >= 2:
                            pe.wait_ge(s_pv, 100 + 2 * (l - 1))
                        nc.tensor.matmul(bank[6 + l % 2][:, 0:3 * D], wT_sb[:, l, :], wihT_sb[:, :], start=True,
                                         stop=True).then_inc(s_pp, 1)

                @block.vector
                def _(dve):
                    v = nc.vector
                    done = [0]

                    def own(ins):
                        ins.then_inc(s_pv, 1)
                        done[0] += 1
                        return done[0]

                    dve.wait_ge(s_w, WL)
                    own(v.memset(fcb_k[:, :], 0.0))
                    own(v.memset(fcb_q[:, :], 0.0))
                    dve.wait_ge(s_pv, 2)
                    for part in (0, LO):
                        v.tensor_copy(fcb_k[:, K_ROWS + part:K_ROWS + part + HEADS], fcb_sb[:, :])
                        v.tensor_copy(fcb_q[:, Q_ROWS + part:Q_ROWS + part + HEADS], fcb_sb[:, :])
                    for ind, rows in ((k_ind, K_ROWS), (q_ind, Q_ROWS)):
                        v.memset(ind[:, 0:rows], 0.0) if rows else None
                        v.memset(ind[:, rows + HEADS:rows + LO], 0.0)
                        v.memset(ind[:, rows + LO + HEADS:128], 0.0)
                        for part in (0, LO):
                            v.memset(ind[:, rows + part:rows + part + HEADS], 1.0)
                    v.memset(ones_row[:, :], 1.0)
                    own(v.tensor_copy(fcb_rep[:, :, :], fcb_sb[:, :].unsqueeze(2).broadcast_to([128, HEADS, 128])))

                    def split(src, hi, lo):
                        n = own(v.tensor_copy(hi, src))
                        dve.wait_ge(s_pv, n)
                        return own(v.tensor_tensor(lo, src, hi, ALU.subtract))

                    own(v.tensor_copy(ident16[:, :], ident[:, :]))
                    for half in range(2):
                        dve.wait_ge(s_pp, P_G0 + half)
                        c = slice(half * 4 * D, (half + 1) * 4 * D)
                        split(bank[half][:, :], G_hi[:, c], G_lo[:, c])
                    dve.wait_ge(s_pp, P_WKQ)
                    n = own(v.memset(wkq[:, :], 0.0))
                    dve.wait_ge(s_pv, n)
                    qk = bank[2][:, 0:2 * HEADS].rearrange("p (h t) -> p t h", t=2)
                    for part in (0, LO):
                        own(v.tensor_copy(wkq[:, Q_ROWS + part:Q_ROWS + part + HEADS], qk[:, 0, :]))
                        n = own(v.tensor_copy(wkq[:, K_ROWS + part:K_ROWS + part + HEADS], qk[:, 1, :]))
                    dve.wait_ge(s_pv, n)
                    split(wkq[:, :], wkq_hi[:, :], wkq_lo[:, :])
                    dve.wait_ge(s_pp, P_BKQ)
                    own(v.tensor_copy(kq_bias[:, :], bank[3][:, 0:1]))
                    dve.wait_ge(s_pp, P_B0)
                    own(v.tensor_copy(l0_bias[:, :], bank[4][:, 0:D]))
                    dve.wait_ge(s_pp, P_SRC)
                    split(l1W_sb[:, :], W_hi[:, :], W_lo[:, :])
                    split(src_dst_ps[:, 0:1].broadcast_to([128, 128]), wsrc_hi[:, :], wsrc_lo[:, :])
                    split(src_dst_ps[:, 1:2].broadcast_to([128, 128]), wdst_hi[:, :], wdst_lo[:, :])
                    n = own(v.tensor_scalar(eps_sb[:, :], eps_sb[:, :], 1.0, None, ALU.add))
                    dve.wait_ge(s_pv, n)
                    own(v.tensor_scalar(ident_eps[:, :], ident[:, :], eps_sb[:, 0:1], None, ALU.mult))
                    split(W1_sb[:, :], W1_hi[:, :], W1_lo[:, :])
                    split(whhT_sb[:, :], whh_hi[:, :], whh_lo[:, :])
                    n = own(v.tensor_tensor(brz_sb[:, :], bih_sb[:, 0:2], bhh_sb[:, 0:2], ALU.add))
                    dve.wait_ge(s_pv, n)
                    own(v.tensor_scalar(brz_sb[:, :], brz_sb[:, :], 0.5, None, ALU.mult))
                    own(v.tensor_scalar(bhn_sb[:, :], bhh_sb[:, 2:3], 0.5, None, ALU.mult))
                    assert done[0] <= 100
                    v.memset(ones_row[:, :], 1.0).then_inc(s_pv, 100 - done[0])
                    done[0] = 100
                    for l in range(LAYERS):
                        dve.wait_ge(s_pp, P_L3 + l)
                        split(bank[6 + l % 2][:, 0:3 * D], wih_hi[:, l, :], wih_lo[:, l, :])

        x_in = sb("x_in", [128, 2, W4])
        adj_in = sb("adj_in", [128, 2, W4])
        mask_in = sb("mask_in", [128, NB])
        xw = sb("xw", [128, S, W4])
        xd = sb("xd", [128, S, W4])
        l0_mask = sb("l0_mask_t", [128, 2, W4])
        l1_mask = sb("l1_mask_t", [128, S, W4], mybir.dt.bfloat16)
        adj_self = sb("adj_self_t", [128, S, W4])
        edges_next = sb("edges_next", [128, S, W4], f16)
        edges = sb("edges_t", [128, S, W4], f16)
        ln_stats_t = [sb(f"ln_stats_t{f}", [128, 2, GB, 6]) for f in range(2)]
        ln_mom_t = [sb(f"ln_mom_t{f}", [128, 2, GB, 2]) for f in range(2)]
        ln_var_t = [sb(f"ln_var_t{f}", [128, 2, GB]) for f in range(2)]
        ln_rstd_t = [sb(f"ln_rstd_t{f}", [128, 2, GB]) for f in range(2)]
        ln_negmean_t = [sb(f"ln_negmean_t{f}", [128, 2, GB]) for f in range(2)]
        ln_shift_t = [sb(f"ln_shift_t{f}", [128, 2, GB]) for f in range(2)]
        hn = [sb(f"hn{n}", [128, 1 if n in (1, 2) else 2, W4]) for n in range(4)]
        hT_hi_t = [sb(f"hT_hi{n}", [128, 2, W4], f16) for n in range(2)]
        hT_lo_t = [sb(f"hT_lo{n}", [128, 2, W4], f16) for n in range(2)]
        h0b = sb("h0b", [128, 2, W4])
        x_half_t = sb("x_half_t", [128, 2, W4])
        kq = sb("kq", [128, 2, W4], f16)
        RT, RP, RU, RPT = 2, 3, 3, 2
        logit = sb("logit", [128, RT, HEADS * N])
        negmax = sb("negmax", [128, RT, HEADS])
        prob = sb("prob", [128, RP, HEADS * N])
        rowsum = sb("rowsum", [128, RP, HEADS])
        rowinv = sb("rowinv", [128, RP, HEADS])
        probT = sb("probT", [128, RPT, HEADS * N])
        u_t = sb("u_t", [128, RU, HEADS * D])
        e1_t = sb("e1_t", [128, W4])
        negmax1 = sb("negmax1", [128, GB])
        prob1 = sb("prob1", [128, W4])
        rowsum1 = sb("rowsum1", [128, GB])
        rowinv1 = sb("rowinv1", [128, GB])
        prob1T = sb("prob1T", [128, W4])
        v_t = sb("v_t", [128, W4])
        x2b = sb("x2b", [128, W4])
        z_hi_t = sb("z_hi_t", [128, W4], f16)
        z_lo_t = sb("z_lo_t", [128, W4], f16)
        hid_t = sb("hid_t", [128, 2, W4])
        hs = sb("hs", [128, S, W4])
        hs_hi = sb("hs_hi", [128, S, W4], f16)
        hs_lo = sb("hs_lo", [128, S, W4], f16)
        nat = sb("nat", [128, 2, 2 * W4], f16)
        agg_hi_t = sb("agg_hi_t", [128, 2, W4], f16)
        agg_lo_t = sb("agg_lo_t", [128, 2, W4], f16)
        rn_t = sb("rn_t", [128, 2, W4])
        hnb_t = sb("hnb_t", [128, W4])
        z_t = sb("z_t", [128, 2, W4])
        diff_t = sb("diff_t", [128, 2, W4])

        x_loaded = [signal(f"x_loaded{i}", S // 2, 16) for i in range(2)]
        adj_loaded = [signal(f"adj_loaded{i}", S // 2, 16) for i in range(2)]
        mask_loaded = signal("mask_loaded", 1, 16, lag=1)
        out_stored = [signal(f"out_stored{g}", 1, 16, lag=1) for g in range(S)]
        ln_stats, ln_moments, h_normed = ([signal(f"{name}{f}", (3, 1)[f] * S * GB, lag=f) for f in range(2)]
                                          for name in ("ln_stats", "ln_moments", "h_normed"))
        ln_var, ln_rstd, ln_shift = ([signal(f"{name}{f}", (3, 1)[f] * S, lag=f) for f in range(2)]
                                     for name in ("ln_var", "ln_rstd", "ln_shift"))
        hT_ready = signal("hT_ready", 2 * S)
        hT_hi = signal("hT_hi", 2 * S)
        hT_lo = signal("hT_lo", 2 * S)
        kq_ready = signal("kq_ready", S)
        kq_hi = signal("kq_hi", S)
        kq_lo = signal("kq_lo", 2 * S)
        adjT_ready = signal("adjT_ready", S)
        adj_self_ready = signal("adj_self_ready", S)
        l1_mask_ready = signal("l1_mask_ready", S)
        edges_ready = signal("edges_ready", S)
        l0_mask_ready = signal("l0_mask_ready", S)
        h0_biased = signal("h0_biased", S)
        x_half = signal("x_half", S)
        s_ready = signal("s_ready", 2 * NB)
        s_masked = signal("s_masked", 2 * NB)
        s_leaky = signal("s_leaky", 2 * NB)
        s_negmax = signal("s_negmax", 2 * NB)
        exps = signal("exps", HEADS * NB)
        row_inv = signal("row_inv", NB)
        prob_normed = signal("prob_normed", 2 * NB)
        probT_ready = signal("probT_ready", 2 * NB)
        probT_act = signal("probT_act", NB)
        probT_dve = signal("probT_dve", NB)
        u_ready = signal("u_ready", 2 * NB)
        u_kept = signal("u_kept", 2 * NB)
        o_ready = signal("o_ready", NB)
        y_ready = signal("y_ready", NB)
        y_tanh = signal("y_tanh", S)
        x1_ready = signal("x1_ready", S)
        e_ready = signal("e_ready", S)
        e_masked = signal("e_masked", S)
        e_leaky = signal("e_leaky", S)
        e_negmax = signal("e_negmax", S)
        exps1 = signal("exps1", GB * S)
        row_inv1 = signal("row_inv1", S)
        prob1T_ready = signal("prob1T_ready", S)
        prob1T_kept = signal("prob1T_kept", S)
        v_ready = signal("v_ready", S)
        v_kept = signal("v_kept", S)
        o1_ready = signal("o1_ready", S)
        x2_ready = signal("x2_ready", GB * S)
        x2_biased = signal("x2_biased", S)
        z_ready = signal("z_ready", S)
        z_hi = signal("z_hi", S)
        z_lo = signal("z_lo", S)
        hid_ready = signal("hid_ready", 2 * S)
        hid_kept = signal("hid_kept", 2 * S)
        l2_ready = signal("l2_ready", S)
        x3_ready = signal("x3_ready", S)
        xd_ready = signal("xd_ready", S, lag=1)
        edges_moved = signal("edges_moved", S, lag=1)
        h3T_ready = signal("h3T_ready", S, lag=1)
        h_init = signal("h_init", S, lag=1)
        h_hi = signal("h_hi", LAYERS * S, lag=1)
        h_lo = signal("h_lo", LAYERS * S, lag=1)
        h_new = signal("h_new", LAYERS * S, lag=1)
        nat_ready = signal("nat_ready", LAYERS * S, lag=1)
        nat_kept = signal("nat_kept", LAYERS * S, lag=1)
        agg_ready = signal("agg_ready", LAYERS * S, lag=1)
        agg_hi = signal("agg_hi", LAYERS * S, lag=1)
        agg_lo = signal("agg_lo", LAYERS * S, lag=1)
        gates_a_ready = signal("gates_a_ready", 2 * LAYERS * S, lag=1)
        gates_b_ready = signal("gates_b_ready", 2 * LAYERS * S, lag=1)
        r_gate = signal("r_gate", LAYERS * S, lag=1)
        z_gate = signal("z_gate", LAYERS * S, lag=1)
        hn_biased = signal("hn_biased", LAYERS * S, lag=1)
        hn_gated = signal("hn_gated", LAYERS * S, lag=1)
        n_pre = signal("n_pre", LAYERS * S, lag=1)
        n_gate = signal("n_gate", LAYERS * S, lag=1)
        diff = signal("diff", LAYERS * S, lag=1)
        zdiff = signal("zdiff", LAYERS * S, lag=1)
        outT_ready = signal("outT_ready", S, lag=1)
        out_ready = signal("out_ready", GB * S, lag=1)

        LN_AT = {st[1:]: i for i, st in enumerate(st for st in FIRST["vector"] if st[0] == "LN")}
        LN_AT |= {st[1:]: i for i, st in enumerate(st for st in LAST["vector"] if st[0] == "LN")}
        HT_AT = {st[1:]: i for i, st in enumerate(st for st in FIRST["tensor"] if st[0] == "HT")}

        def ht_at(n, g):
            return HT_AT[n, g % S] + g // S * 2 * S

        RELEASES = {
            "HT": lambda n, g: [(hT_lo, HT_AT[n, g])],
            "KQ": lambda g: [(kq_lo, 2 * g + 1)],
            "ADJ": lambda g: [(adj_self_ready, g)],
            "S": lambda b: [(s_masked, 2 * b), (s_masked, 2 * b + 1)],
            "U": lambda b: [(u_kept, 2 * b), (u_kept, 2 * b + 1)],
            "PT": lambda b: [(probT_act, b), (probT_dve, b)],
            "O": lambda b: [(y_ready, b)],
            "D1": lambda g: [(e_masked, g)],
            "V1": lambda g: [(v_kept, g)],
            "PT1": lambda g: [(prob1T_kept, g)],
            "O1": lambda g: [(x2_ready, GB * g + GB - 1)],
            "Z": lambda g: [(z_lo, g)],
            "H": lambda g: [(hid_kept, 2 * g), (hid_kept, 2 * g + 1)],
            "Y": lambda g: [(x3_ready, g)],
            "HT3": lambda g: [(h_init, g)],
            "T": lambda s: [(nat_kept, s)],
            "AG": lambda s: [(agg_lo, s)],
            "GA": lambda s: [(r_gate, s), (hn_biased, s)],
            "GB": lambda s: [(n_pre, s), (z_gate, s)],
            "XT": lambda g: [(out_ready, GB * g + GB - 1)],
        }
        RING_OF = {kind: "singles" for kind in RELEASES}
        RING_OF |= {kind: "pairs" for kind in ("S", "U", "PT", "H")}
        RING_OF |= {kind: "gru" for kind in ("HT3", "T", "AG", "GA", "GB", "XT")}

        class Banks:

            def __init__(self, steps, repeats):
                self.repeats, self.job = repeats, {}
                self.released = {ring: [] for ring in RING_BANKS}
                for st in steps:
                    if st[0] in RELEASES:
                        ring = RING_OF[st[0]]
                        self.job[st] = ring, len(self.released[ring])
                        self.released[ring] += RELEASES[st[0]](*st[1:])

            def of(self, step, part=0):
                ring, n = self.job[step]
                banks = RING_BANKS[ring]
                return bank[banks[(n + part) % len(banks)]]

            def free(self, it, step, part=0):
                return [(sig.sem, sig.at(it, k)) for sig, k in self.release(step, part)]

            def release(self, step, part=0):
                ring, n = self.job[step]
                n, size, released = n + part, len(RING_BANKS[ring]), self.released[ring]
                if n >= size:
                    sig, k = released[n - size]
                elif self.repeats:
                    sig, k = released[max(m for m in range(len(released)) if m % size == n)]
                    k -= sig.per
                else:
                    return []
                return [(sig, k)]

        def cols(b):
            return slice(b * N, (b + 1) * N)

        GROUP = GB * N * D

        def rows(t, start):
            return t[bass.ds(start, GROUP)].rearrange("(b n d) -> n b d", b=GB, n=N)

        def four(ap):
            return ap.rearrange("p (b j) -> p b j", b=GB)

        def load_block(sp, it):
            for g in range(S):
                for sig in (x_half, kq_ready, adj_self_ready, edges_ready, l1_mask_ready, l0_mask_ready):
                    sp.wait_ge(sig.sem, sig.at(it, g - 2))
                start = it * (S * GROUP) + g * GROUP
                sp.dma_start(four(x_in[:, g % 2, :]), rows(x_flat, start)).then_inc(x_loaded[g % 2].sem, 16)
                sp.dma_start(four(adj_in[:, g % 2, :]), rows(adj_flat, start)).then_inc(adj_loaded[g % 2].sem, 16)

        def load_mask(sp, it):
            sp.wait_ge(out_ready.sem, out_ready.at(it, -1))
            sp.dma_start(mask_in[:, :], maskT[:, bass.ds(it * NB - NB, NB)]).then_inc(mask_loaded.sem, 16)

        def tensor_steps(pe, it, steps, banks):
            mm = nc.tensor.matmul

            def split_product(dst, a_hi, a_lo, b_hi, b_lo, start, stop):
                mm(dst, a_hi, b_hi, start=start, stop=False)
                mm(dst, a_hi, b_lo, start=False, stop=False)
                return mm(dst, a_lo, b_hi, start=False, stop=stop)

            for st in steps["tensor"]:
                kind = st[0]
                if kind == "HT":
                    _, n, g = st
                    pe.wait_ge(h_normed[0].sem, h_normed[0].at(it, GB * LN_AT[n, g] + GB - 1))
                    for free in banks.free(it, st):
                        pe.wait_ge(*free)
                    ps = banks.of(st)
                    for b in range(GB):
                        last = nc.tensor.transpose(ps[:, cols(b)], hn[n][:, g % hn[n].shape[1], cols(b)], ident[:, :])
                    last.then_inc(hT_ready.sem, 1)
                elif kind == "KQ":
                    g = st[1]
                    pe.wait_ge(hT_lo.sem, hT_lo.at(it, HT_AT[0, g]))
                    for free in banks.free(it, st):
                        pe.wait_ge(*free)
                    split_product(banks.of(st)[:, :], wkq_hi[:, :], wkq_lo[:, :], hT_hi_t[0][:, g % 2, :],
                                  hT_lo_t[0][:, g % 2, :], True, True).then_inc(kq_ready.sem, 1)
                elif kind == "ADJ":
                    g = st[1]
                    pe.wait_ge(adj_loaded[g % 2].sem, adj_loaded[g % 2].at(it, g // 2))
                    for free in banks.free(it, st):
                        pe.wait_ge(*free)
                    ps = banks.of(st)
                    for b in range(GB):
                        last = nc.tensor.transpose(ps[:, cols(b)], adj_in[:, g % 2, cols(b)], ident[:, :])
                    last.then_inc(adjT_ready.sem, 1)
                elif kind == "S":
                    b = st[1]
                    g, j = divmod(b, GB)
                    pe.wait_ge(kq_lo.sem, kq_lo.at(it, 2 * g + 1))
                    for half in range(2):
                        for free in banks.free(it, st, half):
                            pe.wait_ge(*free)
                        ps = banks.of(st, half)
                        mm(ps[:, :], kq[:, g % 2, cols(j)], sel_q[:, 4 * half:4 * half + 4, :],
                           start=True, stop=False)
                        for h in range(4):
                            last = mm(ps[:, cols(h)], sel_k[:, 4 * half + h, :], kq[:, g % 2, cols(j)],
                                      start=False, stop=(h == 3))
                        last.then_inc(s_ready.sem, 1)
                elif kind == "U":
                    b = st[1]
                    g, j = divmod(b, GB)
                    pe.wait_ge(hT_lo.sem, hT_lo.at(it, HT_AT[0, g]))
                    for half in range(2):
                        for free in banks.free(it, st, half):
                            pe.wait_ge(*free)
                        c = slice(half * 4 * D, (half + 1) * 4 * D)
                        split_product(banks.of(st, half)[:, :], hT_hi_t[0][:, g % 2, cols(j)],
                                      hT_lo_t[0][:, g % 2, cols(j)], G_hi[:, c], G_lo[:, c],
                                      True, True).then_inc(u_ready.sem, 1)
                elif kind == "PT":
                    b = st[1]
                    for half in range(2):
                        pe.wait_ge(prob_normed.sem, prob_normed.at(it, 2 * b + half))
                        for free in banks.free(it, st, half):
                            pe.wait_ge(*free)
                        ps = banks.of(st, half)
                        for h in range(4):
                            last = nc.tensor.transpose(ps[:, cols(h)], prob[:, b % RP, cols(4 * half + h)],
                                                       ident[:, :])
                        last.then_inc(probT_ready.sem, 1)
                elif kind == "O":
                    b = st[1]
                    free = dict(banks.release(st))
                    pe.wait_ge(probT_act.sem, probT_act.at(it, max(b, free.pop(probT_act, b))))
                    pe.wait_ge(probT_dve.sem, probT_dve.at(it, max(b, free.pop(probT_dve, b))))
                    pe.wait_ge(u_kept.sem, u_kept.at(it, max(2 * b + 1, free.pop(u_kept, 0))))
                    for sig, k in free.items():
                        pe.wait_ge(sig.sem, sig.at(it, k))
                    for h in range(HEADS):
                        last = mm(banks.of(st)[:, 0:D], probT[:, b % RPT, cols(h)], u_t[:, b % RU, cols(h)],
                                  start=(h == 0), stop=(h == HEADS - 1))
                    last.then_inc(o_ready.sem, 1)
                elif kind == "D1":
                    g = st[1]
                    pe.wait_ge(hT_lo.sem, hT_lo.at(it, HT_AT[1, g]))
                    for free in banks.free(it, st):
                        pe.wait_ge(*free)
                    ps = banks.of(st)
                    split_product(ps[:, :], wdst_hi[:, :], wdst_lo[:, :], hT_hi_t[1][:, g % 2, :],
                                  hT_lo_t[1][:, g % 2, :], True, False)
                    for b in range(GB):
                        last = split_product(ps[:, cols(b)], hT_hi_t[1][:, g % 2, cols(b)],
                                             hT_lo_t[1][:, g % 2, cols(b)], wsrc_hi[:, :], wsrc_lo[:, :],
                                             False, b == GB - 1)
                    last.then_inc(e_ready.sem, 1)
                elif kind == "V1":
                    g = st[1]
                    pe.wait_ge(hT_lo.sem, hT_lo.at(it, HT_AT[1, g]))
                    for free in banks.free(it, st):
                        pe.wait_ge(*free)
                    for b in range(GB):
                        last = split_product(banks.of(st)[:, cols(b)], hT_hi_t[1][:, g % 2, cols(b)],
                                             hT_lo_t[1][:, g % 2, cols(b)], W_hi[:, :], W_lo[:, :], True, True)
                    last.then_inc(v_ready.sem, 1)
                elif kind == "PT1":
                    g = st[1]
                    pe.wait_ge(exps1.sem, exps1.at(it, GB * g + GB - 1))
                    for free in banks.free(it, st):
                        pe.wait_ge(*free)
                    for b in range(GB):
                        last = nc.tensor.transpose(banks.of(st)[:, cols(b)], prob1[:, cols(b)], ident[:, :])
                    last.then_inc(prob1T_ready.sem, 1)
                elif kind == "O1":
                    g = st[1]
                    pe.wait_ge(v_kept.sem, v_kept.at(it, g))
                    pe.wait_ge(prob1T_kept.sem, prob1T_kept.at(it, g))
                    for free in banks.free(it, st):
                        pe.wait_ge(*free)
                    for b in range(GB):
                        last = mm(banks.of(st)[:, cols(b)], prob1T[:, cols(b)], v_t[:, cols(b)],
                                  start=True, stop=True)
                    last.then_inc(o1_ready.sem, 1)
                elif kind == "Z":
                    g = st[1]
                    pe.wait_ge(h_normed[0].sem, h_normed[0].at(it, GB * LN_AT[2, g] + GB - 1))
                    pe.wait_ge(adj_self_ready.sem, adj_self_ready.at(it, g))
                    for free in banks.free(it, st):
                        pe.wait_ge(*free)
                    for b in range(GB):
                        last = mm(banks.of(st)[:, cols(b)], hn[2][:, 0, cols(b)], adj_self[:, g, cols(b)],
                                  start=True, stop=True)
                    last.then_inc(z_ready.sem, 1)
                elif kind == "H":
                    g = st[1]
                    pe.wait_ge(z_lo.sem, z_lo.at(it, g))
                    for c in range(2):
                        for free in banks.free(it, st, c):
                            pe.wait_ge(*free)
                        split_product(banks.of(st, c)[:, :], W1_hi[:, c * 128:(c + 1) * 128],
                                      W1_lo[:, c * 128:(c + 1) * 128], z_hi_t[:, :], z_lo_t[:, :],
                                      True, True).then_inc(hid_ready.sem, 1)
                elif kind == "Y":
                    g = st[1]
                    pe.wait_ge(hid_kept.sem, hid_kept.at(it, 2 * g + 1))
                    for free in banks.free(it, st):
                        pe.wait_ge(*free)
                    for b in range(GB):
                        for c in range(2):
                            last = mm(banks.of(st)[:, cols(b)], hid_t[:, c, cols(b)], W2_sb[:, c, :],
                                      start=(c == 0), stop=(c == 1))
                    last.then_inc(l2_ready.sem, 1)
                elif kind == "HT3":
                    g = st[1]
                    pe.wait_ge(h_normed[1].sem, h_normed[1].at(it, GB * LN_AT[3, g] + GB - 1))
                    for free in banks.free(it, st):
                        pe.wait_ge(*free)
                    for b in range(GB):
                        last = nc.tensor.transpose(banks.of(st)[:, cols(b)], hn[3][:, g % 2, cols(b)], ident[:, :])
                    last.then_inc(h3T_ready.sem, 1)
                elif kind == "T":
                    s = st[1]
                    g = s % S
                    pe.wait_ge(h_lo.sem, h_lo.at(it, s))
                    for free in banks.free(it, st):
                        pe.wait_ge(*free)
                    ps = banks.of(st)[:, :].bitcast(f16)
                    for part, src in enumerate((hs_hi, hs_lo)):
                        for b in range(GB):
                            last = nc.tensor.transpose(ps[:, part * W4 + b * N:part * W4 + (b + 1) * N],
                                                       src[:, g, cols(b)], ident16[:, :])
                    last.then_inc(nat_ready.sem, 1)
                elif kind == "AG":
                    s = st[1]
                    g = s % S
                    pe.wait_ge(nat_kept.sem, nat_kept.at(it, s))
                    pe.wait_ge(edges_moved.sem, edges_moved.at(it, g))
                    for free in banks.free(it, st):
                        pe.wait_ge(*free)
                    for b in range(GB):
                        for part in range(2):
                            last = mm(banks.of(st)[:, cols(b)],
                                      nat[:, s % 2, part * W4 + b * N:part * W4 + (b + 1) * N],
                                      edges[:, g, cols(b)], start=(part == 0), stop=(part == 1))
                    last.then_inc(agg_ready.sem, 1)
                elif kind in ("GA", "GB"):
                    s = st[1]
                    l, g = divmod(s, S)
                    gates = ((0, True, True), (2, False, True)) if kind == "GA" else \
                        ((2, True, False), (1, True, True))
                    for part, (gate, agg_in, h_in) in enumerate(gates):
                        for free in banks.free(it, st, part):
                            pe.wait_ge(*free)
                        ps = banks.of(st, part)[:, :]
                        c = slice(gate * D, (gate + 1) * D)
                        if h_in:
                            last = split_product(ps, whh_hi[:, c], whh_lo[:, c], hs_hi[:, g, :],
                                                 hs_lo[:, g, :], True, not agg_in)
                        if agg_in:
                            pe.wait_ge(agg_lo.sem, agg_lo.at(it, s))
                            last = split_product(ps, wih_hi[:, l, c], wih_lo[:, l, c], agg_hi_t[:, s % 2, :],
                                                 agg_lo_t[:, s % 2, :], not h_in, True)
                        last.then_inc((gates_a_ready if kind == "GA" else gates_b_ready).sem, 1)
                elif kind == "XT":
                    g = st[1]
                    pe.wait_ge(h_new.sem, h_new.at(it, (LAYERS - 1) * S + g))
                    for free in banks.free(it, st):
                        pe.wait_ge(*free)
                    for b in range(GB):
                        last = nc.tensor.transpose(banks.of(st)[:, cols(b)], hs[:, g, cols(b)], ident[:, :])
                    last.then_inc(outT_ready.sem, 1)

        def scalar_steps(act, it, steps, banks):
            a = nc.scalar
            for st in steps["scalar"]:
                kind = st[0]
                if kind == "LN":
                    _, n, g = st
                    k, f = LN_AT[n, g], n // 3
                    act.wait_ge(ln_shift[f].sem, ln_shift[f].at(it, k))
                    if n == 0:
                        act.wait_ge(h0_biased.sem, h0_biased.at(it, g - 2))
                        act.wait_ge(hT_ready.sem, hT_ready.at(it, ht_at(0, g - 2)))
                    elif n == 1:
                        act.wait_ge(hT_ready.sem, hT_ready.at(it, ht_at(1, g - 1)))
                    elif n == 2:
                        act.wait_ge(z_ready.sem, z_ready.at(it, g - 1))
                    else:
                        act.wait_ge(h3T_ready.sem, h3T_ready.at(it, g - 2))
                    for b in range(GB):
                        src = x_in[:, g % 2, cols(b)] if n == 0 else xw[:, g, cols(b)]
                        a.activation(hn[n][:, g % hn[n].shape[1], cols(b)], src, ACT.Relu,
                                     bias=ln_shift_t[f][:, k % 2, b:b + 1], scale=ln_rstd_t[f][:, k % 2, b:b + 1])\
                            .then_inc(h_normed[f].sem, 1)
                elif kind == "HT":
                    _, n, g = st
                    act.wait_ge(hT_ready.sem, hT_ready.at(it, HT_AT[n, g]))
                    if n == 0:
                        act.wait_ge(kq_ready.sem, kq_ready.at(it, g - 2))
                        act.wait_ge(u_ready.sem, u_ready.at(it, 2 * (GB * (g - 2) + GB - 1) + 1))
                    else:
                        act.wait_ge(e_ready.sem, e_ready.at(it, g - 2))
                        act.wait_ge(v_ready.sem, v_ready.at(it, g - 2))
                    a.activation(hT_hi_t[n][:, g % 2, :], banks.of(st)[:, :], ACT.Copy).then_inc(hT_hi.sem, 1)
                elif kind == "KQ":
                    g = st[1]
                    act.wait_ge(kq_ready.sem, kq_ready.at(it, g))
                    act.wait_ge(s_ready.sem, s_ready.at(it, 2 * (GB * (g - 2) + GB - 1) + 1))
                    a.activation(kq[:, g % 2, :], banks.of(st)[:, :], ACT.Identity, bias=kq_bias[:, 0:1])\
                        .then_inc(kq_hi.sem, 1)
                elif kind == "U":
                    b = st[1]
                    act.wait_ge(o_ready.sem, o_ready.at(it, b - RU))
                    for half in range(2):
                        act.wait_ge(u_ready.sem, u_ready.at(it, 2 * b + half))
                        a.activation(u_t[:, b % RU, half * 4 * D:(half + 1) * 4 * D], banks.of(st, half)[:, :],
                                     ACT.Copy).then_inc(u_kept.sem, 1)
                elif kind == "E":
                    b = st[1]
                    act.wait_ge(s_negmax.sem, s_negmax.at(it, 2 * b + 1))
                    act.wait_ge(probT_ready.sem, probT_ready.at(it, 2 * (b - RP) + 1))
                    for h in range(HEADS):
                        a.activation(prob[:, b % RP, cols(h)], logit[:, b % RT, cols(h)], ACT.Exp,
                                     bias=negmax[:, b % RT, h:h + 1], accum_out=rowsum[:, b % RP, h:h + 1])\
                            .then_inc(exps.sem, 1)
                elif kind == "PT":
                    b = st[1]
                    act.wait_ge(probT_ready.sem, probT_ready.at(it, 2 * b))
                    act.wait_ge(o_ready.sem, o_ready.at(it, b - RPT))
                    a.activation(probT[:, b % RPT, 0:4 * N], banks.of(st)[:, :], ACT.Copy)\
                        .then_inc(probT_act.sem, 1)
                elif kind == "X1":
                    g = st[1]
                    act.wait_ge(y_ready.sem, y_ready.at(it, GB * g + GB - 1))
                    a.activation(h0b[:, g % 2, :], h0b[:, g % 2, :], ACT.Tanh, scale=0.5).then_inc(y_tanh.sem, 1)
                elif kind == "V1":
                    g = st[1]
                    act.wait_ge(v_ready.sem, v_ready.at(it, g))
                    act.wait_ge(o1_ready.sem, o1_ready.at(it, g - 1))
                    a.activation(v_t[:, :], banks.of(st)[:, :], ACT.Copy).then_inc(v_kept.sem, 1)
                elif kind == "E1":
                    g = st[1]
                    act.wait_ge(e_negmax.sem, e_negmax.at(it, g))
                    act.wait_ge(prob1T_ready.sem, prob1T_ready.at(it, g - 1))
                    act.wait_ge(row_inv1.sem, row_inv1.at(it, g - 1))
                    for b in range(GB):
                        a.activation(prob1[:, cols(b)], e1_t[:, cols(b)], ACT.Exp,
                                     bias=negmax1[:, b:b + 1], accum_out=rowsum1[:, b:b + 1])\
                            .then_inc(exps1.sem, 1)
                elif kind == "PT1":
                    g = st[1]
                    act.wait_ge(prob1T_ready.sem, prob1T_ready.at(it, g))
                    act.wait_ge(o1_ready.sem, o1_ready.at(it, g - 1))
                    a.activation(prob1T[:, :], banks.of(st)[:, :], ACT.Copy).then_inc(prob1T_kept.sem, 1)
                elif kind == "Z":
                    g = st[1]
                    act.wait_ge(z_ready.sem, z_ready.at(it, g))
                    act.wait_ge(hid_ready.sem, hid_ready.at(it, 2 * (g - 1) + 1))
                    a.activation(z_hi_t[:, :], banks.of(st)[:, :], ACT.Copy).then_inc(z_hi.sem, 1)
                elif kind == "H":
                    g = st[1]
                    act.wait_ge(l2_ready.sem, l2_ready.at(it, g - 1))
                    for c in range(2):
                        act.wait_ge(hid_ready.sem, hid_ready.at(it, 2 * g + c))
                        a.activation(hid_t[:, c, :], banks.of(st, c)[:, :], ACT.Relu, bias=b1_sb[:, c:c + 1])\
                            .then_inc(hid_kept.sem, 1)
                elif kind == "HT3":
                    g = st[1]
                    act.wait_ge(h3T_ready.sem, h3T_ready.at(it, g))
                    act.wait_ge(outT_ready.sem, outT_ready.at(it, g - S))
                    a.activation(hs[:, g, :], banks.of(st)[:, :], ACT.Copy).then_inc(h_init.sem, 1)
                elif kind == "T":
                    s = st[1]
                    act.wait_ge(nat_ready.sem, nat_ready.at(it, s))
                    act.wait_ge(agg_ready.sem, agg_ready.at(it, s - 2))
                    a.activation(nat[:, s % 2, :], banks.of(st)[:, :].bitcast(f16), ACT.Copy).then_inc(nat_kept.sem, 1)
                elif kind == "AG":
                    s = st[1]
                    act.wait_ge(agg_ready.sem, agg_ready.at(it, s))
                    act.wait_ge(gates_a_ready.sem, gates_a_ready.at(it, 2 * (s - 2) + 1))
                    act.wait_ge(gates_b_ready.sem, gates_b_ready.at(it, 2 * (s - 2) + 1))
                    a.activation(agg_hi_t[:, s % 2, :], banks.of(st)[:, :], ACT.Copy).then_inc(agg_hi.sem, 1)
                elif kind == "GA":
                    s = st[1]
                    act.wait_ge(h_new.sem, h_new.at(it, s - 2))
                    act.wait_ge(gates_a_ready.sem, gates_a_ready.at(it, 2 * s))
                    a.activation(rn_t[:, s % 2, :], banks.of(st, 0)[:, :], ACT.Tanh, bias=brz_sb[:, 0:1], scale=0.5)\
                        .then_inc(r_gate.sem, 1)
                    act.wait_ge(gates_a_ready.sem, gates_a_ready.at(it, 2 * s + 1))
                    act.wait_ge(hn_gated.sem, hn_gated.at(it, s - 1))
                    a.activation(hnb_t[:, :], banks.of(st, 1)[:, :], ACT.Identity, bias=bhn_sb[:, 0:1], scale=0.5)\
                        .then_inc(hn_biased.sem, 1)
                elif kind == "GB":
                    s = st[1]
                    act.wait_ge(n_pre.sem, n_pre.at(it, s))
                    a.activation(rn_t[:, s % 2, :], rn_t[:, s % 2, :], ACT.Tanh, bias=bih_sb[:, 2:3])\
                        .then_inc(n_gate.sem, 1)
                    act.wait_ge(gates_b_ready.sem, gates_b_ready.at(it, 2 * s + 1))
                    act.wait_ge(zdiff.sem, zdiff.at(it, s - 2))
                    a.activation(z_t[:, s % 2, :], banks.of(st, 1)[:, :], ACT.Tanh, bias=brz_sb[:, 1:2], scale=0.5)\
                        .then_inc(z_gate.sem, 1)
                elif kind == "XT":
                    g = st[1]
                    act.wait_ge(out_ready.sem, out_ready.at(it, GB * g + GB - 1))
                    act.dma_start(rows(out_flat, it * (S * GROUP) + (g - S) * GROUP), four(xd[:, g, :]))\
                        .then_inc(out_stored[g].sem, 16)

        def gpsimd_steps(pool, it, steps):
            p = nc.gpsimd
            for st in steps["gpsimd"]:
                kind = st[0]
                if kind == "LN":
                    k, f = LN_AT[st[1:]], st[1] // 3
                    pool.wait_ge(ln_moments[f].sem, ln_moments[f].at(it, GB * k + GB - 1))
                    pool.wait_ge(h_normed[f].sem, h_normed[f].at(it, GB * (k - 2) + GB - 1))
                    p.tensor_tensor(ln_negmean_t[f][:, k % 2, :], ln_mom_t[f][:, k % 2, :, 0], minus_one[:, :], ALU.mult)
                    p.tensor_tensor(ln_var_t[f][:, k % 2, :], ln_mom_t[f][:, k % 2, :, 1], ln_eps[:, :], ALU.add)\
                        .then_inc(ln_var[f].sem, 1)
                    pool.wait_ge(ln_var[f].sem, ln_var[f].at(it, k))
                    p.tensor_tensor(ln_rstd_t[f][:, k % 2, :], ln_var_t[f][:, k % 2, :], minus_half[:, :], ALU.pow)\
                        .then_inc(ln_rstd[f].sem, 1)
                    pool.wait_ge(ln_rstd[f].sem, ln_rstd[f].at(it, k))
                    p.tensor_tensor(ln_shift_t[f][:, k % 2, :], ln_negmean_t[f][:, k % 2, :], ln_rstd_t[f][:, k % 2, :],
                                    ALU.mult).then_inc(ln_shift[f].sem, 1)
                if kind == "XB":
                    g = st[1]
                    pool.wait_ge(x_loaded[g % 2].sem, x_loaded[g % 2].at(it, g // 2))
                    pool.wait_ge(x1_ready.sem, x1_ready.at(it, g - 2))
                    p.tensor_tensor(x_half_t[:, g % 2, :], x_in[:, g % 2, :], half_col[:, :].broadcast_to([128, W4]),
                                    ALU.add).then_inc(x_half.sem, 1)
                    pool.wait_ge(h_normed[0].sem, h_normed[0].at(it, GB * LN_AT[0, g] + GB - 1))
                    pool.wait_ge(y_ready.sem, y_ready.at(it, GB * (g - 2) + GB - 1))
                    p.tensor_tensor(four(h0b[:, g % 2, :]), four(hn[0][:, g % 2, :]),
                                    l0_bias[:, :].unsqueeze(1).broadcast_to([128, GB, D]), ALU.add)\
                        .then_inc(h0_biased.sem, 1)
                elif kind == "E":
                    b = st[1]
                    pool.wait_ge(row_inv.sem, row_inv.at(it, b))
                    for half in range(2):
                        c = slice(half * 4 * N, (half + 1) * 4 * N)
                        p.tensor_tensor(four(prob[:, b % RP, c]), four(prob[:, b % RP, c]),
                                        rowinv[:, b % RP, 4 * half:4 * half + 4].unsqueeze(2)
                                        .broadcast_to([128, 4, N]), ALU.mult).then_inc(prob_normed.sem, 1)
                elif kind == "LN" and st[1] == 2:
                    g = st[2]
                    pool.wait_ge(x2_ready.sem, x2_ready.at(it, GB * g + GB - 1))
                    pool.wait_ge(x3_ready.sem, x3_ready.at(it, g - 1))
                    p.tensor_tensor(four(x2b[:, :]), four(xw[:, g, :]),
                                    b2_sb[:, :].unsqueeze(1).broadcast_to([128, GB, D]), ALU.add)\
                        .then_inc(x2_biased.sem, 1)
                elif kind == "GB":
                    s = st[1]
                    g = s % S
                    pool.wait_ge(n_gate.sem, n_gate.at(it, s))
                    pool.wait_ge(h_new.sem, h_new.at(it, s - 2))
                    p.tensor_tensor(diff_t[:, s % 2, :], hs[:, g, :], rn_t[:, s % 2, :], ALU.subtract)\
                        .then_inc(diff.sem, 1)
                elif kind == "XD":
                    g = st[1]
                    pool.wait_ge(x3_ready.sem, x3_ready.at(it, g - S))
                    pool.wait_ge(out_stored[g].sem, out_stored[g].at(it, -1))
                    p.tensor_tensor(xd[:, g, :], xw[:, g, :], zero_col[:, :].broadcast_to([128, W4]), ALU.add)\
                        .then_inc(xd_ready.sem, 1)

        def vector_steps(dve, it, steps, banks):
            v = nc.vector
            for st in steps["vector"]:
                kind = st[0]
                if kind == "LN":
                    _, n, g = st
                    k, f = LN_AT[n, g], n // 3
                    if n == 0:
                        dve.wait_ge(x_loaded[g % 2].sem, x_loaded[g % 2].at(it, g // 2))
                    elif n == 1:
                        dve.wait_ge(x1_ready.sem, x1_ready.at(it, g))
                    elif n == 2:
                        dve.wait_ge(x2_ready.sem, x2_ready.at(it, GB * g + GB - 1))
                    else:
                        dve.wait_ge(x3_ready.sem, x3_ready.at(it, g - S))
                    dve.wait_ge(ln_shift[f].sem, ln_shift[f].at(it, k - 2))
                    for b in range(GB):
                        src = x_in[:, g % 2, cols(b)] if n == 0 else xw[:, g, cols(b)]
                        v.bn_stats(ln_stats_t[f][:, k % 2, b, :], src).then_inc(ln_stats[f].sem, 1)
                    dve.drain()
                    for b in range(GB):
                        v.bn_aggr(ln_mom_t[f][:, k % 2, b, :], ln_stats_t[f][:, k % 2, b, :]).then_inc(ln_moments[f].sem, 1)
                elif kind == "HT":
                    _, n, g = st
                    dve.wait_ge(hT_hi.sem, hT_hi.at(it, HT_AT[n, g]))
                    v.tensor_tensor(hT_lo_t[n][:, g % 2, :], banks.of(st)[:, :], hT_hi_t[n][:, g % 2, :],
                                    ALU.subtract).then_inc(hT_lo.sem, 1)
                elif kind == "KQ":
                    g = st[1]
                    dve.wait_ge(kq_hi.sem, kq_hi.at(it, g))
                    for rows in (K_ROWS, Q_ROWS):
                        r = slice(rows + LO, rows + 2 * LO)
                        v.scalar_tensor_tensor(kq[r, g % 2, :], banks.of(st)[r, :], kq_bias[r, 0:1],
                                               kq[r, g % 2, :], ALU.add, ALU.subtract).then_inc(kq_lo.sem, 1)
                elif kind == "ADJ":
                    g = st[1]
                    dve.wait_ge(adj_loaded[g % 2].sem, adj_loaded[g % 2].at(it, g // 2))
                    dve.wait_ge(s_masked.sem, s_masked.at(it, 2 * (GB * (g - 2) + GB - 1) + 1))
                    v.tensor_scalar(l0_mask[:, g % 2, :], adj_in[:, g % 2, :], 1.0, 1e9, ALU.subtract, ALU.mult)\
                        .then_inc(l0_mask_ready.sem, 1)
                    dve.wait_ge(adjT_ready.sem, adjT_ready.at(it, g))
                    dve.wait_ge(z_ready.sem, z_ready.at(it, g - S))
                    v.tensor_tensor(four(adj_self[:, g, :]), four(banks.of(st)[:, :]),
                                    ident_eps[:, :].unsqueeze(1).broadcast_to([128, GB, N]), ALU.add)\
                        .then_inc(adj_self_ready.sem, 1)
                    dve.wait_ge(e_masked.sem, e_masked.at(it, g - S))
                    v.tensor_scalar(l1_mask[:, g, :], adj_in[:, g % 2, :], 0.0, -9e15, ALU.is_le, ALU.mult)\
                        .then_inc(l1_mask_ready.sem, 1)
                    dve.wait_ge(edges_moved.sem, edges_moved.at(it, g))
                    v.tensor_scalar(edges_next[:, g, :], adj_in[:, g % 2, :], 0.0, None, ALU.not_equal)\
                        .then_inc(edges_ready.sem, 1)
                elif kind == "S":
                    b = st[1]
                    g, j = divmod(b, GB)
                    dve.wait_ge(l0_mask_ready.sem, l0_mask_ready.at(it, g))
                    dve.wait_ge(exps.sem, exps.at(it, HEADS * (b - RT) + HEADS - 1))
                    halves = [logit[:, b % RT, half * 4 * N:(half + 1) * 4 * N] for half in range(2)]
                    for half, t in enumerate(halves):
                        dve.wait_ge(s_ready.sem, s_ready.at(it, 2 * b + half))
                        v.tensor_tensor(four(t), four(banks.of(st, half)[:, :]),
                                        l0_mask[:, g % 2, cols(j)].unsqueeze(1).broadcast_to([128, 4, N]), ALU.add)\
                            .then_inc(s_masked.sem, 1)
                    for half, t in enumerate(halves):
                        dve.wait_ge(s_masked.sem, s_masked.at(it, 2 * b + half))
                        v.scalar_tensor_tensor(t, t, 0.01, t, ALU.mult, ALU.max).then_inc(s_leaky.sem, 1)
                    for half, t in enumerate(halves):
                        dve.wait_ge(s_leaky.sem, s_leaky.at(it, 2 * b + half))
                        v.tensor_reduce(negmax[:, b % RT, 4 * half:4 * half + 4], four(t), AX.X, ALU.max,
                                        negate=True).then_inc(s_negmax.sem, 1)
                elif kind == "E":
                    b = st[1]
                    dve.wait_ge(exps.sem, exps.at(it, HEADS * b + HEADS - 1))
                    dve.wait_ge(prob_normed.sem, prob_normed.at(it, 2 * (b - RP) + 1))
                    v.reciprocal(rowinv[:, b % RP, :], rowsum[:, b % RP, :]).then_inc(row_inv.sem, 1)
                elif kind == "PT":
                    b = st[1]
                    dve.wait_ge(probT_ready.sem, probT_ready.at(it, 2 * b + 1))
                    dve.wait_ge(o_ready.sem, o_ready.at(it, b - RPT))
                    v.tensor_copy(probT[:, b % RPT, 4 * N:8 * N], banks.of(st, 1)[:, :]).then_inc(probT_dve.sem, 1)
                elif kind == "O":
                    b = st[1]
                    g, j = divmod(b, GB)
                    dve.wait_ge(o_ready.sem, o_ready.at(it, b))
                    dve.wait_ge(h0_biased.sem, h0_biased.at(it, g))
                    v.tensor_tensor(h0b[:, g % 2, cols(j)], banks.of(st)[:, 0:D], h0b[:, g % 2, cols(j)], ALU.add)\
                        .then_inc(y_ready.sem, 1)
                elif kind == "X1":
                    g = st[1]
                    dve.wait_ge(y_tanh.sem, y_tanh.at(it, g))
                    dve.wait_ge(x_half.sem, x_half.at(it, g))
                    dve.wait_ge(xd_ready.sem, xd_ready.at(it, g))
                    dve.wait_ge(h_normed[1].sem, h_normed[1].at(it, GB * LN_AT[3, g] + GB - 1))
                    v.scalar_tensor_tensor(xw[:, g, :], h0b[:, g % 2, :], 0.5, x_half_t[:, g % 2, :],
                                           ALU.mult, ALU.add).then_inc(x1_ready.sem, 1)
                elif kind == "D1":
                    g = st[1]
                    t = e1_t[:, :]
                    dve.wait_ge(e_ready.sem, e_ready.at(it, g))
                    dve.wait_ge(exps1.sem, exps1.at(it, GB * (g - 1) + GB - 1))
                    dve.wait_ge(l1_mask_ready.sem, l1_mask_ready.at(it, g))
                    v.tensor_tensor(t, banks.of(st)[:, :], l1_mask[:, g, :], ALU.add).then_inc(e_masked.sem, 1)
                    dve.wait_ge(e_masked.sem, e_masked.at(it, g))
                    v.scalar_tensor_tensor(t, t, 0.2, t, ALU.mult, ALU.max).then_inc(e_leaky.sem, 1)
                    dve.wait_ge(e_leaky.sem, e_leaky.at(it, g))
                    v.tensor_reduce(negmax1[:, :], four(t), AX.X, ALU.max, negate=True)\
                        .then_inc(e_negmax.sem, 1)
                elif kind == "E1":
                    g = st[1]
                    dve.wait_ge(exps1.sem, exps1.at(it, GB * g + GB - 1))
                    dve.wait_ge(x2_ready.sem, x2_ready.at(it, GB * (g - 1) + GB - 1))
                    v.reciprocal(rowinv1[:, :], rowsum1[:, :]).then_inc(row_inv1.sem, 1)
                elif kind == "O1":
                    g = st[1]
                    dve.wait_ge(o1_ready.sem, o1_ready.at(it, g))
                    dve.wait_ge(row_inv1.sem, row_inv1.at(it, g))
                    for b in range(GB):
                        v.scalar_tensor_tensor(xw[:, g, cols(b)], banks.of(st)[:, cols(b)],
                                               rowinv1[:, b:b + 1], xw[:, g, cols(b)],
                                               ALU.mult, ALU.add).then_inc(x2_ready.sem, 1)
                elif kind == "Z":
                    g = st[1]
                    dve.wait_ge(z_hi.sem, z_hi.at(it, g))
                    v.tensor_tensor(z_lo_t[:, :], banks.of(st)[:, :], z_hi_t[:, :], ALU.subtract)\
                        .then_inc(z_lo.sem, 1)
                elif kind == "Y":
                    g = st[1]
                    dve.wait_ge(l2_ready.sem, l2_ready.at(it, g))
                    dve.wait_ge(x2_biased.sem, x2_biased.at(it, g))
                    v.tensor_tensor(xw[:, g, :], banks.of(st)[:, :], x2b[:, :], ALU.add)\
                        .then_inc(x3_ready.sem, 1)
                elif kind == "HT3":
                    g = st[1]
                    dve.wait_ge(h_init.sem, h_init.at(it, g))
                    dve.wait_ge(gates_b_ready.sem, gates_b_ready.at(it, 2 * (g - S) + 1))
                    v.tensor_copy(hs_hi[:, g, :], hs[:, g, :]).then_inc(h_hi.sem, 1)
                    dve.wait_ge(h_hi.sem, h_hi.at(it, g))
                    v.tensor_tensor(hs_lo[:, g, :], hs[:, g, :], hs_hi[:, g, :], ALU.subtract)\
                        .then_inc(h_lo.sem, 1)
                elif kind == "AG":
                    s = st[1]
                    dve.wait_ge(agg_hi.sem, agg_hi.at(it, s))
                    v.tensor_tensor(agg_lo_t[:, s % 2, :], banks.of(st)[:, :], agg_hi_t[:, s % 2, :],
                                    ALU.subtract).then_inc(agg_lo.sem, 1)
                elif kind == "XD":
                    g = st[1]
                    dve.wait_ge(edges_ready.sem, edges_ready.at(it, g - S))
                    dve.wait_ge(agg_ready.sem, agg_ready.at(it, g - S))
                    v.tensor_copy(edges[:, g, :], edges_next[:, g, :]).then_inc(edges_moved.sem, 1)
                elif kind == "GA":
                    s = st[1]
                    u = rn_t[:, s % 2, :]
                    dve.wait_ge(r_gate.sem, r_gate.at(it, s))
                    dve.wait_ge(hn_biased.sem, hn_biased.at(it, s))
                    v.scalar_tensor_tensor(u, u, 1.0, hnb_t[:, :], ALU.add, ALU.mult).then_inc(hn_gated.sem, 1)
                elif kind == "GB":
                    s = st[1]
                    u = rn_t[:, s % 2, :]
                    dve.wait_ge(gates_b_ready.sem, gates_b_ready.at(it, 2 * s))
                    dve.wait_ge(hn_gated.sem, hn_gated.at(it, s))
                    v.tensor_tensor(u, banks.of(st, 0)[:, :], u, ALU.add).then_inc(n_pre.sem, 1)
                elif kind == "EW":
                    s = st[1]
                    g = s % S
                    t = diff_t[:, s % 2, :]
                    dve.wait_ge(diff.sem, diff.at(it, s))
                    dve.wait_ge(z_gate.sem, z_gate.at(it, s))
                    v.scalar_tensor_tensor(t, z_t[:, s % 2, :], 1.0, t, ALU.add, ALU.mult).then_inc(zdiff.sem, 1)
                    dve.wait_ge(zdiff.sem, zdiff.at(it, s))
                    v.scalar_tensor_tensor(hs[:, g, :], t, 0.5, rn_t[:, s % 2, :], ALU.mult, ALU.add)\
                        .then_inc(h_new.sem, 1)
                    if s < (LAYERS - 1) * S:
                        dve.wait_ge(h_new.sem, h_new.at(it, s))
                        dve.wait_ge(gates_b_ready.sem, gates_b_ready.at(it, 2 * s + 1))
                        v.tensor_copy(hs_hi[:, g, :], hs[:, g, :]).then_inc(h_hi.sem, 1)
                        dve.wait_ge(h_hi.sem, h_hi.at(it, s + S))
                        v.tensor_tensor(hs_lo[:, g, :], hs[:, g, :], hs_hi[:, g, :], ALU.subtract)\
                            .then_inc(h_lo.sem, 1)
                elif kind == "XT":
                    g = st[1]
                    dve.wait_ge(outT_ready.sem, outT_ready.at(it, g))
                    dve.wait_ge(mask_loaded.sem, mask_loaded.at(it, 0))
                    dve.wait_ge(xd_ready.sem, xd_ready.at(it, g))
                    for b in range(GB):
                        v.scalar_tensor_tensor(xd[:, g, cols(b)], banks.of(st)[:, cols(b)],
                                               mask_in[:, g * GB + b:g * GB + b + 1], xd[:, g, cols(b)],
                                               ALU.mult, ALU.add).then_inc(out_ready.sem, 1)

        with nc.Block() as block:
            banks = Banks(FIRST["tensor"], False)

            @block.sync
            def _(sp):
                for s in signals:
                    sp.sem_inc(s.sem, s.per * s.unit)
                load_block(sp, 0)

            @block.tensor
            def _(pe):
                pe.wait_ge(out_stored[S - 1].sem, 16)
                tensor_steps(pe, 0, FIRST, banks)

            @block.scalar
            def _(act):
                act.wait_ge(out_stored[S - 1].sem, 16)
                scalar_steps(act, 0, FIRST, banks)

            @block.gpsimd
            def _(pool):
                pool.wait_ge(out_stored[S - 1].sem, 16)
                gpsimd_steps(pool, 0, FIRST)

            @block.vector
            def _(dve):
                dve.wait_ge(out_stored[S - 1].sem, 16)
                vector_steps(dve, 0, FIRST, banks)

        with nc.Block() as block:
            banks = Banks(LOOP["tensor"], True)

            @block.sync
            def _(sp):
                with sp.Fori(1, ITERS) as it:
                    load_mask(sp, it)
                    load_block(sp, it)

            @block.tensor
            def _(pe):
                with pe.Fori(1, ITERS) as it:
                    tensor_steps(pe, it, LOOP, banks)

            @block.scalar
            def _(act):
                with act.Fori(1, ITERS) as it:
                    scalar_steps(act, it, LOOP, banks)

            @block.gpsimd
            def _(pool):
                with pool.Fori(1, ITERS) as it:
                    gpsimd_steps(pool, it, LOOP)

            @block.vector
            def _(dve):
                with dve.Fori(1, ITERS) as it:
                    vector_steps(dve, it, LOOP, banks)

        with nc.Block() as block:
            banks = Banks(LAST["tensor"], False)

            @block.sync
            def _(sp):
                load_mask(sp, ITERS)
                for g in range(S):
                    sp.wait_ge(out_stored[g].sem, out_stored[g].at(ITERS, 0))

            @block.tensor
            def _(pe):
                tensor_steps(pe, ITERS, LAST, banks)

            @block.scalar
            def _(act):
                scalar_steps(act, ITERS, LAST, banks)

            @block.gpsimd
            def _(pool):
                gpsimd_steps(pool, ITERS, LAST)

            @block.vector
            def _(dve):
                vector_steps(dve, ITERS, LAST, banks)


def kernel(**inputs):
    import numpy as np
    import concourse.bacc as bacc
    from concourse.bass_utils import run_bass_kernel_spmd

    a = {k: np.asarray(v) for k, v in inputs.items()}
    arrays = {
        "x": a["x"],
        "adj": a["adj"],
        "maskT": a["nodemask"].T,
        "ident": np.eye(128, dtype=np.float32),
        "fcwT": a["L0_gnn_fc_w"].reshape(D, HEADS, D).transpose(2, 1, 0),
        "fpw": a["L0_gnn_fp_w"].reshape(HEADS, D, D).transpose(1, 0, 2),
        "fcb": a["L0_gnn_fc_b"].reshape(HEADS, D).T,
        "qkw": np.concatenate([a["L0_gnn_q_w"], a["L0_gnn_k_w"]], axis=1),
        "qkb": np.concatenate([a["L0_gnn_q_b"], a["L0_gnn_k_b"]]).reshape(1, 2),
        "fpb": a["L0_gnn_fp_b"].reshape(1, D),
        "l1W": a["L1_gnn_W"],
        "l1WT": a["L1_gnn_W"].T,
        "l1a": a["L1_gnn_a"].reshape(2, D).T,
        "eps": a["L2_gnn_eps"],
        "l2W1": a["L2_gnn_W1"],
        "l2b1": a["L2_gnn_b1"].reshape(2, 128).T,
        "l2W2": a["L2_gnn_W2"].reshape(2, 128, D).transpose(1, 0, 2),
        "l2b2": a["L2_gnn_b2"],
        "l3wT": a["L3_gnn_weight"].transpose(2, 0, 1),
        "wihT": a["L3_gnn_w_ih"].T,
        "whhT": a["L3_gnn_w_hh"].T,
        "bih": a["L3_gnn_b_ih"].reshape(3, 128).T,
        "bhh": a["L3_gnn_b_hh"].reshape(3, 128).T,
    }
    nc = bacc.Bacc("TRN2", target_bir_lowering=False, num_devices=1)
    data, args = {}, []
    for name, value in arrays.items():
        value = np.ascontiguousarray(value)
        data[f"in_{name}"] = value
        args.append(nc.dram_tensor(f"in_{name}", value.shape, mybir.dt.from_np(value.dtype), kind="ExternalInput").ap())
    args.append(nc.dram_tensor("out_0", (B, N, D), mybir.dt.float32, kind="ExternalOutput").ap())
    adj_gnn_stack_kernel(nc, *args)
    r = run_bass_kernel_spmd(nc, [data], core_ids=[0])
    return r.results[0]["out_0"]
```

```python
import concourse.bass as bass
from concourse import mybir
from contextlib import ExitStack

B, N, D = 128, 128, 128
HEADS = 8
HID = 256
LAYERS = 5
GB = 4
W4 = GB * N
S = 4
NB = S * GB
ITERS = B // NB
RING_BANKS = {
    "first": {"pairs": (0, 1, 2, 3, 4), "singles": (5, 6, 7), "gru": ()},
    "loop": {"pairs": (0, 1, 2, 3), "singles": (4,), "gru": (5, 6, 7)},
    "last": {"pairs": (0, 1), "singles": (2,), "gru": (3, 4, 5, 6, 7)},
}
LN_EPS = 1e-5
K_ROWS, Q_ROWS, LO = 0, 64, 32


class Signal:

    def __init__(self, sem, per, unit=1, lag=0):
        self.sem, self.per, self.unit, self.lag = sem, per, unit, lag

    def at(self, it, k):
        return it * (self.per * self.unit) + (self.per * (1 - self.lag) + k + 1) * self.unit


ORDER = {
    "first": {
        "tensor": """
            ADJ:0 HT:0,0 KQ:0 U:0 S:0 S:1 U:1 HT:0,1 S:2 U:2 ADJ:1 S:3 KQ:1 PT:0 O:0 U:3 PT:1 S:4 U:4 O:1 PT:2 S:5
            U:5 O:2 PT:3 S:6 U:6 HT:0,2 O:3 PT:4 ADJ:2 S:7 KQ:2 U:7 O:4 PT:5 U:8 S:8 O:5 HT:1,0 PT:6 S:9 U:9 D1:0
            O:6 PT:7 HT:0,3 S:10 U:10 V1:0 O:7 PT1:0 PT:8 S:11 KQ:3 U:11 O:8 ADJ:3 PT:9 O1:0 S:12 U:12 O:9 HT:1,1
            PT:10 D1:1 S:13 U:13 O:10 PT:11 S:14 V1:1 U:14 Z:0 O:11 PT:12 PT1:1 S:15 U:15 H:0 O:12 O1:1 PT:13 Y:0
            O:13 HT:1,2 PT:14 D1:2 O:14 PT:15 V1:2 O:15 Z:1 PT1:2 O1:2 H:1 HT:1,3 Y:1 D1:3 Z:2 H:2 Y:2
        """,
        "scalar": """
            LA:0,0 HT:0,0 KQ:0 U:0 LA:0,1 U:1 HT:0,1 E:0 U:2 E:1 PT:0 KQ:1 E:2 U:3 PT:1 E:3 U:4 PT:2 E:4 PT:3 U:5
            LA:0,2 E:5 HT:0,2 PT:4 U:6 X1:0 KQ:2 E:6 PT:5 U:7 E:7 U:8 HT:1,0 PT:6 E:8 LA:0,3 PT:7 U:9 HT:0,3 E:9
            E1:0 U:10 PT:8 V1:0 PT1:0 X1:1 KQ:3 E:10 U:11 PT:9 E:11 U:12 HT:1,1 PT:10 LA:2,0 E:12 U:13 PT:11 E1:1
            V1:1 E:13 U:14 PT:12 Z:0 PT1:1 X1:2 E:14 H:0 U:15 PT:13 E:15 HT:1,2 PT:14 LA:2,1 PT:15 E1:2 V1:2 X1:3
            Z:1 PT1:2 H:1 HT:1,3 LA:2,2 Z:2 H:2
        """,
        "gpsimd": """
            LN:0,0 XB:0 LN:0,1 XB:1 E:0 E:1 E:2 E:3 LN:0,2 E:4 E:5 XB:2 LN:1,0 E:6 LN:0,3 E:7 E:8 E:9 XB:3 LN:1,1
            E:10 LN:2,0 E:11 E:12 E:13 LN:1,2 E:14 LN:2,1 E:15 LN:1,3 LN:2,2
        """,
        "vector": """
            LN:0,0 ADJ:0 LN:0,1 HT:0,0 KQ:0 S:0 S:1 E:0 HT:0,1 S:2 E:1 PT:0 KQ:1 S:3 E:2 PT:1 O:0 ADJ:1 S:4 PT:2 E:3
            LN:0,2 O:1 S:5 PT:3 E:4 O:2 S:6 HT:0,2 E:5 PT:4 O:3 S:7 KQ:2 X1:0 LN:1,0 E:6 PT:5 O:4 ADJ:2 LA:1,0 S:8
            HT:1,0 LN:0,3 E:7 PT:6 O:5 S:9 D1:0 E:8 PT:7 O:6 HT:0,3 S:10 E1:0 E:9 PT:8 O:7 S:11 KQ:3 X1:1 LN:1,1
            E:10 PT:9 O:8 ADJ:3 LA:1,1 O1:0 LN:2,0 HT:1,1 S:12 E:11 PT:10 O:9 D1:1 S:13 E:12 PT:11 O:10 E1:1 S:14
            E:13 PT:12 O:11 Z:0 S:15 X1:2 LN:1,2 PT:13 E:14 O:12 LA:1,2 O1:1 LN:2,1 Y:0 HT:1,2 E:15 O:13 PT:14 D1:2
            O:14 PT:15 E1:2 O:15 X1:3 LN:1,3 Z:1 O1:2 LA:1,3 LN:2,2 HT:1,3 Y:1 D1:3 Z:2 Y:2
        """,
    },
    "loop": {
        "tensor": """
            V1:-1 PT1:-1 O1:-1 ADJ:0 HT3:0 Z:-1 H:-1 HT:0,0 HT3:1 Y:-1 KQ:0 U:0 HT3:2 S:0 T:0 U:1 HT:0,1 T:1 S:1
            HT3:3 AG:0 S:2 U:2 KQ:1 S:3 PT:0 T:2 AG:1 T:3 ADJ:1 S:4 U:3 GA:0 GB:0 O:0 PT:1 GA:1 U:4 GB:1 AG:2 O:1
            S:5 GA:2 PT:2 GB:2 U:5 T:4 AG:3 O:2 S:6 S:7 HT:0,2 PT:3 GA:3 T:5 GB:3 O:3 U:6 AG:4 PT:4 GA:4 KQ:2 U:7
            GB:4 T:6 O:4 ADJ:2 AG:5 S:8 HT:1,0 GA:5 GB:5 T:7 PT:5 U:8 AG:6 S:9 O:5 GA:6 T:8 PT:6 AG:7 D1:0 GB:6 V1:0
            U:9 GA:7 O:6 GB:7 HT:0,3 T:9 AG:8 S:10 T:10 AG:9 PT:7 KQ:3 U:10 GA:8 S:11 GB:8 O:7 GA:9 PT:8 PT1:0 U:11
            O1:0 T:11 GB:9 O:8 AG:10 S:12 T:12 ADJ:3 PT:9 HT:1,1 GA:10 AG:11 GB:10 U:12 O:9 S:13 GA:11 GB:11 D1:1
            T:13 AG:12 V1:1 PT:10 Z:0 S:14 U:13 GA:12 O:10 T:14 GB:12 PT:11 AG:13 U:14 GA:13 O:11 GB:13 T:15 PT1:1
            AG:14 S:15 H:0 O1:1 GA:14 Y:0 PT:12 U:15 GB:14 T:16 O:12 AG:15 PT:13 T:17 HT:1,2 GA:15 D1:2 PT:14 O:13
            GB:15 AG:16 Z:1 T:18 GA:16 GB:16 V1:2 AG:17 PT:15 O:14 GA:17 GB:17 AG:18 T:19 O:15 H:1 PT1:2 GA:18 O1:2
            GB:18 Y:1 XT:0 AG:19 XT:1 HT:1,3 GA:19 D1:3 GB:19 Z:2 XT:2 H:2 XT:3 Y:2
        """,
        "scalar": """
            E1:-1 V1:-1 PT1:-1 HT3:0 LA:2,-1 Z:-1 LA:0,0 H:-1 HT:0,0 HT3:1 KQ:0 U:0 HT3:2 LA:0,1 U:1 T:0 T:1 E:0
            AG:0 HT:0,1 HT3:3 U:2 E:1 KQ:1 PT:0 AG:1 T:2 T:3 E:2 GA:0 E:3 GB:0 U:3 PT:1 GA:1 E:4 AG:2 GB:1 U:4
            LA:0,2 GA:2 PT:2 E:5 T:4 AG:3 U:5 GB:2 HT:0,2 PT:3 GA:3 T:5 E:6 GB:3 AG:4 U:6 X1:0 PT:4 GA:4 KQ:2 E:7
            T:6 GB:4 AG:5 HT:1,0 U:7 GA:5 T:7 PT:5 GB:5 AG:6 E:8 U:8 GA:6 T:8 PT:6 LA:0,3 AG:7 GB:6 V1:0 E1:0 GA:7
            U:9 GB:7 HT:0,3 T:9 AG:8 E:9 T:10 PT:7 AG:9 KQ:3 GA:8 E:10 GB:8 U:10 X1:1 PT:8 PT1:0 GA:9 E:11 T:11 GB:9
            AG:10 U:11 PT:9 T:12 HT:1,1 GA:10 LA:2,0 AG:11 E:12 U:12 GB:10 GA:11 GB:11 AG:12 V1:1 T:13 PT:10 E1:1
            Z:0 E:13 GA:12 U:13 T:14 GB:12 AG:13 PT:11 E:14 GA:13 X1:2 U:14 PT1:1 T:15 AG:14 GB:13 H:0 PT:12 GA:14
            E:15 GB:14 T:16 AG:15 U:15 HT:1,2 T:17 PT:13 LA:2,1 GA:15 E1:2 GB:15 AG:16 T:18 Z:1 GA:16 V1:2 PT:14
            AG:17 GB:16 GA:17 PT:15 AG:18 GB:17 X1:3 T:19 PT1:2 GA:18 H:1 GB:18 AG:19 XT:0 HT:1,3 GA:19 LA:2,2 XT:1
            GB:19 Z:2 H:2 XT:2 XT:3
        """,
        "gpsimd": """
            XD:0 LN:3,0 XD:1 LN:2,-1 LN:0,0 LN:3,1 HT3:0 XD:2 HT3:1 LN:3,2 LN:0,1 XB:0 LN:3,3 XB:1 XD:3 HT3:2 E:0
            HT3:3 E:1 E:2 GB:0 EW:0 LN:0,2 E:3 LO:0 GB:1 EW:1 E:4 LO:1 GB:2 EW:2 LO:2 E:5 GB:3 EW:3 LO:3 LN:1,0 E:6
            GB:4 EW:4 E:7 LO:4 GB:5 EW:5 LN:0,3 LO:5 GB:6 EW:6 E:8 GB:7 LO:6 XB:2 EW:7 LO:7 E:9 GB:8 EW:8 LO:8
            LN:1,1 GB:9 E:10 LN:2,0 EW:9 LO:9 XB:3 GB:10 EW:10 GB:11 EW:11 E:11 E:12 LO:10 E:13 LO:11 GB:12 EW:12
            LN:1,2 LO:12 GB:13 EW:13 E:14 LO:13 GB:14 LN:2,1 EW:14 E:15 LO:14 GB:15 EW:15 LO:15 GB:16 EW:16 GB:17
            EW:17 LN:1,3 GB:18 EW:18 LN:2,2 GB:19 EW:19
        """,
        "vector": """
            XD:0 LN:3,0 LA:3,0 E1:-1 O1:-1 LN:2,-1 LN:0,0 LN:3,1 ADJ:0 Z:-1 XD:1 HT3:0 LN:3,2 LA:3,1 HT:0,0 HT3:1
            Y:-1 LN:0,1 LA:3,2 KQ:0 LN:3,3 S:0 LA:3,3 XD:2 S:1 XD:3 HT3:2 HT:0,1 E:0 S:2 HT3:3 E:1 KQ:1 AG:0 PT:0
            S:3 AG:1 ADJ:1 GA:0 E:2 GB:0 S:4 LN:0,2 E:3 O:0 PT:1 EW:0 GA:1 GB:1 AG:2 O:1 S:5 EW:1 GA:2 PT:2 E:4 GB:2
            O:2 AG:3 S:6 HT:0,2 PT:3 EW:2 E:5 GA:3 GB:3 S:7 AG:4 O:3 E:6 PT:4 X1:0 EW:3 GA:4 LN:1,0 KQ:2 LA:1,0 E:7
            GB:4 O:4 ADJ:2 AG:5 S:8 GA:5 EW:4 GB:5 PT:5 HT:1,0 LN:0,3 AG:6 S:9 O:5 EW:5 GA:6 D1:0 E:8 GB:6 AG:7 PT:6
            E1:0 GA:7 GB:7 O:6 EW:6 HT:0,3 S:10 AG:8 PT:7 EW:7 E:9 AG:9 KQ:3 GA:8 GB:8 S:11 O:7 X1:1 LN:1,1 EW:8
            O1:0 PT:8 GA:9 GB:9 LN:2,0 LA:1,1 E:10 O:8 AG:10 ADJ:3 S:12 HT:1,1 PT:9 AG:11 EW:9 GA:10 GB:10 E:11 O:9
            S:13 GA:11 GB:11 D1:1 AG:12 PT:10 E:12 EW:10 EW:11 E1:1 Z:0 S:14 O:10 E:13 GA:12 GB:12 AG:13 PT:11 O:11
            EW:12 E:14 GA:13 GB:13 X1:2 LN:1,2 AG:14 O1:1 S:15 Y:0 EW:13 PT:12 LA:1,2 GA:14 GB:14 E:15 LN:2,1 O:12
            AG:15 PT:13 HT:1,2 D1:2 EW:14 GA:15 GB:15 O:13 AG:16 E1:2 PT:14 Z:1 GA:16 EW:15 GB:16 AG:17 O:14 GA:17
            GB:17 PT:15 EW:16 AG:18 O:15 X1:3 LN:1,3 EW:17 GA:18 O1:2 GB:18 LN:2,2 LA:1,3 Y:1 XT:0 AG:19 HT:1,3 XT:1
            EW:18 GA:19 GB:19 D1:3 Z:2 XT:2 EW:19 XT:3 Y:2
        """,
    },
    "last": {
        "tensor": """
            V1:-1 PT1:-1 O1:-1 HT3:0 HT3:1 Z:-1 T:0 H:-1 HT3:2 Y:-1 T:1 AG:0 T:2 AG:1 GA:0 HT3:3 GB:0 T:3 AG:2 GA:1
            GB:1 AG:3 GA:2 GB:2 T:4 GA:3 GB:3 AG:4 T:5 GA:4 AG:5 GB:4 T:6 GA:5 AG:6 GB:5 T:7 GA:6 GB:6 AG:7 T:8 GA:7
            AG:8 GB:7 T:9 GA:8 GB:8 AG:9 T:10 GA:9 AG:10 GB:9 T:11 GA:10 GB:10 AG:11 T:12 GA:11 AG:12 GB:11 T:13
            GA:12 GB:12 AG:13 T:14 GA:13 AG:14 GB:13 T:15 GA:14 GB:14 AG:15 T:16 GA:15 AG:16 GB:15 T:17 GA:16 GB:16
            AG:17 T:18 GA:17 AG:18 GB:17 T:19 GA:18 GB:18 AG:19 GA:19 GB:19 XT:0 XT:1 XT:2 XT:3
        """,
        "scalar": """
            E1:-1 V1:-1 PT1:-1 HT3:0 LA:2,-1 HT3:1 Z:-1 T:0 H:-1 HT3:2 T:1 AG:0 T:2 AG:1 HT3:3 GA:0 T:3 GB:0 AG:2
            GA:1 AG:3 GB:1 GA:2 T:4 GB:2 GA:3 AG:4 T:5 GB:3 GA:4 AG:5 T:6 GB:4 AG:6 GA:5 T:7 GB:5 GA:6 AG:7 T:8 GB:6
            GA:7 AG:8 T:9 GB:7 GA:8 AG:9 T:10 GB:8 GA:9 AG:10 T:11 GB:9 GA:10 AG:11 T:12 GB:10 GA:11 AG:12 T:13
            GB:11 GA:12 AG:13 T:14 GB:12 GA:13 AG:14 T:15 GB:13 GA:14 AG:15 T:16 GB:14 GA:15 AG:16 T:17 GB:15 GA:16
            AG:17 T:18 GB:16 GA:17 AG:18 T:19 GB:17 GA:18 AG:19 GB:18 GA:19 GB:19 XT:0 XT:1 XT:2 XT:3
        """,
        "gpsimd": """
            XD:0 LN:3,0 XD:1 LN:3,1 LN:2,-1 HT3:0 LN:3,2 HT3:1 XD:2 HT3:2 XD:3 LN:3,3 HT3:3 GB:0 EW:0 GB:1 LO:0 EW:1
            GB:2 LO:1 EW:2 GB:3 LO:2 EW:3 GB:4 LO:3 EW:4 GB:5 LO:4 EW:5 GB:6 LO:5 EW:6 GB:7 LO:6 EW:7 GB:8 LO:7 EW:8
            GB:9 LO:8 EW:9 GB:10 LO:9 EW:10 GB:11 LO:10 EW:11 GB:12 LO:11 EW:12 GB:13 LO:12 EW:13 GB:14 LO:13 EW:14
            GB:15 LO:14 EW:15 GB:16 LO:15 EW:16 GB:17 EW:17 GB:18 EW:18 GB:19 EW:19
        """,
        "vector": """
            LN:3,0 E1:-1 XD:0 LN:3,1 LA:3,0 O1:-1 LN:2,-1 HT3:0 LA:3,1 XD:1 LN:3,2 XD:2 XD:3 HT3:1 Z:-1 LA:3,2 HT3:2
            Y:-1 LN:3,3 AG:0 LA:3,3 AG:1 HT3:3 GA:0 GB:0 AG:2 GA:1 GB:1 AG:3 EW:0 GA:2 GB:2 EW:1 GA:3 GB:3 AG:4 EW:2
            GA:4 AG:5 GB:4 EW:3 AG:6 GA:5 GB:5 EW:4 GA:6 GB:6 AG:7 EW:5 GA:7 AG:8 GB:7 EW:6 GA:8 GB:8 AG:9 EW:7 GA:9
            AG:10 GB:9 EW:8 GA:10 GB:10 AG:11 EW:9 GA:11 AG:12 GB:11 EW:10 GA:12 GB:12 AG:13 EW:11 GA:13 AG:14 GB:13
            EW:12 GA:14 GB:14 AG:15 EW:13 AG:16 GA:15 GB:15 EW:14 GA:16 GB:16 AG:17 EW:15 GA:17 AG:18 GB:17 EW:16
            GA:18 GB:18 AG:19 EW:17 GA:19 GB:19 EW:18 XT:0 XT:1 XT:2 EW:19 XT:3
        """,
    },
}


def steps_of(words):
    return [(kind, *(int(i) for i in index.split(","))) for kind, index in (word.split(":") for word in words.split())]


def adj_gnn_stack_kernel(nc, x, adj, maskT, ident_in, fcwT, fpw, fcb, qkw, qkb, fpb, l1W, l1WT, l1a,
                         eps, l2W1, l2b1, l2W2, l2b2, l3wT, wihT, whhT, bih, bhh, out):
    f32, f16 = mybir.dt.float32, mybir.dt.float16
    ALU, ACT, AX = mybir.AluOpType, mybir.ActivationFunctionType, mybir.AxisListType
    FIRST, LOOP, LAST = ({engine: steps_of(words) for engine, words in ORDER[phase].items()}
                         for phase in ("first", "loop", "last"))

    x_flat, adj_flat, out_flat = (t.rearrange("b n d -> (b n d)") for t in (x, adj, out))

    ctx = ExitStack()
    with ctx:
        def sb(name, shape, dt=f32):
            return ctx.enter_context(nc.sbuf_tensor(name, shape, dt))

        def sem(name):
            return ctx.enter_context(nc.semaphore(name))

        signals = []

        def signal(name, per, unit=1, lag=0):
            s = Signal(sem(name), per, unit, lag)
            signals.append(s)
            return s

        bank = [ctx.enter_context(nc.psum_tensor(f"bank{i}", [128, W4], f32)) for i in range(8)]

        ident = sb("ident", [128, 128])
        ident16 = sb("ident16", [128, 128], f16)
        sel_k = sb("sel_k", [128, HEADS, 128], f16)
        sel_q = sb("sel_q", [128, HEADS, 128], f16)
        G_hi = sb("G_hi", [128, HEADS * D], f16)
        G_lo = sb("G_lo", [128, HEADS * D], f16)
        wkq_hi = sb("wkq_hi", [128, 128], f16)
        wkq_lo = sb("wkq_lo", [128, 128], f16)
        kq_bias = sb("kq_bias", [128, 1])
        l0_bias = sb("l0_bias", [128, 128])
        W_hi = sb("W_hi", [128, 128], f16)
        W_lo = sb("W_lo", [128, 128], f16)
        wsrc_hi = sb("wsrc_hi", [128, 128], f16)
        wsrc_lo = sb("wsrc_lo", [128, 128], f16)
        wdst_hi = sb("wdst_hi", [128, 128], f16)
        wdst_lo = sb("wdst_lo", [128, 128], f16)
        ident_eps = sb("ident_eps", [128, 128])
        W1_hi = sb("W1_hi", [128, HID], f16)
        W1_lo = sb("W1_lo", [128, HID], f16)
        b1_sb = sb("b1_sb", [128, 2])
        W2_sb = sb("W2_sb", [128, 2, D])
        b2_sb = sb("b2_sb", [128, D])
        wih_hi = sb("wih_hi", [128, LAYERS, 3 * D], f16)
        wih_lo = sb("wih_lo", [128, LAYERS, 3 * D], f16)
        whh_hi = sb("whh_hi", [128, 3 * D], f16)
        whh_lo = sb("whh_lo", [128, 3 * D], f16)
        bih_sb = sb("bih_sb", [128, 3])
        bhh_sb = sb("bhh_sb", [128, 3])
        brz_sb = sb("brz_sb", [128, 2])
        bhn_sb = sb("bhn_sb", [128, 1])
        minus_half = sb("minus_half", [128, GB])
        ln_eps = sb("ln_eps", [128, GB])
        minus_one = sb("minus_one", [128, GB])
        half_col = sb("half_col", [128, 1])
        zero_col = sb("zero_col", [128, 1])

        x_in = sb("x_in", [128, 2, W4])
        adj_in = sb("adj_in", [128, 2, W4])

        x_loaded = [signal(f"x_loaded{i}", S // 2, 16) for i in range(2)]
        adj_loaded = [signal(f"adj_loaded{i}", S // 2, 16) for i in range(2)]
        mask_loaded = signal("mask_loaded", 1, 16, lag=1)
        out_stored = [signal(f"out_stored{g}", 1, 16, lag=1) for g in range(S)]
        ln_stats, ln_moments, h_normed = ([signal(f"{name}{n}", S * GB, lag=n // 3) for n in range(4)]
                                          for name in ("ln_stats", "ln_moments", "h_normed"))
        ln_var, ln_rstd, ln_shift = ([signal(f"{name}{n}", S, lag=n // 3) for n in range(4)]
                                     for name in ("ln_var", "ln_rstd", "ln_shift"))
        hT_ready, hT_hi, hT_lo = ([signal(f"{name}{n}", S) for n in range(2)] for name in ("hT_ready", "hT_hi", "hT_lo"))
        kq_ready = signal("kq_ready", S)
        kq_hi = signal("kq_hi", S)
        kq_lo = signal("kq_lo", 2 * S)
        adjT_ready = signal("adjT_ready", S)
        adj_self_ready = signal("adj_self_ready", S)
        l1_mask_ready = signal("l1_mask_ready", S)
        edges_ready = signal("edges_ready", S)
        l0_mask_ready = signal("l0_mask_ready", S)
        h0_biased = signal("h0_biased", S)
        x_half = signal("x_half", S)
        s_ready = signal("s_ready", 2 * NB)
        s_masked = signal("s_masked", 2 * NB)
        s_leaky = signal("s_leaky", 2 * NB)
        s_negmax = signal("s_negmax", 2 * NB)
        exps = signal("exps", HEADS * NB)
        row_inv = signal("row_inv", NB)
        prob_normed = signal("prob_normed", 2 * NB)
        probT_ready = signal("probT_ready", 2 * NB)
        probT_act = signal("probT_act", NB)
        probT_dve = signal("probT_dve", NB)
        u_ready = signal("u_ready", 2 * NB)
        u_kept = signal("u_kept", 2 * NB)
        o_ready = signal("o_ready", NB)
        y_ready = signal("y_ready", NB)
        y_tanh = signal("y_tanh", S)
        x1_ready = signal("x1_ready", S)
        e_ready = signal("e_ready", S)
        e_masked = signal("e_masked", S)
        e_leaky = signal("e_leaky", S)
        e_negmax = signal("e_negmax", S)
        exps1 = signal("exps1", GB * S)
        row_inv1 = signal("row_inv1", S)
        prob1T_ready = signal("prob1T_ready", S)
        prob1T_kept = signal("prob1T_kept", S)
        v_ready = signal("v_ready", S)
        v_kept = signal("v_kept", S)
        o1_ready = signal("o1_ready", S)
        x2_ready = signal("x2_ready", GB * S)
        x2_biased = signal("x2_biased", S)
        z_ready = signal("z_ready", S)
        z_hi = signal("z_hi", S)
        z_lo = signal("z_lo", S)
        hid_ready = signal("hid_ready", 2 * S)
        hid_kept = signal("hid_kept", 2 * S)
        l2_ready = signal("l2_ready", S)
        x3_ready = signal("x3_ready", S)
        xd_ready = signal("xd_ready", S, lag=1)
        edges_moved = signal("edges_moved", S, lag=1)
        h3T_ready = signal("h3T_ready", S, lag=1)
        h_init = signal("h_init", S, lag=1)
        h_init_hi = signal("h_init_hi", S, lag=1)
        h_init_lo = signal("h_init_lo", S, lag=1)
        h_hi = signal("h_hi", (LAYERS - 1) * S, lag=1)
        h_lo = signal("h_lo", (LAYERS - 1) * S, lag=1)
        h_new = signal("h_new", LAYERS * S, lag=1)
        nat_ready = signal("nat_ready", LAYERS * S, lag=1)
        nat_kept = signal("nat_kept", LAYERS * S, lag=1)
        agg_ready = signal("agg_ready", LAYERS * S, lag=1)
        agg_hi = signal("agg_hi", LAYERS * S, lag=1)
        agg_lo = signal("agg_lo", LAYERS * S, lag=1)
        gates_a_ready = signal("gates_a_ready", 2 * LAYERS * S, lag=1)
        gates_b_ready = signal("gates_b_ready", 2 * LAYERS * S, lag=1)
        r_gate = signal("r_gate", LAYERS * S, lag=1)
        z_gate = signal("z_gate", LAYERS * S, lag=1)
        hn_biased = signal("hn_biased", LAYERS * S, lag=1)
        hn_gated = signal("hn_gated", LAYERS * S, lag=1)
        n_pre = signal("n_pre", LAYERS * S, lag=1)
        n_gate = signal("n_gate", LAYERS * S, lag=1)
        diff = signal("diff", LAYERS * S, lag=1)
        z_scaled = signal("z_scaled", LAYERS * S, lag=1)
        zdiff = signal("zdiff", LAYERS * S, lag=1)
        outT_ready = signal("outT_ready", S, lag=1)
        out_ready = signal("out_ready", GB * S, lag=1)

        def cols(b):
            return slice(b * N, (b + 1) * N)

        GROUP = GB * N * D

        def rows(t, start):
            return t[bass.ds(start, GROUP)].rearrange("(b n d) -> n b d", b=GB, n=N)

        def four(ap):
            return ap.rearrange("p (b j) -> p b j", b=GB)

        def load_group(sp, it, g):
            for sig in (x_half, kq_ready, adj_self_ready, edges_ready, l1_mask_ready, l0_mask_ready):
                sp.wait_ge(sig.sem, sig.at(it, g - 2))
            start = it * (S * GROUP) + g * GROUP
            sp.dma_start(four(x_in[:, g % 2, :]), rows(x_flat, start)).then_inc(x_loaded[g % 2].sem, 16)
            sp.dma_start(four(adj_in[:, g % 2, :]), rows(adj_flat, start)).then_inc(adj_loaded[g % 2].sem, 16)

        s_w = sem("first_weights_loaded")
        s_w2 = sem("other_weights_loaded")
        s_zero = sem("zeroed")
        s_sel = sem("selectors_ready")
        s_pp = sem("prep_products")
        s_pv = sem("prep_vector")
        with ExitStack() as prep:
            def tmp(name, shape, dt=f32):
                return prep.enter_context(nc.sbuf_tensor(name, shape, dt))

            fcwT_sb = tmp("fcwT_sb", [128, HEADS, D])
            fpw_sb = tmp("fpw_sb", [128, HEADS, D])
            fcb_sb = tmp("fcb_sb", [128, HEADS])
            qkw_sb = tmp("qkw_sb", [128, 2])
            qkb_sb = tmp("qkb_sb", [1, 2])
            fpb_sb = tmp("fpb_sb", [1, D])
            fcb_rep = tmp("fcb_rep", [128, HEADS, 128])
            fcb_k = tmp("fcb_k", [128, 128])
            fcb_q = tmp("fcb_q", [128, 128])
            k_ind = tmp("k_ind", [1, 128])
            q_ind = tmp("q_ind", [1, 128])
            ones_row = tmp("ones_row", [1, 128])
            l1W_sb = tmp("l1W_sb", [128, 128])
            l1WT_sb = tmp("l1WT_sb", [128, 128])
            l1a_sb = tmp("l1a_sb", [128, 2])
            eps_sb = tmp("eps_sb", [128, 1])
            W1_sb = tmp("W1_sb", [128, HID])
            wT_sb = tmp("wT_sb", [128, LAYERS, D])
            wihT_sb = tmp("wihT_sb", [128, 3 * D])
            whhT_sb = tmp("whhT_sb", [128, 3 * D])
            wkq = tmp("wkq", [128, 128])
            loads = [(ident, ident_in), (fcwT_sb, fcwT), (fpw_sb, fpw), (fcb_sb, fcb), (qkw_sb, qkw),
                     (qkb_sb, qkb), (fpb_sb, fpb), (l1W_sb, l1W), (l1WT_sb, l1WT), (l1a_sb, l1a),
                     (W1_sb, l2W1), (b1_sb, l2b1), (W2_sb, l2W2), (wT_sb, l3wT), (wihT_sb, wihT),
                     (whhT_sb, whhT), (bih_sb, bih), (bhh_sb, bhh)]
            FIRST_LOADS = 7
            WL = 16 * FIRST_LOADS
            WL2 = 16 * (len(loads) - FIRST_LOADS + 2)
            P_G0, P_G1, P_WKQ, P_BKQ, P_B0, P_SRC, P_L3 = 1, 2, 3, 4, 5, 6, 7
            src_dst_ps = bank[5]

            with nc.Block() as block:
                @block.sync
                def _(sp):
                    for dst, src in loads[:FIRST_LOADS]:
                        sp.dma_start(dst[...], src).then_inc(s_w, 16)
                    for sig in signals:
                        sp.sem_inc(sig.sem, sig.per * sig.unit)
                    for g in range(2):
                        load_group(sp, 0, g)

                @block.scalar
                def _(act):
                    for dst, src in loads[FIRST_LOADS:]:
                        act.dma_start(dst[...], src).then_inc(s_w2, 16)
                    act.dma_start(eps_sb[:, :], eps.partition_broadcast(128)).then_inc(s_w2, 16)
                    act.dma_start(b2_sb[:, :], l2b2.partition_broadcast(128)).then_inc(s_w2, 16)
                    act.wait_ge(s_w2, WL2)

                @block.gpsimd
                def _(pool):
                    pool.memset(minus_half[:, :], -0.5)
                    pool.memset(ln_eps[:, :], LN_EPS)
                    pool.memset(minus_one[:, :], -1.0)
                    pool.memset(half_col[:, :], 0.5)
                    pool.memset(zero_col[:, :], 0.0)
                    pool.memset(sel_k[:, :, :], 0.0).then_inc(s_zero, 1)
                    pool.memset(sel_q[:, :, :], 0.0).then_inc(s_zero, 1)
                    pool.wait_ge(s_zero, 2)
                    n = 0
                    for rows, tile in ((K_ROWS, sel_k), (Q_ROWS, sel_q)):
                        for part in (0, LO):
                            if n:
                                pool.wait_ge(s_sel, n)
                            pool.affine_select(out=tile[:, :, :], in_=tile[:, :, :], compare_op=ALU.not_equal,
                                               fill=1.0, base=-(rows + part), pattern=[[-1, HEADS], [0, 128]],
                                               channel_multiplier=1).then_inc(s_sel, 1)
                            n += 1

                @block.tensor
                def _(pe):
                    pe.wait_ge(s_w, WL)
                    for half in range(2):
                        for h in range(4):
                            hh = 4 * half + h
                            mm = nc.tensor.matmul(bank[half][:, h * D:(h + 1) * D], fcwT_sb[:, hh, :],
                                                  fpw_sb[:, hh, :], start=True, stop=True)
                        mm.then_inc(s_pp, 1)
                    for h in range(HEADS):
                        mm = nc.tensor.matmul(bank[2][:, 2 * h:2 * h + 2], fcwT_sb[:, h, :], qkw_sb[:, :],
                                              start=True, stop=True)
                    mm.then_inc(s_pp, 1)
                    pe.wait_ge(s_pv, 3)
                    nc.tensor.matmul(bank[3][:, 0:1], fcb_k[:, :], qkw_sb[:, 1:2], start=True, stop=False)
                    nc.tensor.matmul(bank[3][:, 0:1], fcb_q[:, :], qkw_sb[:, 0:1], start=False, stop=False)
                    nc.tensor.matmul(bank[3][:, 0:1], k_ind[:, :], qkb_sb[:, 1:2], start=False, stop=False)
                    nc.tensor.matmul(bank[3][:, 0:1], q_ind[:, :], qkb_sb[:, 0:1], start=False,
                                     stop=True).then_inc(s_pp, 1)
                    for h in range(HEADS):
                        nc.tensor.matmul(bank[4][:, 0:D], fcb_rep[:, h, :], fpw_sb[:, h, :], start=(h == 0), stop=False)
                    nc.tensor.matmul(bank[4][:, 0:D], ones_row[:, :], fpb_sb[:, :], start=False,
                                     stop=True).then_inc(s_pp, 1)
                    pe.wait_ge(s_w2, WL2)
                    nc.tensor.matmul(src_dst_ps[:, 0:2], l1WT_sb[:, :], l1a_sb[:, :], start=True,
                                     stop=True).then_inc(s_pp, 1)
                    for l in range(LAYERS):
                        if l >= 2:
                            pe.wait_ge(s_pv, 100 + 2 * (l - 1))
                        nc.tensor.matmul(bank[6 + l % 2][:, 0:3 * D], wT_sb[:, l, :], wihT_sb[:, :], start=True,
                                         stop=True).then_inc(s_pp, 1)

                @block.vector
                def _(dve):
                    v = nc.vector
                    done = [0]

                    def own(ins):
                        ins.then_inc(s_pv, 1)
                        done[0] += 1
                        return done[0]

                    dve.wait_ge(s_w, WL)
                    own(v.memset(fcb_k[:, :], 0.0))
                    own(v.memset(fcb_q[:, :], 0.0))
                    dve.wait_ge(s_pv, 2)
                    for part in (0, LO):
                        v.tensor_copy(fcb_k[:, K_ROWS + part:K_ROWS + part + HEADS], fcb_sb[:, :])
                        v.tensor_copy(fcb_q[:, Q_ROWS + part:Q_ROWS + part + HEADS], fcb_sb[:, :])
                    for ind, rows in ((k_ind, K_ROWS), (q_ind, Q_ROWS)):
                        v.memset(ind[:, 0:rows], 0.0) if rows else None
                        v.memset(ind[:, rows + HEADS:rows + LO], 0.0)
                        v.memset(ind[:, rows + LO + HEADS:128], 0.0)
                        for part in (0, LO):
                            v.memset(ind[:, rows + part:rows + part + HEADS], 1.0)
                    v.memset(ones_row[:, :], 1.0)
                    own(v.tensor_copy(fcb_rep[:, :, :], fcb_sb[:, :].unsqueeze(2).broadcast_to([128, HEADS, 128])))

                    def split(src, hi, lo):
                        n = own(v.tensor_copy(hi, src))
                        dve.wait_ge(s_pv, n)
                        return own(v.tensor_tensor(lo, src, hi, ALU.subtract))

                    own(v.tensor_copy(ident16[:, :], ident[:, :]))
                    for half in range(2):
                        dve.wait_ge(s_pp, P_G0 + half)
                        c = slice(half * 4 * D, (half + 1) * 4 * D)
                        split(bank[half][:, :], G_hi[:, c], G_lo[:, c])
                    dve.wait_ge(s_pp, P_WKQ)
                    n = own(v.memset(wkq[:, :], 0.0))
                    dve.wait_ge(s_pv, n)
                    qk = bank[2][:, 0:2 * HEADS].rearrange("p (h t) -> p t h", t=2)
                    for part in (0, LO):
                        own(v.tensor_copy(wkq[:, Q_ROWS + part:Q_ROWS + part + HEADS], qk[:, 0, :]))
                        n = own(v.tensor_copy(wkq[:, K_ROWS + part:K_ROWS + part + HEADS], qk[:, 1, :]))
                    dve.wait_ge(s_pv, n)
                    split(wkq[:, :], wkq_hi[:, :], wkq_lo[:, :])
                    dve.wait_ge(s_pp, P_BKQ)
                    own(v.tensor_copy(kq_bias[:, :], bank[3][:, 0:1]))
                    dve.wait_ge(s_pp, P_B0)
                    own(v.tensor_copy(l0_bias[:, :], bank[4][:, 0:D]))
                    dve.wait_ge(s_pp, P_SRC)
                    dve.wait_ge(s_w2, WL2)
                    split(l1W_sb[:, :], W_hi[:, :], W_lo[:, :])
                    split(src_dst_ps[:, 0:1].broadcast_to([128, 128]), wsrc_hi[:, :], wsrc_lo[:, :])
                    split(src_dst_ps[:, 1:2].broadcast_to([128, 128]), wdst_hi[:, :], wdst_lo[:, :])
                    n = own(v.tensor_scalar(eps_sb[:, :], eps_sb[:, :], 1.0, None, ALU.add))
                    dve.wait_ge(s_pv, n)
                    own(v.tensor_scalar(ident_eps[:, :], ident[:, :], eps_sb[:, 0:1], None, ALU.mult))
                    split(W1_sb[:, :], W1_hi[:, :], W1_lo[:, :])
                    split(whhT_sb[:, :], whh_hi[:, :], whh_lo[:, :])
                    n = own(v.tensor_tensor(brz_sb[:, :], bih_sb[:, 0:2], bhh_sb[:, 0:2], ALU.add))
                    dve.wait_ge(s_pv, n)
                    own(v.tensor_scalar(brz_sb[:, :], brz_sb[:, :], 0.5, None, ALU.mult))
                    own(v.tensor_scalar(bhn_sb[:, :], bhh_sb[:, 2:3], 0.5, None, ALU.mult))
                    assert done[0] <= 100
                    v.memset(ones_row[:, :], 1.0).then_inc(s_pv, 100 - done[0])
                    done[0] = 100
                    for l in range(LAYERS):
                        dve.wait_ge(s_pp, P_L3 + l)
                        split(bank[6 + l % 2][:, 0:3 * D], wih_hi[:, l, :], wih_lo[:, l, :])

        mask_in = sb("mask_in", [128, NB])
        xw = sb("xw", [128, S, W4])
        xd = sb("xd", [128, S, W4])
        l0_mask = sb("l0_mask_t", [128, 2, W4])
        l1_mask = sb("l1_mask_t", [128, S, W4], mybir.dt.bfloat16)
        adj_self = sb("adj_self_t", [128, S, W4])
        edges_next = sb("edges_next", [128, S, W4], f16)
        edges = sb("edges_t", [128, S, W4], f16)
        ln_stats_t = [sb(f"ln_stats_t{n}", [128, 2, GB, 6]) for n in range(4)]
        ln_mom_t = [sb(f"ln_mom_t{n}", [128, 2, GB, 2]) for n in range(4)]
        ln_var_t = [sb(f"ln_var_t{n}", [128, 2, GB]) for n in range(4)]
        ln_rstd_t = [sb(f"ln_rstd_t{n}", [128, 2, GB]) for n in range(4)]
        ln_negmean_t = [sb(f"ln_negmean_t{n}", [128, 2, GB]) for n in range(4)]
        ln_shift_t = [sb(f"ln_shift_t{n}", [128, 2, GB]) for n in range(4)]
        hn = [sb(f"hn{n}", [128, 1 if n in (1, 2) else 2, W4]) for n in range(4)]
        hT_hi_t = [sb(f"hT_hi{n}", [128, 2, W4], f16) for n in range(2)]
        hT_lo_t = [sb(f"hT_lo{n}", [128, 2, W4], f16) for n in range(2)]
        h0b = sb("h0b", [128, 2, W4])
        x_half_t = sb("x_half_t", [128, 2, W4])
        kq = sb("kq", [128, 2, W4], f16)
        RT, RP, RU, RPT = 2, 3, 3, 2
        logit = sb("logit", [128, RT, HEADS * N])
        negmax = sb("negmax", [128, RT, HEADS])
        prob = sb("prob", [128, RP, HEADS * N])
        rowsum = sb("rowsum", [128, RP, HEADS])
        rowinv = sb("rowinv", [128, RP, HEADS])
        probT = sb("probT", [128, RPT, HEADS * N])
        u_t = sb("u_t", [128, RU, HEADS * D])
        e1_t = sb("e1_t", [128, W4])
        negmax1 = sb("negmax1", [128, GB])
        prob1 = sb("prob1", [128, W4])
        rowsum1 = sb("rowsum1", [128, GB])
        rowinv1 = sb("rowinv1", [128, GB])
        prob1T = sb("prob1T", [128, W4])
        v_t = sb("v_t", [128, W4])
        x2b = sb("x2b", [128, W4])
        z_hi_t = sb("z_hi_t", [128, W4], f16)
        z_lo_t = sb("z_lo_t", [128, W4], f16)
        hid_t = sb("hid_t", [128, 2, W4])
        hs = sb("hs", [128, S, W4])
        hs_hi = sb("hs_hi", [128, S, W4], f16)
        hs_lo = sb("hs_lo", [128, S, W4], f16)
        nat = sb("nat", [128, 2, 2 * W4], f16)
        agg_hi_t = sb("agg_hi_t", [128, 2, W4], f16)
        agg_lo_t = sb("agg_lo_t", [128, 2, W4], f16)
        rn_t = sb("rn_t", [128, 2, W4])
        hnb_t = sb("hnb_t", [128, W4])
        z_t = sb("z_t", [128, 2, W4])
        diff_t = sb("diff_t", [128, 2, W4])

        RELEASES = {
            "HT": lambda n, g: [(hT_lo[n], g)],
            "KQ": lambda g: [(kq_lo, 2 * g + 1)],
            "ADJ": lambda g: [(adj_self_ready, g)],
            "S": lambda b: [(s_masked, 2 * b), (s_masked, 2 * b + 1)],
            "U": lambda b: [(u_kept, 2 * b), (u_kept, 2 * b + 1)],
            "PT": lambda b: [(probT_act, b), (probT_dve, b)],
            "O": lambda b: [(y_ready, b)],
            "D1": lambda g: [(e_masked, g)],
            "V1": lambda g: [(v_kept, g)],
            "PT1": lambda g: [(prob1T_kept, g)],
            "O1": lambda g: [(x2_ready, GB * g + GB - 1)],
            "Z": lambda g: [(z_lo, g)],
            "H": lambda g: [(hid_kept, 2 * g), (hid_kept, 2 * g + 1)],
            "Y": lambda g: [(x3_ready, g)],
            "HT3": lambda g: [(h_init, g)],
            "T": lambda s: [(nat_kept, s)],
            "AG": lambda s: [(agg_lo, s)],
            "GA": lambda s: [(r_gate, s), (hn_biased, s)],
            "GB": lambda s: [(n_pre, s), (z_gate, s)],
            "XT": lambda g: [(out_ready, GB * g + GB - 1)],
        }
        RING_OF = {kind: "singles" for kind in RELEASES}
        RING_OF |= {kind: "pairs" for kind in ("S", "U", "PT", "H")}
        RING_OF |= {kind: "gru" for kind in ("HT3", "T", "AG", "GA", "GB", "XT")}

        class Banks:

            def __init__(self, steps, phase):
                self.repeats, self.rings, self.job = phase == "loop", RING_BANKS[phase], {}
                self.released = {ring: [] for ring in self.rings}
                for st in steps:
                    if st[0] in RELEASES:
                        ring = RING_OF[st[0]]
                        self.job[st] = ring, len(self.released[ring])
                        self.released[ring] += RELEASES[st[0]](*st[1:])

            def of(self, step, part=0):
                ring, n = self.job[step]
                banks = self.rings[ring]
                return bank[banks[(n + part) % len(banks)]]

            def free(self, it, step, part=0):
                return [(sig.sem, sig.at(it, k)) for sig, k in self.release(step, part)]

            def release(self, step, part=0):
                ring, n = self.job[step]
                n, size, released = n + part, len(self.rings[ring]), self.released[ring]
                if n >= size:
                    sig, k = released[n - size]
                elif self.repeats:
                    sig, k = released[max(m for m in range(len(released)) if m % size == n)]
                    k -= sig.per
                else:
                    return []
                return [(sig, k)]

        def load_mask(sp, it):
            sp.wait_ge(out_ready.sem, out_ready.at(it, -1))
            sp.dma_start(mask_in[:, :], maskT[:, bass.ds(it * NB - NB, NB)]).then_inc(mask_loaded.sem, 16)

        def tensor_steps(pe, it, steps, banks):
            mm = nc.tensor.matmul

            def split_product(dst, a_hi, a_lo, b_hi, b_lo, start, stop):
                mm(dst, a_hi, b_hi, start=start, stop=False)
                mm(dst, a_hi, b_lo, start=False, stop=False)
                return mm(dst, a_lo, b_hi, start=False, stop=stop)

            for st in steps["tensor"]:
                kind = st[0]
                if kind == "HT":
                    _, n, g = st
                    pe.wait_ge(h_normed[n].sem, h_normed[n].at(it, GB * g + GB - 1))
                    for free in banks.free(it, st):
                        pe.wait_ge(*free)
                    ps = banks.of(st)
                    for b in range(GB):
                        last = nc.tensor.transpose(ps[:, cols(b)], hn[n][:, g % hn[n].shape[1], cols(b)], ident[:, :])
                    last.then_inc(hT_ready[n].sem, 1)
                elif kind == "KQ":
                    g = st[1]
                    pe.wait_ge(hT_lo[0].sem, hT_lo[0].at(it, g))
                    for free in banks.free(it, st):
                        pe.wait_ge(*free)
                    split_product(banks.of(st)[:, :], wkq_hi[:, :], wkq_lo[:, :], hT_hi_t[0][:, g % 2, :],
                                  hT_lo_t[0][:, g % 2, :], True, True).then_inc(kq_ready.sem, 1)
                elif kind == "ADJ":
                    g = st[1]
                    pe.wait_ge(adj_loaded[g % 2].sem, adj_loaded[g % 2].at(it, g // 2))
                    for free in banks.free(it, st):
                        pe.wait_ge(*free)
                    ps = banks.of(st)
                    for b in range(GB):
                        last = nc.tensor.transpose(ps[:, cols(b)], adj_in[:, g % 2, cols(b)], ident[:, :])
                    last.then_inc(adjT_ready.sem, 1)
                elif kind == "S":
                    b = st[1]
                    g, j = divmod(b, GB)
                    if j == 0:
                        pe.wait_ge(kq_lo.sem, kq_lo.at(it, 2 * g + 1))
                    for half in range(2):
                        for free in banks.free(it, st, half):
                            pe.wait_ge(*free)
                        ps = banks.of(st, half)
                        mm(ps[:, :], kq[:, g % 2, cols(j)], sel_q[:, 4 * half:4 * half + 4, :],
                           start=True, stop=False)
                        for h in range(4):
                            last = mm(ps[:, cols(h)], sel_k[:, 4 * half + h, :], kq[:, g % 2, cols(j)],
                                      start=False, stop=(h == 3))
                        last.then_inc(s_ready.sem, 1)
                elif kind == "U":
                    b = st[1]
                    g, j = divmod(b, GB)
                    if j == 0:
                        pe.wait_ge(hT_lo[0].sem, hT_lo[0].at(it, g))
                    for half in range(2):
                        for free in banks.free(it, st, half):
                            pe.wait_ge(*free)
                        c = slice(half * 4 * D, (half + 1) * 4 * D)
                        split_product(banks.of(st, half)[:, :], hT_hi_t[0][:, g % 2, cols(j)],
                                      hT_lo_t[0][:, g % 2, cols(j)], G_hi[:, c], G_lo[:, c],
                                      True, True).then_inc(u_ready.sem, 1)
                elif kind == "PT":
                    b = st[1]
                    for half in range(2):
                        pe.wait_ge(prob_normed.sem, prob_normed.at(it, 2 * b + half))
                        for free in banks.free(it, st, half):
                            pe.wait_ge(*free)
                        ps = banks.of(st, half)
                        for h in range(4):
                            last = nc.tensor.transpose(ps[:, cols(h)], prob[:, b % RP, cols(4 * half + h)],
                                                       ident[:, :])
                        last.then_inc(probT_ready.sem, 1)
                elif kind == "O":
                    b = st[1]
                    free = dict(banks.release(st))
                    pe.wait_ge(probT_act.sem, probT_act.at(it, max(b, free.pop(probT_act, b))))
                    pe.wait_ge(probT_dve.sem, probT_dve.at(it, max(b, free.pop(probT_dve, b))))
                    pe.wait_ge(u_kept.sem, u_kept.at(it, max(2 * b + 1, free.pop(u_kept, 0))))
                    for sig, k in free.items():
                        pe.wait_ge(sig.sem, sig.at(it, k))
                    for h in range(HEADS):
                        last = mm(banks.of(st)[:, 0:D], probT[:, b % RPT, cols(h)], u_t[:, b % RU, cols(h)],
                                  start=(h == 0), stop=(h == HEADS - 1))
                    last.then_inc(o_ready.sem, 1)
                elif kind == "D1":
                    g = st[1]
                    pe.wait_ge(hT_lo[1].sem, hT_lo[1].at(it, g))
                    for free in banks.free(it, st):
                        pe.wait_ge(*free)
                    ps = banks.of(st)
                    split_product(ps[:, :], wdst_hi[:, :], wdst_lo[:, :], hT_hi_t[1][:, g % 2, :],
                                  hT_lo_t[1][:, g % 2, :], True, False)
                    for b in range(GB):
                        last = split_product(ps[:, cols(b)], hT_hi_t[1][:, g % 2, cols(b)],
                                             hT_lo_t[1][:, g % 2, cols(b)], wsrc_hi[:, :], wsrc_lo[:, :],
                                             False, b == GB - 1)
                    last.then_inc(e_ready.sem, 1)
                elif kind == "V1":
                    g = st[1]
                    pe.wait_ge(hT_lo[1].sem, hT_lo[1].at(it, g))
                    for free in banks.free(it, st):
                        pe.wait_ge(*free)
                    for b in range(GB):
                        last = split_product(banks.of(st)[:, cols(b)], hT_hi_t[1][:, g % 2, cols(b)],
                                             hT_lo_t[1][:, g % 2, cols(b)], W_hi[:, :], W_lo[:, :], True, True)
                    last.then_inc(v_ready.sem, 1)
                elif kind == "PT1":
                    g = st[1]
                    pe.wait_ge(exps1.sem, exps1.at(it, GB * g + GB - 1))
                    for free in banks.free(it, st):
                        pe.wait_ge(*free)
                    for b in range(GB):
                        last = nc.tensor.transpose(banks.of(st)[:, cols(b)], prob1[:, cols(b)], ident[:, :])
                    last.then_inc(prob1T_ready.sem, 1)
                elif kind == "O1":
                    g = st[1]
                    pe.wait_ge(v_kept.sem, v_kept.at(it, g))
                    pe.wait_ge(prob1T_kept.sem, prob1T_kept.at(it, g))
                    for free in banks.free(it, st):
                        pe.wait_ge(*free)
                    for b in range(GB):
                        last = mm(banks.of(st)[:, cols(b)], prob1T[:, cols(b)], v_t[:, cols(b)],
                                  start=True, stop=True)
                    last.then_inc(o1_ready.sem, 1)
                elif kind == "Z":
                    g = st[1]
                    pe.wait_ge(h_normed[2].sem, h_normed[2].at(it, GB * g + GB - 1))
                    pe.wait_ge(adj_self_ready.sem, adj_self_ready.at(it, g))
                    for free in banks.free(it, st):
                        pe.wait_ge(*free)
                    for b in range(GB):
                        last = mm(banks.of(st)[:, cols(b)], hn[2][:, 0, cols(b)], adj_self[:, g % S, cols(b)],
                                  start=True, stop=True)
                    last.then_inc(z_ready.sem, 1)
                elif kind == "H":
                    g = st[1]
                    pe.wait_ge(z_lo.sem, z_lo.at(it, g))
                    for c in range(2):
                        for free in banks.free(it, st, c):
                            pe.wait_ge(*free)
                        split_product(banks.of(st, c)[:, :], W1_hi[:, c * 128:(c + 1) * 128],
                                      W1_lo[:, c * 128:(c + 1) * 128], z_hi_t[:, :], z_lo_t[:, :],
                                      True, True).then_inc(hid_ready.sem, 1)
                elif kind == "Y":
                    g = st[1]
                    pe.wait_ge(hid_kept.sem, hid_kept.at(it, 2 * g + 1))
                    for free in banks.free(it, st):
                        pe.wait_ge(*free)
                    for b in range(GB):
                        for c in range(2):
                            last = mm(banks.of(st)[:, cols(b)], hid_t[:, c, cols(b)], W2_sb[:, c, :],
                                      start=(c == 0), stop=(c == 1))
                    last.then_inc(l2_ready.sem, 1)
                elif kind == "HT3":
                    g = st[1]
                    pe.wait_ge(h_normed[3].sem, h_normed[3].at(it, GB * g + GB - 1))
                    for free in banks.free(it, st):
                        pe.wait_ge(*free)
                    for b in range(GB):
                        last = nc.tensor.transpose(banks.of(st)[:, cols(b)], hn[3][:, g % 2, cols(b)], ident[:, :])
                    last.then_inc(h3T_ready.sem, 1)
                elif kind == "T":
                    s = st[1]
                    g = s % S
                    if s < S:
                        pe.wait_ge(h_init_lo.sem, h_init_lo.at(it, s))
                    else:
                        pe.wait_ge(h_lo.sem, h_lo.at(it, s - S))
                    for free in banks.free(it, st):
                        pe.wait_ge(*free)
                    ps = banks.of(st)[:, :].bitcast(f16)
                    for part, src in enumerate((hs_hi, hs_lo)):
                        for b in range(GB):
                            last = nc.tensor.transpose(ps[:, part * W4 + b * N:part * W4 + (b + 1) * N],
                                                       src[:, g, cols(b)], ident16[:, :])
                    last.then_inc(nat_ready.sem, 1)
                elif kind == "AG":
                    s = st[1]
                    g = s % S
                    pe.wait_ge(nat_kept.sem, nat_kept.at(it, s))
                    if s < S:
                        pe.wait_ge(edges_moved.sem, edges_moved.at(it, g))
                    for free in banks.free(it, st):
                        pe.wait_ge(*free)
                    for b in range(GB):
                        for part in range(2):
                            last = mm(banks.of(st)[:, cols(b)],
                                      nat[:, s % 2, part * W4 + b * N:part * W4 + (b + 1) * N],
                                      edges[:, g % S, cols(b)], start=(part == 0), stop=(part == 1))
                    last.then_inc(agg_ready.sem, 1)
                elif kind in ("GA", "GB"):
                    s = st[1]
                    l, g = divmod(s, S)
                    gates = ((0, True, True), (2, False, True)) if kind == "GA" else \
                        ((2, True, False), (1, True, True))
                    for part, (gate, agg_in, h_in) in enumerate(gates):
                        for free in banks.free(it, st, part):
                            pe.wait_ge(*free)
                        ps = banks.of(st, part)[:, :]
                        c = slice(gate * D, (gate + 1) * D)
                        if h_in:
                            last = split_product(ps, whh_hi[:, c], whh_lo[:, c], hs_hi[:, g % S, :],
                                                 hs_lo[:, g % S, :], True, not agg_in)
                        if agg_in:
                            if kind == "GA":
                                pe.wait_ge(agg_lo.sem, agg_lo.at(it, s))
                            last = split_product(ps, wih_hi[:, l, c], wih_lo[:, l, c], agg_hi_t[:, s % 2, :],
                                                 agg_lo_t[:, s % 2, :], not h_in, True)
                        last.then_inc((gates_a_ready if kind == "GA" else gates_b_ready).sem, 1)
                elif kind == "XT":
                    g = st[1]
                    pe.wait_ge(h_new.sem, h_new.at(it, (LAYERS - 1) * S + g))
                    for free in banks.free(it, st):
                        pe.wait_ge(*free)
                    for b in range(GB):
                        last = nc.tensor.transpose(banks.of(st)[:, cols(b)], hs[:, g % S, cols(b)], ident[:, :])
                    last.then_inc(outT_ready.sem, 1)

        def scalar_steps(act, it, steps, banks):
            a = nc.scalar
            for st in steps["scalar"]:
                kind = st[0]
                if kind == "LA" and st[1] in (0, 2):
                    _, n, g = st
                    act.wait_ge(ln_shift[n].sem, ln_shift[n].at(it, g))
                    if n == 0:
                        act.wait_ge(h0_biased.sem, h0_biased.at(it, g - 2))
                        act.wait_ge(hT_ready[0].sem, hT_ready[0].at(it, g - 2))
                    else:
                        act.wait_ge(z_ready.sem, z_ready.at(it, g - 1))
                    for b in range(GB):
                        src = x_in[:, g % 2, cols(b)] if n == 0 else xw[:, g % S, cols(b)]
                        a.activation(hn[n][:, g % hn[n].shape[1], cols(b)], src, ACT.Relu,
                                     bias=ln_shift_t[n][:, g % 2, b:b + 1], scale=ln_rstd_t[n][:, g % 2, b:b + 1])\
                            .then_inc(h_normed[n].sem, 1)
                elif kind == "HT":
                    _, n, g = st
                    act.wait_ge(hT_ready[n].sem, hT_ready[n].at(it, g))
                    if n == 0:
                        act.wait_ge(kq_ready.sem, kq_ready.at(it, g - 2))
                        act.wait_ge(u_ready.sem, u_ready.at(it, 2 * (GB * (g - 2) + GB - 1) + 1))
                    else:
                        act.wait_ge(e_ready.sem, e_ready.at(it, g - 2))
                        act.wait_ge(v_ready.sem, v_ready.at(it, g - 2))
                    a.activation(hT_hi_t[n][:, g % 2, :], banks.of(st)[:, :], ACT.Relu).then_inc(hT_hi[n].sem, 1)
                elif kind == "KQ":
                    g = st[1]
                    act.wait_ge(kq_ready.sem, kq_ready.at(it, g))
                    act.wait_ge(s_ready.sem, s_ready.at(it, 2 * (GB * (g - 2) + GB - 1) + 1))
                    a.activation(kq[:, g % 2, :], banks.of(st)[:, :], ACT.Identity, bias=kq_bias[:, 0:1])\
                        .then_inc(kq_hi.sem, 1)
                elif kind == "U":
                    b = st[1]
                    act.wait_ge(o_ready.sem, o_ready.at(it, b - RU))
                    for half in range(2):
                        act.wait_ge(u_ready.sem, u_ready.at(it, 2 * b + half))
                        a.activation(u_t[:, b % RU, half * 4 * D:(half + 1) * 4 * D], banks.of(st, half)[:, :],
                                     ACT.Copy).then_inc(u_kept.sem, 1)
                elif kind == "E":
                    b = st[1]
                    act.wait_ge(s_negmax.sem, s_negmax.at(it, 2 * b + 1))
                    act.wait_ge(probT_ready.sem, probT_ready.at(it, 2 * (b - RP) + 1))
                    for h in range(HEADS):
                        a.activation(prob[:, b % RP, cols(h)], logit[:, b % RT, cols(h)], ACT.Exp,
                                     bias=negmax[:, b % RT, h:h + 1], accum_out=rowsum[:, b % RP, h:h + 1])\
                            .then_inc(exps.sem, 1)
                elif kind == "PT":
                    b = st[1]
                    act.wait_ge(probT_ready.sem, probT_ready.at(it, 2 * b))
                    a.activation(probT[:, b % RPT, 0:4 * N], banks.of(st)[:, :], ACT.Copy)\
                        .then_inc(probT_act.sem, 1)
                elif kind == "X1":
                    g = st[1]
                    act.wait_ge(y_ready.sem, y_ready.at(it, GB * g + GB - 1))
                    a.activation(h0b[:, g % 2, :], h0b[:, g % 2, :], ACT.Tanh, scale=0.5).then_inc(y_tanh.sem, 1)
                elif kind == "V1":
                    g = st[1]
                    act.wait_ge(v_ready.sem, v_ready.at(it, g))
                    act.wait_ge(o1_ready.sem, o1_ready.at(it, g - 1))
                    a.activation(v_t[:, :], banks.of(st)[:, :], ACT.Copy).then_inc(v_kept.sem, 1)
                elif kind == "E1":
                    g = st[1]
                    act.wait_ge(e_negmax.sem, e_negmax.at(it, g))
                    act.wait_ge(prob1T_ready.sem, prob1T_ready.at(it, g - 1))
                    act.wait_ge(row_inv1.sem, row_inv1.at(it, g - 1))
                    for b in range(GB):
                        a.activation(prob1[:, cols(b)], e1_t[:, cols(b)], ACT.Exp,
                                     bias=negmax1[:, b:b + 1], accum_out=rowsum1[:, b:b + 1])\
                            .then_inc(exps1.sem, 1)
                elif kind == "PT1":
                    g = st[1]
                    act.wait_ge(prob1T_ready.sem, prob1T_ready.at(it, g))
                    act.wait_ge(o1_ready.sem, o1_ready.at(it, g - 1))
                    a.activation(prob1T[:, :], banks.of(st)[:, :], ACT.Copy).then_inc(prob1T_kept.sem, 1)
                elif kind == "Z":
                    g = st[1]
                    act.wait_ge(z_ready.sem, z_ready.at(it, g))
                    act.wait_ge(hid_ready.sem, hid_ready.at(it, 2 * (g - 1) + 1))
                    a.activation(z_hi_t[:, :], banks.of(st)[:, :], ACT.Copy).then_inc(z_hi.sem, 1)
                elif kind == "H":
                    g = st[1]
                    act.wait_ge(l2_ready.sem, l2_ready.at(it, g - 1))
                    for c in range(2):
                        act.wait_ge(hid_ready.sem, hid_ready.at(it, 2 * g + c))
                        a.activation(hid_t[:, c, :], banks.of(st, c)[:, :], ACT.Relu, bias=b1_sb[:, c:c + 1])\
                            .then_inc(hid_kept.sem, 1)
                elif kind == "HT3":
                    g = st[1]
                    act.wait_ge(h3T_ready.sem, h3T_ready.at(it, g))
                    act.wait_ge(outT_ready.sem, outT_ready.at(it, g - S))
                    a.activation(hs[:, g % S, :], banks.of(st)[:, :], ACT.Relu).then_inc(h_init.sem, 1)
                elif kind == "T":
                    s = st[1]
                    act.wait_ge(nat_ready.sem, nat_ready.at(it, s))
                    a.activation(nat[:, s % 2, :], banks.of(st)[:, :].bitcast(f16), ACT.Copy).then_inc(nat_kept.sem, 1)
                elif kind == "AG":
                    s = st[1]
                    act.wait_ge(agg_ready.sem, agg_ready.at(it, s))
                    a.activation(agg_hi_t[:, s % 2, :], banks.of(st)[:, :], ACT.Copy).then_inc(agg_hi.sem, 1)
                elif kind == "GA":
                    s = st[1]
                    act.wait_ge(h_new.sem, h_new.at(it, s - 2))
                    act.wait_ge(gates_a_ready.sem, gates_a_ready.at(it, 2 * s))
                    a.activation(rn_t[:, s % 2, :], banks.of(st, 0)[:, :], ACT.Tanh, bias=brz_sb[:, 0:1], scale=0.5)\
                        .then_inc(r_gate.sem, 1)
                    act.wait_ge(gates_a_ready.sem, gates_a_ready.at(it, 2 * s + 1))
                    act.wait_ge(hn_gated.sem, hn_gated.at(it, s - 1))
                    a.activation(hnb_t[:, :], banks.of(st, 1)[:, :], ACT.Identity, bias=bhn_sb[:, 0:1], scale=0.5)\
                        .then_inc(hn_biased.sem, 1)
                elif kind == "GB":
                    s = st[1]
                    act.wait_ge(n_pre.sem, n_pre.at(it, s))
                    a.activation(rn_t[:, s % 2, :], rn_t[:, s % 2, :], ACT.Tanh, bias=bih_sb[:, 2:3])\
                        .then_inc(n_gate.sem, 1)
                    act.wait_ge(gates_b_ready.sem, gates_b_ready.at(it, 2 * s + 1))
                    act.wait_ge(zdiff.sem, zdiff.at(it, s - 2))
                    a.activation(z_t[:, s % 2, :], banks.of(st, 1)[:, :], ACT.Tanh, bias=brz_sb[:, 1:2], scale=0.5)\
                        .then_inc(z_gate.sem, 1)
                elif kind == "XT":
                    g = st[1]
                    act.wait_ge(out_ready.sem, out_ready.at(it, GB * g + GB - 1))
                    act.dma_start(rows(out_flat, it * (S * GROUP) + (g - S) * GROUP), four(xd[:, g % S, :]))\
                        .then_inc(out_stored[g].sem, 16)

        def gpsimd_steps(pool, it, steps):
            p = nc.gpsimd
            for st in steps["gpsimd"]:
                kind = st[0]
                if kind == "LN":
                    _, n, g = st
                    pool.wait_ge(ln_moments[n].sem, ln_moments[n].at(it, GB * g + GB - 1))
                    pool.wait_ge(h_normed[n].sem, h_normed[n].at(it, GB * (g - 2) + GB - 1))
                    p.tensor_tensor(ln_negmean_t[n][:, g % 2, :], ln_mom_t[n][:, g % 2, :, 0], minus_one[:, :], ALU.mult)
                    p.tensor_tensor(ln_var_t[n][:, g % 2, :], ln_mom_t[n][:, g % 2, :, 1], ln_eps[:, :], ALU.add)\
                        .then_inc(ln_var[n].sem, 1)
                    pool.wait_ge(ln_var[n].sem, ln_var[n].at(it, g))
                    p.tensor_tensor(ln_rstd_t[n][:, g % 2, :], ln_var_t[n][:, g % 2, :], minus_half[:, :], ALU.pow)\
                        .then_inc(ln_rstd[n].sem, 1)
                    pool.wait_ge(ln_rstd[n].sem, ln_rstd[n].at(it, g))
                    p.tensor_tensor(ln_shift_t[n][:, g % 2, :], ln_negmean_t[n][:, g % 2, :], ln_rstd_t[n][:, g % 2, :],
                                    ALU.mult).then_inc(ln_shift[n].sem, 1)
                if kind == "XB":
                    g = st[1]
                    pool.wait_ge(x_loaded[g % 2].sem, x_loaded[g % 2].at(it, g // 2))
                    pool.wait_ge(x1_ready.sem, x1_ready.at(it, g - 2))
                    p.tensor_tensor(x_half_t[:, g % 2, :], x_in[:, g % 2, :], half_col[:, :].broadcast_to([128, W4]),
                                    ALU.add).then_inc(x_half.sem, 1)
                    pool.wait_ge(h_normed[0].sem, h_normed[0].at(it, GB * g + GB - 1))
                    pool.wait_ge(y_ready.sem, y_ready.at(it, GB * (g - 2) + GB - 1))
                    p.tensor_tensor(four(h0b[:, g % 2, :]), four(hn[0][:, g % 2, :]),
                                    l0_bias[:, :].unsqueeze(1).broadcast_to([128, GB, D]), ALU.add)\
                        .then_inc(h0_biased.sem, 1)
                elif kind == "E":
                    b = st[1]
                    pool.wait_ge(row_inv.sem, row_inv.at(it, b))
                    for half in range(2):
                        c = slice(half * 4 * N, (half + 1) * 4 * N)
                        p.tensor_tensor(four(prob[:, b % RP, c]), four(prob[:, b % RP, c]),
                                        rowinv[:, b % RP, 4 * half:4 * half + 4].unsqueeze(2)
                                        .broadcast_to([128, 4, N]), ALU.mult).then_inc(prob_normed.sem, 1)
                elif kind == "LN" and st[1] == 2:
                    g = st[2]
                    pool.wait_ge(x2_ready.sem, x2_ready.at(it, GB * g + GB - 1))
                    pool.wait_ge(x3_ready.sem, x3_ready.at(it, g - 1))
                    p.tensor_tensor(four(x2b[:, :]), four(xw[:, g % S, :]),
                                    b2_sb[:, :].unsqueeze(1).broadcast_to([128, GB, D]), ALU.add)\
                        .then_inc(x2_biased.sem, 1)
                elif kind == "GB":
                    s = st[1]
                    g = s % S
                    pool.wait_ge(n_gate.sem, n_gate.at(it, s))
                    pool.wait_ge(h_new.sem, h_new.at(it, s - 2))
                    p.tensor_tensor(diff_t[:, s % 2, :], hs[:, g % S, :], rn_t[:, s % 2, :], ALU.subtract)\
                        .then_inc(diff.sem, 1)
                elif kind == "EW":
                    s = st[1]
                    pool.wait_ge(z_gate.sem, z_gate.at(it, s))
                    pool.wait_ge(diff.sem, diff.at(it, s))
                    p.tensor_tensor(z_t[:, s % 2, :], z_t[:, s % 2, :], diff_t[:, s % 2, :], ALU.mult)\
                        .then_inc(z_scaled.sem, 1)
                    pool.wait_ge(z_scaled.sem, z_scaled.at(it, s))
                    p.tensor_tensor(diff_t[:, s % 2, :], diff_t[:, s % 2, :], z_t[:, s % 2, :], ALU.add)\
                        .then_inc(zdiff.sem, 1)
                elif kind in ("HT3", "LO"):
                    g = st[1] % S
                    hi, lo = (h_init_hi, h_init_lo) if kind == "HT3" else (h_hi, h_lo)
                    pool.wait_ge(hi.sem, hi.at(it, st[1]))
                    p.tensor_tensor(hs_lo[:, g, :], hs[:, g, :], hs_hi[:, g, :], ALU.subtract).then_inc(lo.sem, 1)
                elif kind == "XD":
                    g = st[1]
                    pool.wait_ge(x3_ready.sem, x3_ready.at(it, g - S))
                    pool.wait_ge(out_stored[g].sem, out_stored[g].at(it, -1))
                    p.tensor_tensor(xd[:, g % S, :], xw[:, g % S, :], zero_col[:, :].broadcast_to([128, W4]), ALU.add)\
                        .then_inc(xd_ready.sem, 1)

        def vector_steps(dve, it, steps, banks):
            v = nc.vector
            for st in steps["vector"]:
                kind = st[0]
                if kind == "LN":
                    _, n, g = st
                    if n == 0:
                        dve.wait_ge(x_loaded[g % 2].sem, x_loaded[g % 2].at(it, g // 2))
                    elif n == 1:
                        dve.wait_ge(x1_ready.sem, x1_ready.at(it, g))
                    elif n == 2:
                        dve.wait_ge(x2_ready.sem, x2_ready.at(it, GB * g + GB - 1))
                    else:
                        dve.wait_ge(x3_ready.sem, x3_ready.at(it, g - S))
                    dve.wait_ge(ln_shift[n].sem, ln_shift[n].at(it, g - 2))
                    for b in range(GB):
                        src = x_in[:, g % 2, cols(b)] if n == 0 else xw[:, g % S, cols(b)]
                        v.bn_stats(ln_stats_t[n][:, g % 2, b, :], src).then_inc(ln_stats[n].sem, 1)
                    dve.drain()
                    for b in range(GB):
                        v.bn_aggr(ln_mom_t[n][:, g % 2, b, :], ln_stats_t[n][:, g % 2, b, :]).then_inc(ln_moments[n].sem, 1)
                elif kind == "LA" and st[1] in (1, 3):
                    _, n, g = st
                    dve.wait_ge(ln_shift[n].sem, ln_shift[n].at(it, g))
                    if n == 1:
                        dve.wait_ge(hT_ready[1].sem, hT_ready[1].at(it, g - 1))
                    else:
                        dve.wait_ge(h3T_ready.sem, h3T_ready.at(it, g - 2))
                    for b in range(GB):
                        v.tensor_scalar(hn[n][:, g % hn[n].shape[1], cols(b)], xw[:, g % S, cols(b)],
                                        ln_rstd_t[n][:, g % 2, b:b + 1], ln_shift_t[n][:, g % 2, b:b + 1],
                                        ALU.mult, ALU.add).then_inc(h_normed[n].sem, 1)
                elif kind == "HT":
                    _, n, g = st
                    dve.wait_ge(hT_hi[n].sem, hT_hi[n].at(it, g))
                    v.scalar_tensor_tensor(hT_lo_t[n][:, g % 2, :], banks.of(st)[:, :], 0.0, hT_hi_t[n][:, g % 2, :],
                                           ALU.max, ALU.subtract).then_inc(hT_lo[n].sem, 1)
                elif kind == "KQ":
                    g = st[1]
                    dve.wait_ge(kq_hi.sem, kq_hi.at(it, g))
                    for rows in (K_ROWS, Q_ROWS):
                        r = slice(rows + LO, rows + 2 * LO)
                        v.scalar_tensor_tensor(kq[r, g % 2, :], banks.of(st)[r, :], kq_bias[r, 0:1],
                                               kq[r, g % 2, :], ALU.add, ALU.subtract).then_inc(kq_lo.sem, 1)
                elif kind == "ADJ":
                    g = st[1]
                    dve.wait_ge(adj_loaded[g % 2].sem, adj_loaded[g % 2].at(it, g // 2))
                    dve.wait_ge(s_masked.sem, s_masked.at(it, 2 * (GB * (g - 2) + GB - 1) + 1))
                    v.tensor_scalar(l0_mask[:, g % 2, :], adj_in[:, g % 2, :], 1.0, 1e9, ALU.subtract, ALU.mult)\
                        .then_inc(l0_mask_ready.sem, 1)
                    dve.wait_ge(adjT_ready.sem, adjT_ready.at(it, g))
                    dve.wait_ge(z_ready.sem, z_ready.at(it, g - S))
                    v.tensor_tensor(four(adj_self[:, g % S, :]), four(banks.of(st)[:, :]),
                                    ident_eps[:, :].unsqueeze(1).broadcast_to([128, GB, N]), ALU.add)\
                        .then_inc(adj_self_ready.sem, 1)
                    dve.wait_ge(e_masked.sem, e_masked.at(it, g - S))
                    v.tensor_scalar(l1_mask[:, g % S, :], adj_in[:, g % 2, :], 0.0, -9e15, ALU.is_le, ALU.mult)\
                        .then_inc(l1_mask_ready.sem, 1)
                    dve.wait_ge(edges_moved.sem, edges_moved.at(it, g))
                    v.tensor_scalar(edges_next[:, g % S, :], adj_in[:, g % 2, :], 0.0, None, ALU.not_equal)\
                        .then_inc(edges_ready.sem, 1)
                elif kind == "S":
                    b = st[1]
                    g, j = divmod(b, GB)
                    if j == 0:
                        dve.wait_ge(l0_mask_ready.sem, l0_mask_ready.at(it, g))
                    halves = [logit[:, b % RT, half * 4 * N:(half + 1) * 4 * N] for half in range(2)]
                    for half, t in enumerate(halves):
                        dve.wait_ge(s_ready.sem, s_ready.at(it, 2 * b + half))
                        v.tensor_tensor(four(t), four(banks.of(st, half)[:, :]),
                                        l0_mask[:, g % 2, cols(j)].unsqueeze(1).broadcast_to([128, 4, N]), ALU.add)\
                            .then_inc(s_masked.sem, 1)
                    for half, t in enumerate(halves):
                        dve.wait_ge(s_masked.sem, s_masked.at(it, 2 * b + half))
                        v.scalar_tensor_tensor(t, t, 0.01, t, ALU.mult, ALU.max).then_inc(s_leaky.sem, 1)
                    for half, t in enumerate(halves):
                        dve.wait_ge(s_leaky.sem, s_leaky.at(it, 2 * b + half))
                        v.tensor_reduce(negmax[:, b % RT, 4 * half:4 * half + 4], four(t), AX.X, ALU.max,
                                        negate=True).then_inc(s_negmax.sem, 1)
                elif kind == "E":
                    b = st[1]
                    dve.wait_ge(exps.sem, exps.at(it, HEADS * b + HEADS - 1))
                    dve.wait_ge(prob_normed.sem, prob_normed.at(it, 2 * (b - RP) + 1))
                    v.reciprocal(rowinv[:, b % RP, :], rowsum[:, b % RP, :]).then_inc(row_inv.sem, 1)
                elif kind == "PT":
                    b = st[1]
                    dve.wait_ge(probT_ready.sem, probT_ready.at(it, 2 * b + 1))
                    v.tensor_copy(probT[:, b % RPT, 4 * N:8 * N], banks.of(st, 1)[:, :]).then_inc(probT_dve.sem, 1)
                elif kind == "O":
                    b = st[1]
                    g, j = divmod(b, GB)
                    dve.wait_ge(o_ready.sem, o_ready.at(it, b))
                    if j == 0:
                        dve.wait_ge(h0_biased.sem, h0_biased.at(it, g))
                    v.tensor_tensor(h0b[:, g % 2, cols(j)], banks.of(st)[:, 0:D], h0b[:, g % 2, cols(j)], ALU.add)\
                        .then_inc(y_ready.sem, 1)
                elif kind == "X1":
                    g = st[1]
                    dve.wait_ge(y_tanh.sem, y_tanh.at(it, g))
                    dve.wait_ge(x_half.sem, x_half.at(it, g))
                    dve.wait_ge(xd_ready.sem, xd_ready.at(it, g))
                    dve.wait_ge(h_normed[3].sem, h_normed[3].at(it, GB * g + GB - 1))
                    v.scalar_tensor_tensor(xw[:, g % S, :], h0b[:, g % 2, :], 0.5, x_half_t[:, g % 2, :],
                                           ALU.mult, ALU.add).then_inc(x1_ready.sem, 1)
                elif kind == "D1":
                    g = st[1]
                    t = e1_t[:, :]
                    dve.wait_ge(e_ready.sem, e_ready.at(it, g))
                    dve.wait_ge(exps1.sem, exps1.at(it, GB * (g - 1) + GB - 1))
                    dve.wait_ge(l1_mask_ready.sem, l1_mask_ready.at(it, g))
                    v.tensor_tensor(t, banks.of(st)[:, :], l1_mask[:, g % S, :], ALU.add).then_inc(e_masked.sem, 1)
                    dve.wait_ge(e_masked.sem, e_masked.at(it, g))
                    v.scalar_tensor_tensor(t, t, 0.2, t, ALU.mult, ALU.max).then_inc(e_leaky.sem, 1)
                    dve.wait_ge(e_leaky.sem, e_leaky.at(it, g))
                    v.tensor_reduce(negmax1[:, :], four(t), AX.X, ALU.max, negate=True)\
                        .then_inc(e_negmax.sem, 1)
                elif kind == "E1":
                    g = st[1]
                    dve.wait_ge(exps1.sem, exps1.at(it, GB * g + GB - 1))
                    dve.wait_ge(x2_ready.sem, x2_ready.at(it, GB * (g - 1) + GB - 1))
                    v.reciprocal(rowinv1[:, :], rowsum1[:, :]).then_inc(row_inv1.sem, 1)
                elif kind == "O1":
                    g = st[1]
                    dve.wait_ge(o1_ready.sem, o1_ready.at(it, g))
                    dve.wait_ge(row_inv1.sem, row_inv1.at(it, g))
                    for b in range(GB):
                        v.scalar_tensor_tensor(xw[:, g % S, cols(b)], banks.of(st)[:, cols(b)],
                                               rowinv1[:, b:b + 1], xw[:, g % S, cols(b)],
                                               ALU.mult, ALU.add).then_inc(x2_ready.sem, 1)
                elif kind == "Z":
                    g = st[1]
                    dve.wait_ge(z_hi.sem, z_hi.at(it, g))
                    v.tensor_tensor(z_lo_t[:, :], banks.of(st)[:, :], z_hi_t[:, :], ALU.subtract)\
                        .then_inc(z_lo.sem, 1)
                elif kind == "Y":
                    g = st[1]
                    dve.wait_ge(l2_ready.sem, l2_ready.at(it, g))
                    dve.wait_ge(x2_biased.sem, x2_biased.at(it, g))
                    v.tensor_tensor(xw[:, g % S, :], banks.of(st)[:, :], x2b[:, :], ALU.add)\
                        .then_inc(x3_ready.sem, 1)
                elif kind == "HT3":
                    g = st[1]
                    dve.wait_ge(h_init.sem, h_init.at(it, g))
                    dve.wait_ge(gates_b_ready.sem, gates_b_ready.at(it, 2 * (g - S) + 1))
                    v.tensor_copy(hs_hi[:, g % S, :], hs[:, g % S, :]).then_inc(h_init_hi.sem, 1)
                elif kind == "AG":
                    s = st[1]
                    dve.wait_ge(agg_hi.sem, agg_hi.at(it, s))
                    v.tensor_tensor(agg_lo_t[:, s % 2, :], banks.of(st)[:, :], agg_hi_t[:, s % 2, :],
                                    ALU.subtract).then_inc(agg_lo.sem, 1)
                elif kind == "XD":
                    g = st[1]
                    dve.wait_ge(edges_ready.sem, edges_ready.at(it, g - S))
                    dve.wait_ge(agg_ready.sem, agg_ready.at(it, g - S))
                    v.tensor_copy(edges[:, g % S, :], edges_next[:, g % S, :]).then_inc(edges_moved.sem, 1)
                elif kind == "GA":
                    s = st[1]
                    u = rn_t[:, s % 2, :]
                    dve.wait_ge(r_gate.sem, r_gate.at(it, s))
                    dve.wait_ge(hn_biased.sem, hn_biased.at(it, s))
                    v.scalar_tensor_tensor(u, u, 1.0, hnb_t[:, :], ALU.add, ALU.mult).then_inc(hn_gated.sem, 1)
                elif kind == "GB":
                    s = st[1]
                    u = rn_t[:, s % 2, :]
                    dve.wait_ge(gates_b_ready.sem, gates_b_ready.at(it, 2 * s))
                    dve.wait_ge(hn_gated.sem, hn_gated.at(it, s))
                    v.tensor_tensor(u, banks.of(st, 0)[:, :], u, ALU.add).then_inc(n_pre.sem, 1)
                elif kind == "EW":
                    s = st[1]
                    g = s % S
                    t = diff_t[:, s % 2, :]
                    dve.wait_ge(zdiff.sem, zdiff.at(it, s))
                    v.scalar_tensor_tensor(hs[:, g % S, :], t, 0.5, rn_t[:, s % 2, :], ALU.mult, ALU.add)\
                        .then_inc(h_new.sem, 1)
                    if s < (LAYERS - 1) * S:
                        dve.wait_ge(h_new.sem, h_new.at(it, s))
                        v.tensor_copy(hs_hi[:, g % S, :], hs[:, g % S, :]).then_inc(h_hi.sem, 1)
                elif kind == "XT":
                    g = st[1]
                    dve.wait_ge(outT_ready.sem, outT_ready.at(it, g))
                    dve.wait_ge(mask_loaded.sem, mask_loaded.at(it, 0))
                    dve.wait_ge(xd_ready.sem, xd_ready.at(it, g))
                    for b in range(GB):
                        v.scalar_tensor_tensor(xd[:, g % S, cols(b)], banks.of(st)[:, cols(b)],
                                               mask_in[:, g * GB + b:g * GB + b + 1], xd[:, g % S, cols(b)],
                                               ALU.mult, ALU.add).then_inc(out_ready.sem, 1)

        with nc.Block() as block:
            banks = Banks(FIRST["tensor"], "first")

            @block.sync
            def _(sp):
                for g in range(2, S):
                    load_group(sp, 0, g)

            @block.tensor
            def _(pe):
                tensor_steps(pe, 0, FIRST, banks)

            @block.scalar
            def _(act):
                scalar_steps(act, 0, FIRST, banks)

            @block.gpsimd
            def _(pool):
                gpsimd_steps(pool, 0, FIRST)

            @block.vector
            def _(dve):
                vector_steps(dve, 0, FIRST, banks)

        with nc.Block() as block:
            banks = Banks(LOOP["tensor"], "loop")

            @block.sync
            def _(sp):
                with sp.Fori(1, ITERS) as it:
                    load_mask(sp, it)
                    for g in range(S):
                        load_group(sp, it, g)

            @block.tensor
            def _(pe):
                with pe.Fori(1, ITERS) as it:
                    tensor_steps(pe, it, LOOP, banks)

            @block.scalar
            def _(act):
                with act.Fori(1, ITERS) as it:
                    scalar_steps(act, it, LOOP, banks)

            @block.gpsimd
            def _(pool):
                with pool.Fori(1, ITERS) as it:
                    gpsimd_steps(pool, it, LOOP)

            @block.vector
            def _(dve):
                with dve.Fori(1, ITERS) as it:
                    vector_steps(dve, it, LOOP, banks)

        with nc.Block() as block:
            banks = Banks(LAST["tensor"], "last")

            @block.sync
            def _(sp):
                load_mask(sp, ITERS)
                for g in range(S):
                    sp.wait_ge(out_stored[g].sem, out_stored[g].at(ITERS, 0))

            @block.tensor
            def _(pe):
                tensor_steps(pe, ITERS, LAST, banks)

            @block.scalar
            def _(act):
                scalar_steps(act, ITERS, LAST, banks)

            @block.gpsimd
            def _(pool):
                gpsimd_steps(pool, ITERS, LAST)

            @block.vector
            def _(dve):
                vector_steps(dve, ITERS, LAST, banks)


def kernel(**inputs):
    import numpy as np
    import concourse.bacc as bacc
    from concourse.bass_utils import run_bass_kernel_spmd

    a = {k: np.asarray(v) for k, v in inputs.items()}
    arrays = {
        "x": a["x"],
        "adj": a["adj"],
        "maskT": a["nodemask"].T,
        "ident": np.eye(128, dtype=np.float32),
        "fcwT": a["L0_gnn_fc_w"].reshape(D, HEADS, D).transpose(2, 1, 0),
        "fpw": a["L0_gnn_fp_w"].reshape(HEADS, D, D).transpose(1, 0, 2),
        "fcb": a["L0_gnn_fc_b"].reshape(HEADS, D).T,
        "qkw": np.concatenate([a["L0_gnn_q_w"], a["L0_gnn_k_w"]], axis=1),
        "qkb": np.concatenate([a["L0_gnn_q_b"], a["L0_gnn_k_b"]]).reshape(1, 2),
        "fpb": a["L0_gnn_fp_b"].reshape(1, D),
        "l1W": a["L1_gnn_W"],
        "l1WT": a["L1_gnn_W"].T,
        "l1a": a["L1_gnn_a"].reshape(2, D).T,
        "eps": a["L2_gnn_eps"],
        "l2W1": a["L2_gnn_W1"],
        "l2b1": a["L2_gnn_b1"].reshape(2, 128).T,
        "l2W2": a["L2_gnn_W2"].reshape(2, 128, D).transpose(1, 0, 2),
        "l2b2": a["L2_gnn_b2"],
        "l3wT": a["L3_gnn_weight"].transpose(2, 0, 1),
        "wihT": a["L3_gnn_w_ih"].T,
        "whhT": a["L3_gnn_w_hh"].T,
        "bih": a["L3_gnn_b_ih"].reshape(3, 128).T,
        "bhh": a["L3_gnn_b_hh"].reshape(3, 128).T,
    }
    nc = bacc.Bacc("TRN2", target_bir_lowering=False, num_devices=1)
    data, args = {}, []
    for name, value in arrays.items():
        value = np.ascontiguousarray(value)
        data[f"in_{name}"] = value
        args.append(nc.dram_tensor(f"in_{name}", value.shape, mybir.dt.from_np(value.dtype), kind="ExternalInput").ap())
    args.append(nc.dram_tensor("out_0", (B, N, D), mybir.dt.float32, kind="ExternalOutput").ap())
    adj_gnn_stack_kernel(nc, *args)
    r = run_bass_kernel_spmd(nc, [data], core_ids=[0])
    return r.results[0]["out_0"]
```
